# Optimizing a Trainium2 kernel written in Bass

```python
import numpy as np
import jax
import jax.numpy as jnp

def _softmax(x, axis=-1):
    return jax.nn.softmax(x, axis=axis)

def _gelu(x):
    return jax.nn.gelu(x, approximate=True)

def _silu(x):
    return jax.nn.silu(x)

def _sigmoid(x):
    return jax.nn.sigmoid(x)

def _layernorm(x, axis=-1, eps=1e-05):
    m = jnp.mean(x, axis=axis, keepdims=True)
    v = jnp.var(x, axis=axis, keepdims=True)
    return (x - m) / jnp.sqrt(v + eps)

def _scatter_add(tgt, idx, src, axis=0):
    return tgt.at[idx].add(src)

def _segment_sum(src, seg, n):
    return jax.ops.segment_sum(src, seg, n)
kernel_name = 'mk_xattn_ffn_d2_seqx_r4_075898'

def setup_inputs(seed: int=0):
    np.random.seed(seed)
    _w = jnp.asarray

    def _rec_inputs():
        import jax
        import jax.numpy as jnp
        _rk = jax.random.key(seed)
        x = -0.0002928 + 1 * jax.random.normal(jax.random.fold_in(_rk, 1), (4, 512, 256), jnp.float32)
        _lenS = 512 - jax.random.randint(jax.random.fold_in(_rk, 7), (4,), 0, max(1, 512 // 4) + 1, jnp.int32)
        _lenS2 = 512 - jax.random.randint(jax.random.fold_in(_rk, 8), (4,), 0, max(1, 512 // 4) + 1, jnp.int32)
        _ctx_1024P = jax.random.normal(jax.random.fold_in(_rk, 11), (4, 16, 256), jnp.float32)
        _ctx_1024c = jax.random.dirichlet(jax.random.fold_in(_rk, 511), 0.3 * jnp.ones((16,), jnp.float32), (4, 512))
        _ctx_1024t = jnp.einsum('bsk,bkd->bsd', _ctx_1024c, _ctx_1024P)
        _ctx_1024t = _ctx_1024t * jax.lax.rsqrt(jnp.mean(jnp.square(_ctx_1024t)) + 1e-12) * 0.953939
        ctx_1024 = -1.52775e-05 + 0.999936 * (_ctx_1024t + 0.3 * jax.random.normal(jax.random.fold_in(_rk, 611), (4, 512, 256), jnp.float32))
        _validS = jnp.arange(512)[None, :] < _lenS[:, None]
        _validS2 = jnp.arange(512)[None, :] < _lenS2[:, None]
        _causal = jnp.tril(jnp.ones((512, 512), dtype=bool))
        mask_1x1xSxS2_bk1 = jnp.broadcast_to(_validS2[0:1, None, None, :], (1, 1, 512, 512))
        return (x, ctx_1024, mask_1x1xSxS2_bk1)
    x, ctx_1024, mask_1x1xSxS2_bk1 = _rec_inputs()

    def _L0_xattn_setup():
        import jax, jax.numpy as jnp
        import numpy as np
        DIM = 256
        NUM_HEADS = 8
        HEAD_DIM = 64
        INNER = NUM_HEADS * HEAD_DIM
        key = jax.random.key(seed)
        ks = jax.random.split(key, 7)
        B, N, M = (8, 128, 1024)
        x = jax.random.normal(ks[0], (B, N, DIM), dtype=jnp.float32)
        context = jax.random.normal(ks[1], (B, M, DIM), dtype=jnp.float32)
        s_in = 1.0 / np.sqrt(DIM)
        s_inner = 1.0 / np.sqrt(INNER)
        Wq = jax.random.normal(ks[2], (DIM, INNER), dtype=jnp.float32) * s_in
        Wk = jax.random.normal(ks[3], (DIM, INNER), dtype=jnp.float32) * s_in
        Wv = jax.random.normal(ks[4], (DIM, INNER), dtype=jnp.float32) * s_in
        Wo = jax.random.normal(ks[5], (INNER, DIM), dtype=jnp.float32) * s_inner
        bo = jax.random.normal(ks[6], (DIM,), dtype=jnp.float32) * 0.01
        return {'x': x, 'context': context, 'Wq': Wq, 'Wk': Wk, 'Wv': Wv, 'Wo': Wo, 'bo': bo}
    _L0_xattn_all = _L0_xattn_setup()
    _L0_xattn_in = {k: v for k, v in _L0_xattn_all.items() if k in ('Wq', 'Wk', 'Wv', 'Wo', 'bo')}
    del _L0_xattn_all

    def _L0_ffn_setup():
        import jax, jax.numpy as jnp
        import numpy as np
        S, B, D = (256, 2, 256)
        E, TOPK = (15, 3)
        F = 256
        FS = 512

        def _uinit(k, shape, out_dim):
            std = out_dim ** (-0.5)
            return jax.random.uniform(k, shape, jnp.float32, -std, std)
        key = jax.random.key(seed)
        ks = jax.random.split(key, 10)
        return {'x': jax.random.normal(ks[0], (S, B, D), jnp.float32), 'gate_w': jax.random.normal(ks[1], (E, D), jnp.float32) * D ** (-0.5), 'fc1_w': _uinit(ks[2], (E, 2 * F, D), 2 * F), 'fc1_b': _uinit(ks[3], (E, 2 * F), 2 * F), 'geglu_mult': jnp.ones((E, F), jnp.float32), 'fc2_w': _uinit(ks[4], (E, D, F), D), 'fc2_b': _uinit(ks[5], (E, D), D), 's_fc1_w': _uinit(ks[6], (2 * FS, D), 2 * FS), 's_fc1_b': _uinit(ks[7], (2 * FS,), 2 * FS), 's_geglu_mult': jnp.ones((FS,), jnp.float32), 's_fc2_w': _uinit(ks[8], (D, FS), D), 's_fc2_b': _uinit(ks[9], (D,), D)}
    _L0_ffn_all = _L0_ffn_setup()
    _L0_ffn_in = {k: v for k, v in _L0_ffn_all.items() if k in ('gate_w', 'fc1_w', 'fc1_b', 'geglu_mult', 'fc2_w', 'fc2_b', 's_fc1_w', 's_fc1_b', 's_geglu_mult', 's_fc2_w', 's_fc2_b')}
    del _L0_ffn_all

    def _L1_xattn_setup():
        import jax, jax.numpy as jnp
        import numpy as np
        D_MODEL = 256
        N_HEADS = 16
        D_HEAD = D_MODEL // N_HEADS
        B, T = (4, 512)
        key = jax.random.key(seed)
        ks = jax.random.split(key, 7)
        s = 0.02
        q = jax.random.normal(ks[0], (B, T, D_MODEL), dtype=jnp.float32)
        k = jax.random.normal(ks[1], (B, T, D_MODEL), dtype=jnp.float32)
        v = jax.random.normal(ks[2], (B, T, D_MODEL), dtype=jnp.float32)
        mask = jnp.triu(jnp.ones((T, T), dtype=bool), k=1)[None, None, :, :]
        Wq = jax.random.normal(ks[3], (D_MODEL, D_MODEL), dtype=jnp.float32) * s
        Wk = jax.random.normal(ks[4], (D_MODEL, D_MODEL), dtype=jnp.float32) * s
        Wv = jax.random.normal(ks[5], (D_MODEL, D_MODEL), dtype=jnp.float32) * s
        Wo = jax.random.normal(ks[6], (D_MODEL, D_MODEL), dtype=jnp.float32) * s
        return {'q': q, 'k': k, 'v': v, 'mask': mask, 'Wq': Wq, 'Wk': Wk, 'Wv': Wv, 'Wo': Wo}
    _L1_xattn_all = _L1_xattn_setup()
    _L1_xattn_in = {k: v for k, v in _L1_xattn_all.items() if k in ('Wq', 'Wk', 'Wv', 'Wo')}
    del _L1_xattn_all

    def _L1_ffn_setup():
        import jax, jax.numpy as jnp
        import numpy as np
        D_IN, D_HID = (256, 1024)

        def _ternary(key, shape):
            return jax.random.randint(key, shape, -1, 2).astype(jnp.float32)

        def _tlin(x, w, s):
            return jnp.einsum('bsi,oi->bso', x, w) * s
        key = jax.random.key(seed)
        ks = jax.random.split(key, 12)
        inv = lambda fan: 1.0 / np.sqrt(fan).astype(np.float32)
        return {'x': jax.random.normal(ks[0], (4, 512, D_IN), dtype=jnp.float32), 'w1_w': _ternary(ks[1], (D_HID, D_IN)), 'w1_s': jax.random.uniform(ks[2], (D_HID,), dtype=jnp.float32) * inv(D_IN), 'w2_w': _ternary(ks[3], (D_HID, D_IN)), 'w2_s': jax.random.uniform(ks[4], (D_HID,), dtype=jnp.float32) * inv(D_IN), 'h1_w': _ternary(ks[5], (D_HID, D_HID)), 'h1_s': jax.random.uniform(ks[6], (D_HID,), dtype=jnp.float32) * inv(D_HID), 'h2_w': _ternary(ks[7], (D_HID, D_HID)), 'h2_s': jax.random.uniform(ks[8], (D_HID,), dtype=jnp.float32) * inv(D_HID), 'w3_w': _ternary(ks[9], (D_IN, D_HID)), 'w3_s': jax.random.uniform(ks[10], (D_IN,), dtype=jnp.float32) * inv(D_HID)}
    _L1_ffn_all = _L1_ffn_setup()
    _L1_ffn_in = {k: v for k, v in _L1_ffn_all.items() if k in ('w1_w', 'w1_s', 'w2_w', 'w2_s', 'h1_w', 'h1_s', 'h2_w', 'h2_s', 'w3_w', 'w3_s')}
    del _L1_ffn_all
    return {'x': x, 'ctx_1024': ctx_1024, 'mask_1x1xSxS2_bk1': mask_1x1xSxS2_bk1, 'L0_xattn_Wq': _L0_xattn_in['Wq'], 'L0_xattn_Wk': _L0_xattn_in['Wk'], 'L0_xattn_Wv': _L0_xattn_in['Wv'], 'L0_xattn_Wo': _L0_xattn_in['Wo'], 'L0_xattn_bo': _L0_xattn_in['bo'], 'L0_ffn_gate_w': _L0_ffn_in['gate_w'], 'L0_ffn_fc1_w': _L0_ffn_in['fc1_w'], 'L0_ffn_fc1_b': _L0_ffn_in['fc1_b'], 'L0_ffn_geglu_mult': _L0_ffn_in['geglu_mult'], 'L0_ffn_fc2_w': _L0_ffn_in['fc2_w'], 'L0_ffn_fc2_b': _L0_ffn_in['fc2_b'], 'L0_ffn_s_fc1_w': _L0_ffn_in['s_fc1_w'], 'L0_ffn_s_fc1_b': _L0_ffn_in['s_fc1_b'], 'L0_ffn_s_geglu_mult': _L0_ffn_in['s_geglu_mult'], 'L0_ffn_s_fc2_w': _L0_ffn_in['s_fc2_w'], 'L0_ffn_s_fc2_b': _L0_ffn_in['s_fc2_b'], 'L1_xattn_Wq': _L1_xattn_in['Wq'], 'L1_xattn_Wk': _L1_xattn_in['Wk'], 'L1_xattn_Wv': _L1_xattn_in['Wv'], 'L1_xattn_Wo': _L1_xattn_in['Wo'], 'L1_ffn_w1_w': _L1_ffn_in['w1_w'], 'L1_ffn_w1_s': _L1_ffn_in['w1_s'], 'L1_ffn_w2_w': _L1_ffn_in['w2_w'], 'L1_ffn_w2_s': _L1_ffn_in['w2_s'], 'L1_ffn_h1_w': _L1_ffn_in['h1_w'], 'L1_ffn_h1_s': _L1_ffn_in['h1_s'], 'L1_ffn_h2_w': _L1_ffn_in['h2_w'], 'L1_ffn_h2_s': _L1_ffn_in['h2_s'], 'L1_ffn_w3_w': _L1_ffn_in['w3_w'], 'L1_ffn_w3_s': _L1_ffn_in['w3_s']}

def reference(x, ctx_1024, mask_1x1xSxS2_bk1, L0_xattn_Wq, L0_xattn_Wk, L0_xattn_Wv, L0_xattn_Wo, L0_xattn_bo, L0_ffn_gate_w, L0_ffn_fc1_w, L0_ffn_fc1_b, L0_ffn_geglu_mult, L0_ffn_fc2_w, L0_ffn_fc2_b, L0_ffn_s_fc1_w, L0_ffn_s_fc1_b, L0_ffn_s_geglu_mult, L0_ffn_s_fc2_w, L0_ffn_s_fc2_b, L1_xattn_Wq, L1_xattn_Wk, L1_xattn_Wv, L1_xattn_Wo, L1_ffn_w1_w, L1_ffn_w1_s, L1_ffn_w2_w, L1_ffn_w2_s, L1_ffn_h1_w, L1_ffn_h1_s, L1_ffn_h2_w, L1_ffn_h2_s, L1_ffn_w3_w, L1_ffn_w3_s):
    import jax
    import jax.numpy as jnp

    def _L0_xattn_ref(x, context, Wq, Wk, Wv, Wo, bo):
        import jax, jax.numpy as jnp
        import numpy as np
        DIM = 256
        NUM_HEADS = 8
        HEAD_DIM = 64
        INNER = NUM_HEADS * HEAD_DIM
        B, N, _ = x.shape
        M = context.shape[1]
        scale = HEAD_DIM ** (-0.5)
        q = (x @ Wq).reshape(B, N, NUM_HEADS, HEAD_DIM).transpose(0, 2, 1, 3)
        k = (context @ Wk).reshape(B, M, NUM_HEADS, HEAD_DIM).transpose(0, 2, 1, 3)
        v = (context @ Wv).reshape(B, M, NUM_HEADS, HEAD_DIM).transpose(0, 2, 1, 3)
        attn = jax.nn.softmax(jnp.einsum('bhnd,bhmd->bhnm', q, k) * scale, axis=-1)
        out = jnp.einsum('bhnm,bhmd->bhnd', attn, v)
        out = out.transpose(0, 2, 1, 3).reshape(B, N, INNER)
        return out @ Wo + bo

    def _L0_ffn_ref(x, gate_w, fc1_w, fc1_b, geglu_mult, fc2_w, fc2_b, s_fc1_w, s_fc1_b, s_geglu_mult, s_fc2_w, s_fc2_b):
        import jax, jax.numpy as jnp
        import numpy as np
        S, B, D = (256, 2, 256)
        E, TOPK = (15, 3)
        F = 256
        FS = 512

        def _uinit(k, shape, out_dim):
            std = out_dim ** (-0.5)
            return jax.random.uniform(k, shape, jnp.float32, -std, std)
        s, b, d = x.shape
        xt = x.reshape(-1, d)
        T = xt.shape[0]
        logits = xt @ gate_w.T
        scores = jax.nn.softmax(logits, axis=-1)
        topk_w, topk_idx = jax.lax.top_k(scores, TOPK)
        topk_w = topk_w / (jnp.sum(topk_w, axis=-1, keepdims=True) + 1e-20)
        comb = jnp.zeros((T, E), xt.dtype).at[jnp.arange(T)[:, None], topk_idx].add(topk_w)
        h = jnp.einsum('td,efd->etf', xt, fc1_w) + fc1_b[:, None, :]
        xh, g = (h[..., :F], h[..., F:])
        a = jax.nn.gelu(g, approximate=False) * xh * geglu_mult[:, None, :]
        yexp = jnp.einsum('etf,edf->etd', a, fc2_w) + fc2_b[:, None, :]
        y = jnp.einsum('etd,te->td', yexp, comb)
        hs = xt @ s_fc1_w.T + s_fc1_b
        xs, gs = (hs[..., :FS], hs[..., FS:])
        as_ = jax.nn.gelu(gs, approximate=False) * xs * s_geglu_mult
        ys = as_ @ s_fc2_w.T + s_fc2_b
        return (y + ys).reshape(s, b, d)

    def _L1_xattn_ref(q, k, v, mask, Wq, Wk, Wv, Wo):
        import jax, jax.numpy as jnp
        import numpy as np
        D_MODEL = 256
        N_HEADS = 16
        D_HEAD = D_MODEL // N_HEADS
        B, T = (4, 512)
        H, Dh = (N_HEADS, D_HEAD)
        scale = Dh ** (-0.5)

        def split(t):
            Bt, Tt, _ = t.shape
            return t.reshape(Bt, Tt, H, Dh).transpose(0, 2, 1, 3)
        Q = split(q @ Wq.T)
        K = split(k @ Wk.T)
        V = split(v @ Wv.T)
        scores = jnp.einsum('bhqd,bhkd->bhqk', Q, K) * scale
        scores = jnp.where(mask, -jnp.inf, scores)
        attn = jax.nn.softmax(scores, axis=-1)
        attn = jnp.nan_to_num(attn)
        out = jnp.einsum('bhqk,bhkd->bhqd', attn, V)
        out = out.transpose(0, 2, 1, 3).reshape(q.shape[0], q.shape[1], H * Dh)
        return out @ Wo.T

    def _L1_ffn_ref(x, w1_w, w1_s, w2_w, w2_s, h1_w, h1_s, h2_w, h2_s, w3_w, w3_s):
        import jax, jax.numpy as jnp
        import numpy as np
        D_IN, D_HID = (256, 1024)

        def _ternary(key, shape):
            return jax.random.randint(key, shape, -1, 2).astype(jnp.float32)

        def _tlin(x, w, s):
            return jnp.einsum('bsi,oi->bso', x, w) * s
        h = jax.nn.silu(_tlin(x, w1_w, w1_s)) * _tlin(x, w2_w, w2_s)
        h = jax.nn.gelu(_tlin(h, h1_w, h1_s), approximate=False)
        h = jax.nn.gelu(_tlin(h, h2_w, h2_s), approximate=False)
        return _tlin(h, w3_w, w3_s)
    x = x + _L0_xattn_ref(_layernorm(x, axis=-1), ctx_1024, L0_xattn_Wq, L0_xattn_Wk, L0_xattn_Wv, L0_xattn_Wo, L0_xattn_bo)
    x = x + _L0_ffn_ref(_layernorm(x, axis=-1), L0_ffn_gate_w, L0_ffn_fc1_w, L0_ffn_fc1_b, L0_ffn_geglu_mult, L0_ffn_fc2_w, L0_ffn_fc2_b, L0_ffn_s_fc1_w, L0_ffn_s_fc1_b, L0_ffn_s_geglu_mult, L0_ffn_s_fc2_w, L0_ffn_s_fc2_b)
    x = x + _L1_xattn_ref(_layernorm(x, axis=-1), ctx_1024, ctx_1024, mask_1x1xSxS2_bk1, L1_xattn_Wq, L1_xattn_Wk, L1_xattn_Wv, L1_xattn_Wo)
    x = x + _L1_ffn_ref(_layernorm(x, axis=-1), L1_ffn_w1_w, L1_ffn_w1_s, L1_ffn_w2_w, L1_ffn_w2_s, L1_ffn_h1_w, L1_ffn_h1_s, L1_ffn_h2_w, L1_ffn_h2_s, L1_ffn_w3_w, L1_ffn_w3_s)
    return x

_drawn_inputs = setup_inputs


def setup_inputs(seed=0):
    import zlib

    import numpy as np

    out = dict(_drawn_inputs(seed))
    spreads = {'L0_ffn_geglu_mult': (1.0, 0.2), 'L0_ffn_s_geglu_mult': (1.0, 0.2)}
    factors = {}
    for name, (base, spread) in spreads.items():
        noise = np.random.default_rng([zlib.crc32(name.encode()), seed]).standard_normal(out[name].shape)
        drawn = base * np.exp(spread * noise) if base else spread * noise
        out[name] = jnp.asarray(drawn.astype(out[name].dtype))
    for name, factor in factors.items():
        out[name] = (out[name] * factor).astype(out[name].dtype)
    return out
```

```python
from contextlib import ExitStack

import numpy as np

import concourse.bass as bass
from concourse import mybir
from concourse.alu_op_type import AluOpType as ALU

F32 = mybir.dt.float32
F32R = mybir.dt.float32r
BF16 = mybir.dt.bfloat16
U8 = mybir.dt.uint8
ACT = mybir.ActivationFunctionType
AX = mybir.AxisListType

P = 128
B, S, D = 4, 512, 256
KT = D // P
TT = S // P
T = B * S
NT = T // P
LN_EPS = 1e-5

H0, DH0 = 8, 64
INNER = H0 * DH0
PAIRS = H0 // 2
H1, DH1 = 16, 16
GROUPS, GH = 4, 4
E, TOPK, F, FS = 15, 3, 256, 512
FT, FST = F // P, FS // P
HID = 1024
HT = HID // P
MASKED = -1.0e30
LEAST_MAX = -1.0e29
DMA = 16


def hi_lo(pe, nc, out, stat, move, first, last):
    (sh, sl), (mh, ml) = stat, move
    nc.tensor.matmul(out, sh, ml, start=first, stop=False)
    nc.tensor.matmul(out, sl, mh, start=False, stop=False)
    return nc.tensor.matmul(out, sh, mh, start=False, stop=last)


class Core:
    pass


def apart(engine, c):
    engine.sem_inc(c.waited, 1)


def semaphores(nc, ctx, phase, names):
    return [ctx.enter_context(nc.semaphore(f"{phase}_{n}")) for n in names.split()]


def layernorm_phase(nc, c, turn):
    setup = turn == 0
    with ExitStack() as ctx:
        sb = lambda n, s, d=F32: ctx.enter_context(nc.sbuf_tensor(f"ln{turn}_{n}", s, d))
        stats = sb("stats", [P, TT, 6])
        mean = sb("mean", [P, TT])
        diff = sb("diff", [P, TT])
        m2 = sb("m2", [P, TT])
        ve = sb("ve", [P, TT])
        y = sb("y", [P, TT])
        t1 = sb("t1", [P, TT])
        half = sb("half", [P, TT])
        rstd = sb("rstd", [P, TT])
        xn = sb("xn", [P, TT, D])
        (loaded, const, stat_done, step, var_done, pow_done, rstd_done, xn_done, tr_done, hi_done, lo_done) = c.ln_sems
        CONST = 3 + turn
        block = ctx.enter_context(nc.Block())

        @block.sync
        def _(sp):
            if setup:
                sp.dma_start(c.X[:, :, :], c.ins["x"].rearrange("(n p) d -> p n d", p=P)).then_inc(loaded, DMA)
                sp.dma_start(c.bo[:, :], c.ins["bo"].partition_broadcast(P)).then_inc(loaded, DMA)

        @block.gpsimd
        def _(pool):
            if setup:
                nc.gpsimd.memset(c.ident[:, :], 0.0).then_inc(const, 1)
                pool.wait_ge(const, 1)
                nc.gpsimd.affine_select(out=c.ident[:, :], in_=c.ident[:, :], compare_op=ALU.not_equal, fill=1.0,
                                        base=0, pattern=[[-1, P]], channel_multiplier=1).then_inc(const, 1)
            nc.gpsimd.memset(half[:, :], -0.5).then_inc(const, 1)
            pool.wait_ge(const, CONST)
            pool.wait_ge(loaded, 2 * DMA)
            with pool.Fori(0, B) as b:
                n = b + turn * B
                pool.wait_ge(var_done, n + 1)
                nc.gpsimd.tensor_tensor(y[:, :], ve[:, :], half[:, :], ALU.pow).then_inc(pow_done, 1)
                if setup:
                    pool.wait_ge(xn_done, n + 1)
                    xb = c.X[:, bass.ds(b * TT, TT), :]
                    nc.gpsimd.tensor_tensor(xb, xb, c.bo[:, :].unsqueeze(1).to_broadcast([P, TT, D]), ALU.add)

        @block.vector
        def _(dve):
            if setup:
                dve.wait_ge(loaded, 2 * DMA)
            with dve.Fori(0, B) as b:
                n = b + turn * B
                for t in range(TT):
                    last = nc.vector.bn_stats(stats[:, t, :], c.X[:, bass.ds(b * TT + t, 1), :].rearrange("p o d -> p (o d)"))
                last.then_inc(stat_done, 1)
                dve.wait_ge(stat_done, n + 1)
                nc.vector.tensor_tensor(mean[:, :], stats[:, :, 1], stats[:, :, 4], ALU.add)
                nc.vector.tensor_tensor(diff[:, :], stats[:, :, 1], stats[:, :, 4], ALU.subtract)
                nc.vector.tensor_tensor(m2[:, :], stats[:, :, 2], stats[:, :, 5], ALU.add).then_inc(step, 1)
                dve.wait_ge(step, 5 * n + 1)
                nc.vector.tensor_scalar(mean[:, :], mean[:, :], 0.5, None, ALU.mult)
                nc.vector.tensor_tensor(diff[:, :], diff[:, :], diff[:, :], ALU.mult).then_inc(step, 1)
                dve.wait_ge(step, 5 * n + 2)
                nc.vector.scalar_tensor_tensor(m2[:, :], diff[:, :], D / 4.0, m2[:, :], ALU.mult, ALU.add).then_inc(step, 1)
                dve.wait_ge(step, 5 * n + 3)
                nc.vector.tensor_scalar(ve[:, :], m2[:, :], 1.0 / D, LN_EPS, ALU.mult, ALU.add).then_inc(var_done, 1)
                dve.wait_ge(pow_done, n + 1)
                nc.vector.scalar_tensor_tensor(t1[:, :], ve[:, :], -0.5, y[:, :], ALU.mult, ALU.mult).then_inc(step, 1)
                dve.wait_ge(step, 5 * n + 4)
                nc.vector.tensor_tensor(t1[:, :], t1[:, :], y[:, :], ALU.mult).then_inc(step, 1)
                dve.wait_ge(step, 5 * n + 5)
                nc.vector.scalar_tensor_tensor(rstd[:, :], t1[:, :], 1.5, y[:, :], ALU.add, ALU.mult).then_inc(rstd_done, 1)
                dve.wait_ge(rstd_done, n + 1)
                for t in range(TT):
                    last = nc.vector.tensor_scalar(xn[:, t, :], c.X[:, bass.ds(b * TT + t, 1), :].rearrange("p o d -> p (o d)"),
                                                   mean[:, t:t + 1], rstd[:, t:t + 1], ALU.subtract, ALU.mult)
                last.then_inc(xn_done, 1)
                for k in range(KT):
                    dve.wait_ge(hi_done, KT * n + k + 1)
                    tok = bass.ds(b * S, S)
                    nc.vector.tensor_tensor(c.xnL[:, k, tok], c.pd[:, k, :], c.xnH[:, k, tok].bitcast(F32),
                                            ALU.subtract).then_inc(lo_done, 1)

        @block.tensor
        def _(pe):
            pe.wait_ge(const, CONST)
            with pe.Fori(0, B) as b:
                n = b + turn * B
                pe.wait_ge(xn_done, n + 1)
                for k in range(KT):
                    for t in range(TT):
                        last = nc.tensor.transpose(c.pd[:, k, t * P:(t + 1) * P], xn[:, t, k * P:(k + 1) * P], c.ident[:, :])
                    last.then_inc(tr_done, 1)

        @block.scalar
        def _(act):
            with act.Fori(0, B) as b:
                n = b + turn * B
                for k in range(KT):
                    act.wait_ge(tr_done, KT * n + k + 1)
                    apart(act, c)
                    nc.scalar.activation(c.xnH[:, k, bass.ds(b * S, S)], c.pd[:, k, :], ACT.Copy).then_inc(hi_done, 1)


def first_attention_phase(nc, c):
    WORK = TT + PAIRS * (2 + 2 * TT) + 2
    with ExitStack() as ctx:
        sb = lambda n, s, d=F32: ctx.enter_context(nc.sbuf_tensor(f"a_{n}", s, d))
        raw = sb("raw", [P, 2, KT * INNER])
        wH = sb("wH", [P, 4, KT * INNER], F32R)
        wL = sb("wL", [P, 4, KT * INNER], F32R)
        ctx_raw = sb("ctx_raw", [P, KT, S])
        ctxH = sb("ctxH", [P, KT, S], F32R)
        ctxL = sb("ctxL", [P, KT, S], F32R)
        V = sb("V", [P, TT, INNER])
        qHL = sb("qHL", [P, 2, 2, S], F32R)
        kHH = sb("kHH", [P, 2, 2, S], F32R)
        kL1 = sb("kL1", [P, 2, 2, S], F32R)
        qHM = sb("qHM", [P, 2, 2, S], F32R)
        mx = sb("mx", [P, 2, 2, TT])
        prob = sb("prob", [P, 2, 2, TT, S])
        half_sum = sb("half_sum", [P, 2, S])
        prob_sum = sb("prob_sum", [P, 2, 2, S])
        ones = sb("ones", [P, DH0])
        inv = sb("inv", [P, S])
        o = sb("o", [P, S])
        oH = sb("oH", [P, PAIRS, S], F32R)
        oL = sb("oL", [P, PAIRS, S], F32R)
        (w_in0, w_in1, w_hi, w_lo, const, ctx_in, ctx_hi, ctx_lo, work_full, work_read, q_hi, k_hi, dup_done, row_full,
         row_done, st_full, exp_done, add_half, add_done, pv_done, norm_step, o_read, o_split, x_done) = semaphores(
            nc, ctx, "a", "w_in0 w_in1 w_hi w_lo const ctx_in ctx_hi ctx_lo work_full work_read q_hi k_hi dup_done row_full "
            "row_done st_full exp_done add_half add_done pv_done norm_step o_read o_split x_done")
        wq, wk, wv, wo = range(4)
        weight = lambda w, k, lo, n: [x[:, w, k * INNER + lo:k * INNER + lo + n] for x in (wH, wL)]
        wo_tile = lambda k: [x[:, wo, k * D:(k + 1) * D] for x in (wH, wL)]
        own = lambda h: slice(h * DH0, (h + 1) * DH0)
        other = lambda h: slice((1 - h) * DH0, (2 - h) * DH0)
        aux = lambda h: slice((1 - h) * DH0, (1 - h) * DH0 + 1)
        use_v = lambda t: t
        use_proj = lambda j, n: TT + n if j == 0 else TT + 2 + (j - 1) * (2 + 2 * TT) + n
        use_s = lambda j, h, t: TT + 2 + j * (2 + 2 * TT) + (2 if j < PAIRS - 1 else 0) + h * TT + t
        use_o = lambda n: WORK - 2 + n
        block = ctx.enter_context(nc.Block())

        @block.sync
        def _(sp):
            for n, name in enumerate(("wq0", "wk0", "wv0", "wo0")):
                if n >= 2:
                    sp.wait_ge(w_lo, n - 1)
                sp.dma_start(raw[:, n % 2, :], c.ins[name]).then_inc(w_in0 if n % 2 == 0 else w_in1, DMA)
            with sp.Fori(0, B) as b:
                sp.wait_ge(ctx_lo, b + 1)
                sp.dma_start(ctx_raw[:, :, :], c.ins["ctx"][:, :, bass.ds(b * S, S)]).then_inc(ctx_in, DMA)

        @block.gpsimd
        def _(pool):
            pool.sem_inc(add_done, 1)
            nc.gpsimd.memset(ones[:, :], 1.0).then_inc(const, 1)
            nc.gpsimd.memset(kL1[:, :, :, :].bitcast(F32), 0.0).then_inc(const, 1)
            nc.gpsimd.memset(qHM[:, :, :, :].bitcast(F32), 0.0).then_inc(const, 1)
            pool.wait_ge(const, 3)
            for h in range(2):
                nc.gpsimd.memset(kL1[aux(h), :, h, :].bitcast(F32), 1.0).then_inc(const, 1)

            with pool.Fori(0, B) as b:
                for j in range(PAIRS):
                    for h in range(2):
                        pool.wait_ge(exp_done, (b * PAIRS + j) * 4 + 3 + h)
                        pool.wait_ge(add_done, (b * PAIRS + j) * 2 + h + 1)
                        nc.gpsimd.tensor_tensor(half_sum[:, :, :], prob[:, j % 2, h, 0:2, :], prob[:, j % 2, h, 2:4, :],
                                                ALU.add).then_inc(add_half, 1)
                        pool.wait_ge(add_half, (b * PAIRS + j) * 2 + h + 1)
                        nc.gpsimd.tensor_tensor(prob_sum[:, j % 2, h, :], half_sum[:, 0, :], half_sum[:, 1, :],
                                                ALU.add).then_inc(add_done, 1)

        @block.scalar
        def _(act):
            for n in range(4):
                act.wait_ge(w_in0 if n % 2 == 0 else w_in1, DMA * (n // 2 + 1))
                nc.scalar.activation(wH[:, n, :], raw[:, n % 2, :], ACT.Copy).then_inc(w_hi, 1)

            def round_hi(b, j):
                act.wait_ge(work_full, b * WORK + use_proj(j, 0) + 1)
                for h in range(2):
                    last = nc.scalar.activation(qHL[own(h), j % 2, h, :], c.pd[own(h), use_proj(j, 0) % 2, :], ACT.Copy)
                last.then_inc(q_hi, 1)
                act.wait_ge(work_full, b * WORK + use_proj(j, 1) + 1)
                for h in range(2):
                    nc.scalar.activation(kHH[own(h), j % 2, h, :], c.pd[own(h), use_proj(j, 1) % 2, :], ACT.Copy)
                    last = nc.scalar.activation(kHH[other(h), j % 2, h, :], c.pd[own(h), use_proj(j, 1) % 2, :], ACT.Copy)
                last.then_inc(k_hi, 1)

            with act.Fori(0, B) as b:
                act.wait_ge(ctx_in, DMA * b + DMA)
                nc.scalar.activation(ctxH[:, :, :], ctx_raw[:, :, :], ACT.Copy).then_inc(ctx_hi, 1)
                round_hi(b, 0)
                for j in range(PAIRS):
                    if j + 1 < PAIRS:
                        round_hi(b, j + 1)
                    for h in range(2):
                        act.wait_ge(row_full, (b * PAIRS + j) * 2 + h + 1)
                        act.wait_ge(dup_done, b * PAIRS + j + 1)
                        nc.scalar.activation(qHM[aux(h), j % 2, h, :], c.pa[0:1, 2 * h, :], ACT.Copy,
                                             scale=-1.0).then_inc(row_done, 1)
                    for n in range(4):
                        h, k2 = n % 2, 2 * (n // 2)
                        act.wait_ge(st_full, (b * PAIRS + j) * 4 + n + 1)
                        act.wait_ge(pv_done, b * PAIRS + j + 1)
                        nc.scalar.activation(prob[:, j % 2, h, k2:k2 + 2, :], c.pa[:, 2 * h:2 * h + 2, :], ACT.Exp,
                                             scale=DH0 ** -0.5).then_inc(exp_done, 1)

        @block.vector
        def _(dve):
            dve.sem_inc(work_read, 2)
            dve.sem_inc(ctx_lo, 1)
            dve.sem_inc(o_read, 1)
            for n in range(4):
                dve.wait_ge(w_hi, n + 1)
                nc.vector.tensor_tensor(wL[:, n, :], raw[:, n % 2, :], wH[:, n, :].bitcast(F32), ALU.subtract).then_inc(w_lo, 1)

            def keep_lo(b, j):
                dve.wait_ge(q_hi, b * PAIRS + j + 1)
                for h in range(2):
                    last = nc.vector.tensor_tensor(qHL[other(h), j % 2, h, :], c.pd[own(h), use_proj(j, 0) % 2, :],
                                                   qHL[own(h), j % 2, h, :].bitcast(F32), ALU.subtract)
                last.then_inc(work_read, 1)
                for h in range(2):
                    last = nc.vector.tensor_copy(qHM[own(h), j % 2, h, :], qHL[own(h), j % 2, h, :].bitcast(F32))
                last.then_inc(dup_done, 1)
                dve.wait_ge(k_hi, b * PAIRS + j + 1)
                for h in range(2):
                    last = nc.vector.tensor_tensor(kL1[own(h), j % 2, h, :], c.pd[own(h), use_proj(j, 1) % 2, :],
                                                   kHH[own(h), j % 2, h, :].bitcast(F32), ALU.subtract)
                last.then_inc(work_read, 1)

            def normalise(b, j):
                dve.wait_ge(pv_done, b * PAIRS + j + 3)
                step = (b * PAIRS + j) * 2
                nc.vector.reciprocal(inv[:, :], c.pd[:, 3, :]).then_inc(norm_step, 1)
                dve.wait_ge(norm_step, step + 1)
                nc.vector.tensor_tensor(o[:, :], c.pd[:, 2, :], inv[:, :], ALU.mult).then_inc(o_read, 1)
                dve.wait_ge(o_read, b * PAIRS + j + 2)
                nc.vector.tensor_copy(oH[:, j, :], o[:, :]).then_inc(norm_step, 1)
                dve.wait_ge(norm_step, step + 2)
                nc.vector.tensor_tensor(oL[:, j, :], o[:, :], oH[:, j, :].bitcast(F32), ALU.subtract).then_inc(o_split, 1)

            with dve.Fori(0, B) as b:
                dve.wait_ge(ctx_hi, b + 1)
                nc.vector.tensor_tensor(ctxL[:, :, :], ctx_raw[:, :, :], ctxH[:, :, :].bitcast(F32),
                                        ALU.subtract).then_inc(ctx_lo, 1)
                for t in range(TT):
                    dve.wait_ge(work_full, b * WORK + use_v(t) + 1)
                    nc.vector.tensor_copy(V[:, t, :], c.pd[:, use_v(t) % 2, :]).then_inc(work_read, 1)
                keep_lo(b, 0)
                for j in range(PAIRS):
                    if j + 1 < PAIRS:
                        keep_lo(b, j + 1)
                    for h in range(2):
                        for t in range(TT):
                            u = use_s(j, h, t)
                            dve.wait_ge(work_full, b * WORK + u + 1)
                            nc.vector.reduce_max(mx[:, j % 2, h, t:t + 1], c.pd[:, u % 2, :], AX.X).then_inc(work_read, 1)
                    if j:
                        normalise(b, j - 1)
                normalise(b, PAIRS - 1)
                for n in range(2):
                    dve.wait_ge(work_full, b * WORK + use_o(n) + 1)
                    xb = c.X[:, bass.ds(b * TT + 2 * n, 2), :].rearrange("p n d -> p (n d)")
                    nc.vector.tensor_tensor(xb, c.pd[:, use_o(n) % 2, :], xb, ALU.add).then_inc(work_read, 1)

        @block.tensor
        def _(pe):
            pe.sem_inc(pv_done, 2)
            pe.wait_ge(w_lo, 4)
            pe.wait_ge(const, 5)

            def free_bank(b, u):
                pe.wait_ge(work_read, b * WORK + u + 1)
                return c.pd[:, u % 2, :]

            def project(b, j):
                out = free_bank(b, use_proj(j, 0))
                for k in range(KT):
                    last = hi_lo(pe, nc, out, weight(wq, k, j * P, P), [x[:, k, bass.ds(b * S, S)] for x in (c.xnH, c.xnL)],
                                 k == 0, k == KT - 1)
                last.then_inc(work_full, 1)
                out = free_bank(b, use_proj(j, 1))
                for k in range(KT):
                    last = hi_lo(pe, nc, out, weight(wk, k, j * P, P), [x[:, k, :] for x in (ctxH, ctxL)],
                                 k == 0, k == KT - 1)
                last.then_inc(work_full, 1)

            def weigh_values(b, j, k):
                if k == 0:
                    pe.wait_ge(o_read, b * PAIRS + j + 1)
                pe.wait_ge(exp_done, (b * PAIRS + j) * 4 + (2 if k < 2 else 4))
                for h in range(2):
                    head = 2 * j + h
                    nc.tensor.matmul(c.pd[own(h), 2, :], V[:, k, head * DH0:(head + 1) * DH0], prob[:, j % 2, h, k, :],
                                     start=k == 0, stop=k == TT - 1)

            def denominators(b, j):
                pe.wait_ge(add_done, (b * PAIRS + j) * 2 + 3)
                for h in range(2):
                    last = nc.tensor.matmul(c.pd[own(h), 3, :], ones[:, :], prob_sum[:, j % 2, h, :], start=True, stop=True)
                last.then_inc(pv_done, 1)

            with pe.Fori(0, B) as b:
                pe.wait_ge(ctx_lo, b + 2)
                for t in range(TT):
                    out = free_bank(b, use_v(t))
                    for k in range(KT):
                        last = hi_lo(pe, nc, out, [x[:, k, t * P:(t + 1) * P] for x in (ctxH, ctxL)],
                                     weight(wv, k, 0, INNER), k == 0, k == KT - 1)
                    last.then_inc(work_full, 1)
                project(b, 0)
                for j in range(PAIRS):
                    if j + 1 < PAIRS:
                        project(b, j + 1)
                    pe.wait_ge(dup_done, b * PAIRS + j + 1)
                    pe.wait_ge(work_read, b * WORK + use_proj(j, 1) + 3)
                    for h in range(2):
                        for t in range(TT):
                            out = free_bank(b, use_s(j, h, t))
                            nc.tensor.matmul(out, qHL[:, j % 2, h, t * P:(t + 1) * P], kHH[:, j % 2, h, :],
                                             start=True, stop=True).then_inc(work_full, 1)
                            if j and h * TT + t >= 2 and t % 2 == 1:
                                weigh_values(b, j - 1, (h * TT + t) // 2 - 1)
                    if j:
                        weigh_values(b, j - 1, TT - 1)
                        denominators(b, j - 1)
                    for h in range(2):
                        pe.wait_ge(work_read, b * WORK + use_s(j, h, TT - 1) + 3)
                        pe.wait_ge(exp_done, (b * PAIRS + j) * 4) if j else None
                        for t in range(TT):
                            last = nc.tensor.transpose(c.pa[0:1, 2 * h, t * P:(t + 1) * P], mx[:, j % 2, h, t:t + 1], c.ident[:, :])
                        last.then_inc(row_full, 1)
                    for n in range(4):
                        h = n % 2
                        if n < 2:
                            pe.wait_ge(row_done, (b * PAIRS + j) * 2 + h + 1)
                        else:
                            pe.wait_ge(exp_done, (b * PAIRS + j) * 4 + n - 1)
                        for k in range(2 * (n // 2), 2 * (n // 2) + 2):
                            out = c.pa[:, 2 * h + k % 2, :]
                            nc.tensor.matmul(out, kHH[:, j % 2, h, k * P:(k + 1) * P], qHL[:, j % 2, h, :], start=True, stop=False)
                            last = nc.tensor.matmul(out, kL1[:, j % 2, h, k * P:(k + 1) * P], qHM[:, j % 2, h, :],
                                                    start=False, stop=True)
                        last.then_inc(st_full, 1)
                for k in range(TT):
                    weigh_values(b, PAIRS - 1, k)
                denominators(b, PAIRS - 1)
                pe.wait_ge(o_split, b * PAIRS + PAIRS)
                for n in range(2):
                    bank = free_bank(b, use_o(n))
                    for t in (2 * n, 2 * n + 1):
                        out = bank[:, (t % 2) * D:(t % 2 + 1) * D]
                        for k in range(PAIRS):
                            last = hi_lo(pe, nc, out, [x[:, k, t * P:(t + 1) * P] for x in (oH, oL)], wo_tile(k),
                                         k == 0, k == PAIRS - 1)
                    last.then_inc(work_full, 1)


def mixture_phase(nc, c):
    EP = E + 1
    RING = 3
    with ExitStack() as ctx:
        sb = lambda n, s, d=F32: ctx.enter_context(nc.sbuf_tensor(f"m_{n}", s, d))
        W1, W2 = KT * 2 * F, FT * D
        SW = KT * 2 * FS + FST * D
        gate_raw = sb("gate_raw", [P, KT * EP])
        gateH = sb("gateH", [P, KT * EP], F32R)
        gateL = sb("gateL", [P, KT * EP], F32R)
        b1 = sb("b1", [P, E, 2 * FT])
        mult = sb("mult", [P, E, FT])
        sb1 = sb("sb1", [P, 2 * FST])
        smult = sb("smult", [P, FST])
        b2 = sb("b2", [EP, D])
        before = sb("before", [P, E, E])
        comb = sb("comb", [P, NT, EP])
        combT = sb("combT", [EP, S])
        (w_in, gate_hi, gate_lo, const) = semaphores(nc, ctx, "m", "w_in gate_hi gate_lo const")

        with ExitStack() as inner:
            sb = lambda n, s, d=F32: inner.enter_context(nc.sbuf_tensor(f"ms_{n}", s, d))
            raw = sb("raw", [P, SW])
            wH = sb("wH", [P, SW], F32R)
            wL = sb("wL", [P, SW], F32R)
            logT = sb("logT", [EP, S])
            lg = sb("lg", [P, TT, EP])
            peak = sb("peak", [P, TT])
            ex = sb("ex", [P, TT, EP])
            tot = sb("tot", [P, TT])
            score = sb("score", [P, TT, E])
            gt = sb("gt", [P, TT, E * E])
            eq = sb("eq", [P, TT, E * E])
            rank = sb("rank", [P, TT, E])
            gl = sb("gl", [P, 2, S])
            up = sb("up", [P, 2, S])
            act_raw = sb("act_raw", [P, 2, S])
            aH = sb("aH", [P, FST, S], F32R)
            aL = sb("aL", [P, FST, S], F32R)
            (sw_in, sw_hi, sw_lo, log_full, log_copied, logtok_full, shifted, exp_done, step, comb_done, combT_full,
             combT_done, g_full, g_done, x_full, x_read, araw_done, hi_done, a_split, y_full, y_read) = semaphores(
                nc, inner, "ms", "sw_in sw_hi sw_lo log_full log_copied logtok_full shifted exp_done step comb_done "
                "combT_full combT_done g_full g_done x_full x_read araw_done hi_done a_split y_full y_read")
            up_w = lambda m, k: [x[:, k * 2 * FS + m * P:k * 2 * FS + (m + 1) * P] for x in (wH, wL)]
            down_w = lambda k: [x[:, KT * 2 * FS + k * D:KT * 2 * FS + (k + 1) * D] for x in (wH, wL)]
            STEPS = 13
            block = inner.enter_context(nc.Block())

            @block.sync
            def _(sp):
                sp.dma_start(gate_raw[:, :], c.ins["gate"]).then_inc(w_in, DMA)
                for dst, name in ((b1[:, :, :], "b1"), (mult[:, :, :], "mult"), (sb1[:, :], "sb1"), (smult[:, :], "smult"),
                                  (b2[:, :], "b2")):
                    sp.dma_start(dst, c.ins[name]).then_inc(w_in, DMA)
                sp.dma_start(raw[:, :], c.ins["sw"]).then_inc(sw_in, DMA)

            @block.gpsimd
            def _(pool):
                nc.gpsimd.memset(before[:, :, :], 1.0).then_inc(const, 1)
                pool.wait_ge(const, 1)
                nc.gpsimd.affine_select(out=before[:, :, :], in_=before[:, :, :], compare_op=ALU.is_gt, fill=0.0, base=0,
                                        pattern=[[1, E], [-1, E]], channel_multiplier=0).then_inc(const, 1)
                with pool.Fori(0, B) as b:
                    for m in range(FST):
                        pool.wait_ge(araw_done, b * FST + m + 1)
                        apart(pool, c)
                        nc.gpsimd.tensor_copy(aH[:, m, :], act_raw[:, m % 2, :]).then_inc(hi_done, 1)

            @block.scalar
            def _(act):
                act.wait_ge(w_in, 6 * DMA)
                nc.scalar.activation(gateH[:, :], gate_raw[:, :], ACT.Copy).then_inc(gate_hi, 1)
                act.wait_ge(sw_in, DMA)
                nc.scalar.activation(wH[:, :], raw[:, :], ACT.Copy).then_inc(sw_hi, 1)
                with act.Fori(0, B) as b:
                    act.wait_ge(shifted, b + 1)
                    nc.scalar.activation(ex[:, :, :], lg[:, :, :], ACT.Exp).then_inc(exp_done, 1)
                    for m in range(FST):
                        act.wait_ge(g_full, b * FST + m + 1)
                        act.wait_ge(araw_done, b * FST + m - 1) if m >= 2 else None
                        nc.scalar.activation(gl[:, m % 2, :], c.pa[:, m % 4, :], ACT.Gelu,
                                             bias=sb1[:, FST + m:FST + m + 1]).then_inc(g_done, 1)

            @block.vector
            def _(dve):
                dve.sem_inc(x_read, 2)
                dve.sem_inc(y_read, 2)
                dve.wait_ge(gate_hi, 1)
                nc.vector.tensor_tensor(gateL[:, :], gate_raw[:, :], gateH[:, :].bitcast(F32), ALU.subtract).then_inc(gate_lo, 1)
                dve.wait_ge(sw_hi, 1)
                nc.vector.tensor_tensor(wL[:, :], raw[:, :], wH[:, :].bitcast(F32), ALU.subtract).then_inc(sw_lo, 1)
                dve.wait_ge(const, 2)
                with dve.Fori(0, B) as b:
                    dve.wait_ge(log_full, b + 1)
                    nc.vector.tensor_copy(logT[:, :], c.pd[0:EP, 0, :]).then_inc(log_copied, 1)
                    dve.wait_ge(logtok_full, b + 1)
                    nc.vector.reduce_max(peak[:, :], c.pd[:, 1, 0:TT * EP].rearrange("p (t e) -> p t e", e=EP)[:, :, 0:E], AX.X).then_inc(step, 1)
                    dve.wait_ge(step, STEPS * b + 1)
                    nc.vector.tensor_tensor(lg[:, :, :], c.pd[:, 1, 0:TT * EP].rearrange("p (t e) -> p t e", e=EP),
                                            peak[:, :].unsqueeze(2).to_broadcast([P, TT, EP]), ALU.subtract).then_inc(shifted, 1)
                    dve.wait_ge(exp_done, b + 1)
                    nc.vector.reduce_sum(tot[:, :], ex[:, :, 0:E], AX.X).then_inc(step, 1)
                    dve.wait_ge(step, STEPS * b + 2)
                    nc.vector.reciprocal(tot[:, :], tot[:, :]).then_inc(step, 1)
                    dve.wait_ge(step, STEPS * b + 3)
                    nc.vector.tensor_tensor(score[:, :, :], ex[:, :, 0:E], tot[:, :].unsqueeze(2).to_broadcast([P, TT, E]),
                                            ALU.mult).then_inc(step, 1)
                    dve.wait_ge(step, STEPS * b + 4)
                    for t in range(TT):
                        others = score[:, t, :].unsqueeze(1).to_broadcast([P, E, E])
                        own = score[:, t, :].unsqueeze(2).to_broadcast([P, E, E])
                        nc.vector.tensor_tensor(gt[:, t, :].rearrange("p (e f) -> p e f", f=E), others, own, ALU.is_gt)
                        last = nc.vector.tensor_tensor(eq[:, t, :].rearrange("p (e f) -> p e f", f=E), others, own, ALU.is_equal)
                    last.then_inc(step, 1)
                    dve.wait_ge(step, STEPS * b + 5)
                    nc.vector.tensor_tensor(eq[:, :, :], eq[:, :, :], before[:, :, :].rearrange("p e f -> p (e f)").unsqueeze(1)
                                            .to_broadcast([P, TT, E * E]), ALU.mult).then_inc(step, 1)
                    dve.wait_ge(step, STEPS * b + 6)
                    nc.vector.tensor_tensor(gt[:, :, :], gt[:, :, :], eq[:, :, :], ALU.add).then_inc(step, 1)
                    dve.wait_ge(step, STEPS * b + 7)
                    nc.vector.reduce_sum(rank[:, :, :].rearrange("p t e -> p (t e)"),
                                         gt[:, :, :].rearrange("p t (e f) -> p (t e) f", f=E), AX.X).then_inc(step, 1)
                    dve.wait_ge(step, STEPS * b + 8)
                    nc.vector.scalar_tensor_tensor(rank[:, :, :], rank[:, :, :], TOPK - 0.5, score[:, :, :], ALU.is_lt, ALU.mult).then_inc(step, 1)
                    dve.wait_ge(step, STEPS * b + 9)
                    nc.vector.reduce_sum(tot[:, :], rank[:, :, :], AX.X).then_inc(step, 1)
                    dve.wait_ge(step, STEPS * b + 10)
                    nc.vector.tensor_scalar(tot[:, :], tot[:, :], 1e-20, None, ALU.add).then_inc(step, 1)
                    dve.wait_ge(step, STEPS * b + 11)
                    nc.vector.reciprocal(tot[:, :], tot[:, :]).then_inc(step, 1)
                    dve.wait_ge(step, STEPS * b + 12)
                    nc.vector.memset(lg[:, :, E:EP], 1.0)
                    nc.vector.tensor_tensor(lg[:, :, 0:E], rank[:, :, :], tot[:, :].unsqueeze(2).to_broadcast([P, TT, E]),
                                            ALU.mult).then_inc(comb_done, 1)
                    dve.wait_ge(comb_done, b + 1)
                    apart(dve, c)
                    nc.vector.tensor_copy(comb[:, bass.ds(b * TT, TT), :], lg[:, :, :]).then_inc(step, 1)
                    dve.wait_ge(combT_full, b + 1)
                    nc.vector.tensor_copy(combT[:, :], c.pd[0:EP, 0, :]).then_inc(combT_done, 1)
                    for m in range(FST):
                        dve.wait_ge(x_full, b * FST + m + 1)
                        nc.vector.tensor_scalar(up[:, m % 2, :], c.pd[:, 2 + m % 2, :], sb1[:, m:m + 1], smult[:, m:m + 1],
                                                ALU.add, ALU.mult).then_inc(x_read, 1)
                        dve.wait_ge(x_read, b * FST + m + 3)
                        dve.wait_ge(g_done, b * FST + m + 1)
                        if m >= 2:
                            dve.wait_ge(hi_done, b * FST + m - 1)
                        nc.vector.tensor_tensor(act_raw[:, m % 2, :], up[:, m % 2, :], gl[:, m % 2, :], ALU.mult).then_inc(araw_done, 1)
                        dve.wait_ge(hi_done, b * FST + m + 1)
                        nc.vector.tensor_tensor(aL[:, m, :], act_raw[:, m % 2, :], aH[:, m, :].bitcast(F32), ALU.subtract).then_inc(a_split, 1)
                    for n in range(2):
                        dve.wait_ge(y_full, 2 * b + n + 1)
                        xb = c.X[:, bass.ds(b * TT + 2 * n, 2), :].rearrange("p n d -> p (n d)")
                        nc.vector.tensor_tensor(xb, c.pd[:, n, :], xb, ALU.add).then_inc(y_read, 1)

            @block.tensor
            def _(pe):
                pe.wait_ge(gate_lo, 1)
                pe.wait_ge(sw_lo, 1)
                with pe.Fori(0, B) as b:
                    xn = lambda k: [x[:, k, bass.ds(b * S, S)] for x in (c.xnH, c.xnL)]
                    pe.wait_ge(y_read, 2 * b + 2)
                    for k in range(KT):
                        last = hi_lo(pe, nc, c.pd[0:EP, 0, :], [x[:, k * EP:(k + 1) * EP] for x in (gateH, gateL)], xn(k),
                                     k == 0, k == KT - 1)
                    last.then_inc(log_full, 1)
                    pe.wait_ge(log_copied, b + 1)
                    apart(pe, c)
                    for t in range(TT):
                        last = nc.tensor.transpose(c.pd[:, 1, t * EP:(t + 1) * EP], logT[:, t * P:(t + 1) * P], c.ident[0:EP, 0:EP])
                    last.then_inc(logtok_full, 1)
                    for m in range(FST):
                        if m == 2:
                            pe.wait_ge(comb_done, b + 1)
                            for t in range(TT):
                                last = nc.tensor.transpose(c.pd[0:EP, 0, t * P:(t + 1) * P], lg[:, t, :], c.ident[:, :])
                            last.then_inc(combT_full, 1)
                        for k in range(KT):
                            last = hi_lo(pe, nc, c.pa[:, m % 4, :], up_w(FST + m, k), xn(k), k == 0, k == KT - 1)
                        last.then_inc(g_full, 1)
                        pe.wait_ge(x_read, b * FST + m + 1)
                        for k in range(KT):
                            last = hi_lo(pe, nc, c.pd[:, 2 + m % 2, :], up_w(m, k), xn(k), k == 0, k == KT - 1)
                        last.then_inc(x_full, 1)
                    pe.wait_ge(combT_done, b + 1)
                    pe.wait_ge(a_split, b * FST + FST)
                    for n in range(2):
                        for t in (2 * n, 2 * n + 1):
                            out = c.pd[:, n, (t % 2) * D:(t % 2 + 1) * D]
                            nc.tensor.matmul(out, combT[:, t * P:(t + 1) * P], b2[:, :], start=True, stop=False)
                            for k in range(FST):
                                last = hi_lo(pe, nc, out, [x[:, k, t * P:(t + 1) * P] for x in (aH, aL)], down_w(k),
                                             False, k == FST - 1)
                        last.then_inc(y_full, 1)

        with ExitStack() as inner:
            sb = lambda n, s, d=F32: inner.enter_context(nc.sbuf_tensor(f"me_{n}", s, d))
            raw = sb("raw", [P, RING, W1 + W2])
            wH = sb("wH", [P, RING, W1 + W2], F32R)
            wL = sb("wL", [P, RING, W1 + W2], F32R)
            gl = sb("gl", [P, 2, FT, S])
            up = sb("up", [P, 2, FT, S])
            act_raw = sb("act_raw", [P, 2, FT, S])
            aH = sb("aH", [P, 2, FT, S], F32R)
            aL = sb("aL", [P, 2, FT, S], F32R)
            w_ins = semaphores(nc, inner, "me", "w_in0 w_in1 w_in2")
            (w_hi, w_lo, g_full, g_done, x_full, x_read, araw_done, hi_done, a_split, y_full, y_read) = semaphores(
                nc, inner, "me", "w_hi w_lo g_full g_done x_full x_read araw_done hi_done a_split y_full y_read")
            up_w = lambda s, m, k: [x[:, s, k * 2 * F + m * P:k * 2 * F + (m + 1) * P] for x in (wH, wL)]
            down_w = lambda s, k: [x[:, s, W1 + k * D:W1 + (k + 1) * D] for x in (wH, wL)]
            PER = RING * B
            block = inner.enter_context(nc.Block())

            @block.sync
            def _(sp):
                with sp.Fori(0, E // RING) as i:
                    for s in range(RING):
                        sp.wait_ge(w_lo, i * RING + s + 1)
                        sp.dma_start(raw[:, s, :], c.ins["ew"][bass.ds(i * RING + s, 1), :, :].rearrange("o p n -> (o p) n")).then_inc(w_ins[s], DMA)

            @block.gpsimd
            def _(pool):
                pool.sem_inc(w_lo, RING)

                def keep_lo(i, s):
                    pool.wait_ge(w_hi, i * RING + s + 1)
                    nc.gpsimd.tensor_tensor(wL[:, s, :], raw[:, s, :], wH[:, s, :].bitcast(F32), ALU.subtract).then_inc(w_lo, 1)

                with pool.Fori(0, E // RING) as i:
                    keep_lo(i, 0)
                    for s in range(RING):
                        for b in range(B):
                            n = s * B + b
                            if b == 2 and s + 1 < RING:
                                keep_lo(i, s + 1)
                            pool.wait_ge(araw_done, i * PER + n + 1)
                            apart(pool, c)
                            nc.gpsimd.tensor_copy(aH[:, n % 2, :, :], act_raw[:, n % 2, :, :]).then_inc(hi_done, 1)

            @block.scalar
            def _(act):
                def keep_hi(i, s):
                    act.wait_ge(w_ins[s], i * DMA + DMA)
                    act.wait_ge(y_full, (i * PER + (s + 1) * B) * 2)
                    nc.scalar.activation(wH[:, s, :], raw[:, s, :], ACT.Copy).then_inc(w_hi, 1)

                with act.Fori(0, E // RING) as i:
                    keep_hi(i, 0)
                    for s in range(RING):
                        for b in range(B):
                            n = s * B + b
                            if b == 2 and s + 1 < RING:
                                keep_hi(i, s + 1)
                            for f in range(FT):
                                if n >= 2:
                                    act.wait_ge(araw_done, i * PER + n - 1)
                                act.wait_ge(g_full, (i * PER + n) * FT + f + 1)
                                apart(act, c)
                                nc.scalar.activation(gl[:, n % 2, f, :], c.pa[:, (n % 2) * 2 + f, :], ACT.Gelu,
                                                     bias=b1[:, bass.ds(i * RING + s, 1), FT + f:FT + f + 1].rearrange("p o f -> p (o f)")).then_inc(g_done, 1)

            @block.vector
            def _(dve):
                dve.sem_inc(x_read, 2)
                dve.sem_inc(y_read, 2)
                with dve.Fori(0, E // RING) as i:
                    for s in range(RING):
                        e1 = bass.ds(i * RING + s, 1)
                        for b in range(B):
                            n = s * B + b
                            for f in range(FT):
                                dve.wait_ge(x_full, (i * PER + n) * FT + f + 1)
                                nc.vector.tensor_scalar(up[:, n % 2, f, :], c.pd[:, f, :], b1[:, e1, f:f + 1].rearrange("p o f -> p (o f)"),
                                                        mult[:, e1, f:f + 1].rearrange("p o f -> p (o f)"), ALU.add, ALU.mult).then_inc(x_read, 1)
                            dve.wait_ge(g_done, (i * PER + n) * FT + FT + 2 * FT)
                            dve.wait_ge(x_read, (i * PER + n) * FT + FT + 2)
                            nc.vector.tensor_tensor(act_raw[:, n % 2, :, :], up[:, n % 2, :, :], gl[:, n % 2, :, :], ALU.mult).then_inc(araw_done, 1)
                            dve.wait_ge(hi_done, i * PER + n + 1)
                            nc.vector.tensor_tensor(aL[:, n % 2, :, :], act_raw[:, n % 2, :, :], aH[:, n % 2, :, :].bitcast(F32),
                                                    ALU.subtract).then_inc(a_split, 1)
                            for t in range(TT):
                                if t % 2 == 0:
                                    dve.wait_ge(y_full, (i * PER + n) * 2 + t // 2 + 1 + 2 * PER)
                                xt = c.X[:, b * TT + t, :]
                                last = nc.vector.scalar_tensor_tensor(xt, c.pd[:, 2 + t // 2, (t % 2) * D:(t % 2 + 1) * D],
                                                                      comb[:, b * TT + t, e1], xt, ALU.mult, ALU.add)
                                if t % 2 == 1:
                                    last.then_inc(y_read, 1)

            @block.tensor
            def _(pe):
                pe.sem_inc(y_full, 2 * PER)
                pe.sem_inc(g_done, 2 * FT)

                def second_layer(i, s, b):
                    n = s * B + b
                    pe.wait_ge(a_split, i * PER + n + 1)
                    for h in range(2):
                        pe.wait_ge(y_read, (i * PER + n) * 2 + h + 1)
                        for t in (2 * h, 2 * h + 1):
                            for k in range(FT):
                                last = hi_lo(pe, nc, c.pd[:, 2 + h, (t % 2) * D:(t % 2 + 1) * D],
                                             [x[:, n % 2, k, t * P:(t + 1) * P] for x in (aH, aL)], down_w(s, k), k == 0, k == FT - 1)
                        last.then_inc(y_full, 1)

                with pe.Fori(0, E // RING) as i:
                    for s in range(RING):
                        pe.wait_ge(w_lo, i * RING + s + RING + 1)
                        for b in range(B):
                            n = s * B + b
                            for f in range(FT):
                                pe.wait_ge(g_done, (i * PER + n) * FT + f + 1)
                                for k in range(KT):
                                    last = hi_lo(pe, nc, c.pa[:, (n % 2) * 2 + f, :], up_w(s, FT + f, k),
                                                 [x[:, k, b * S:(b + 1) * S] for x in (c.xnH, c.xnL)], k == 0, k == KT - 1)
                                last.then_inc(g_full, 1)
                                pe.wait_ge(x_read, (i * PER + n) * FT + f + 1)
                                for k in range(KT):
                                    last = hi_lo(pe, nc, c.pd[:, f, :], up_w(s, f, k),
                                                 [x[:, k, b * S:(b + 1) * S] for x in (c.xnH, c.xnL)], k == 0, k == KT - 1)
                                last.then_inc(x_full, 1)
                            if n:
                                second_layer(i, (n - 1) // B, (n - 1) % B)
                    second_layer(i, RING - 1, B - 1)


def second_projection_phase(nc, c):
    USES = 6
    with ExitStack() as ctx:
        sb = lambda n, s, d=F32: ctx.enter_context(nc.sbuf_tensor(f"p_{n}", s, d))
        raw = sb("raw", [P, 3, KT * D])
        wH = sb("wH", [P, 3, KT * D], F32R)
        wL = sb("wL", [P, 3, KT * D], F32R)
        ctx_raw = sb("ctx_raw", [P, KT, S])
        ctxH = sb("ctxH", [P, KT, S], F32R)
        ctxL = sb("ctxL", [P, KT, S], F32R)
        qkH = sb("qkH", [P, 2 * KT, S], F32R)
        qkL = sb("qkL", [P, 2 * KT, S], F32R)
        V = sb("V", [P, TT, H1, 2 * DH1])
        (w_in, w_hi, w_lo, const, ctx_in, ctx_hi, ctx_lo, use_full, hi_done, use_read, stored) = semaphores(
            nc, ctx, "p", "w_in w_hi w_lo const ctx_in ctx_hi ctx_lo use_full hi_done use_read stored")
        STORES = 5 * DMA
        block = ctx.enter_context(nc.Block())

        @block.sync
        def _(sp):
            for n, name in enumerate(("wq1", "wk1", "wv1")):
                sp.dma_start(raw[:, n, :], c.ins[name]).then_inc(w_in, DMA)
            with sp.Fori(0, B) as b:
                sp.wait_ge(ctx_lo, b + 1)
                sp.dma_start(ctx_raw[:, :, :], c.ins["ctx"][:, :, bass.ds(b * S, S)]).then_inc(ctx_in, DMA)
                for n, part in enumerate((c.q_dram, c.k_dram)):
                    sp.wait_ge(use_read, b * USES + 2 * n + 2 + 3)
                    for l, src in enumerate((qkH, qkL)):
                        sp.dma_start(part[bass.ds(b, 1), l, :, :].rearrange("o (m p) t -> p (o m) t", p=P),
                                     src[:, n * KT:(n + 1) * KT, :].bitcast(F32)).then_inc(stored, DMA)
                sp.wait_ge(use_read, b * USES + USES + 3)
                sp.dma_start(c.v_dram[bass.ds(b, 1), :, :].rearrange("o p n -> (o p) n"),
                             V[:, :, :, :].rearrange("p t h d -> p (t h d)")).then_inc(stored, DMA)
            sp.wait_ge(stored, (B + 1) * STORES)

        @block.gpsimd
        def _(pool):
            nc.gpsimd.memset(V[:, :, :, :], 1.0).then_inc(const, 1)

        @block.scalar
        def _(act):
            act.sem_inc(stored, STORES)
            act.wait_ge(w_in, 3 * DMA)
            nc.scalar.activation(wH[:, :, :], raw[:, :, :], ACT.Copy).then_inc(w_hi, 1)
            with act.Fori(0, B) as b:
                act.wait_ge(ctx_in, b * DMA + DMA)
                nc.scalar.activation(ctxH[:, :, :], ctx_raw[:, :, :], ACT.Copy).then_inc(ctx_hi, 1)
                act.wait_ge(stored, b * STORES + STORES)
                for u in range(2 * KT):
                    act.wait_ge(use_full, b * USES + u + 1)
                    nc.scalar.activation(qkH[:, u, :], c.pd[:, u % 3, :], ACT.Copy).then_inc(hi_done, 1)

        @block.vector
        def _(dve):
            dve.sem_inc(use_read, 3)
            dve.sem_inc(ctx_lo, 1)
            dve.wait_ge(w_hi, 1)
            nc.vector.tensor_tensor(wL[:, :, :], raw[:, :, :], wH[:, :, :].bitcast(F32), ALU.subtract).then_inc(w_lo, 1)
            dve.wait_ge(const, 1)
            with dve.Fori(0, B) as b:
                dve.wait_ge(ctx_hi, b + 1)
                nc.vector.tensor_tensor(ctxL[:, :, :], ctx_raw[:, :, :], ctxH[:, :, :].bitcast(F32), ALU.subtract).then_inc(ctx_lo, 1)
                for u in range(2 * KT):
                    dve.wait_ge(hi_done, b * 2 * KT + u + 1)
                    nc.vector.tensor_tensor(qkL[:, u, :], c.pd[:, u % 3, :], qkH[:, u, :].bitcast(F32), ALU.subtract).then_inc(use_read, 1)
                for n in range(2):
                    u = 2 * KT + n
                    dve.wait_ge(use_full, b * USES + u + 1)
                    dve.wait_ge(stored, b * STORES + STORES)
                    nc.vector.tensor_copy(V[:, 2 * n:2 * n + 2, :, 0:DH1],
                                          c.pd[:, u % 3, :].rearrange("p (t h d) -> p t h d", t=2, d=DH1)).then_inc(use_read, 1)

        @block.tensor
        def _(pe):
            pe.wait_ge(w_lo, 1)
            weight = lambda w, k, lo, n: [x[:, w, k * D + lo:k * D + lo + n] for x in (wH, wL)]
            with pe.Fori(0, B) as b:
                for u in range(2 * KT):
                    if u == KT:
                        pe.wait_ge(ctx_lo, b + 2)
                    pe.wait_ge(use_read, b * USES + u + 1)
                    for k in range(KT):
                        move = [x[:, k, bass.ds(b * S, S)] for x in (c.xnH, c.xnL)] if u < KT else [x[:, k, :] for x in (ctxH, ctxL)]
                        last = hi_lo(pe, nc, c.pd[:, u % 3, :], weight(u // KT, k, (u % KT) * P, P), move, k == 0, k == KT - 1)
                    last.then_inc(use_full, 1)
                for n in range(2):
                    u = 2 * KT + n
                    pe.wait_ge(use_read, b * USES + u + 1)
                    for t in (2 * n, 2 * n + 1):
                        for k in range(KT):
                            last = hi_lo(pe, nc, c.pd[:, u % 3, (t % 2) * D:(t % 2 + 1) * D],
                                         [x[:, k, t * P:(t + 1) * P] for x in (ctxH, ctxL)], weight(2, k, 0, D), k == 0, k == KT - 1)
                    last.then_inc(use_full, 1)


def second_attention_phase(nc, c):
    R = 2 * DH1
    with ExitStack() as ctx:
        sb = lambda n, s, d=F32: ctx.enter_context(nc.sbuf_tensor(f"b_{n}", s, d))
        q4 = sb("q4", [P, 2, GH, S], F32R)
        k4 = sb("k4", [P, 2, GH, S], F32R)
        AUX = 4 * DH1
        V = sb("V", [P, TT, H1, R])
        zeros = sb("zeros", [1, GH * S])
        mask_in = sb("mask_in", [P, 2, TT, S], U8)
        by_query = sb("by_query", [P, TT, S])
        by_key = sb("by_key", [P, TT, S], BF16)
        ident_bf = sb("ident_bf", [P, P], BF16)
        select = sb("select", [P, P])
        masked = sb("masked", [P, 2, S], BF16)
        mx = sb("mx", [P, 4, TT])
        prob = sb("prob", [P, 2, GH, TT, S])
        raw = sb("raw", [P, GROUPS * D])
        woH = sb("woH", [P, GROUPS * D], F32R)
        woL = sb("woL", [P, GROUPS * D], F32R)
        osum = sb("osum", [P, 2, S])
        inv = sb("inv", [P, S])
        oH = sb("oH", [P, GROUPS, S], F32R)
        oL = sb("oL", [P, GROUPS, S], F32R)
        (const, w_in, mask_loaded, w_hi, w_lo, mask_done, v_in, qk_in0, qk_in1, s_full, s_read, row_full, row_done, st_full,
         exp_done, pv_full, osum_done, sel_full, sel_read, norm_step, o_split, y_full, y_read) = semaphores(
            nc, ctx, "b", "const w_in mask_loaded w_hi w_lo mask_done v_in qk_in0 qk_in1 s_full s_read row_full row_done st_full "
            "exp_done pv_full osum_done sel_full sel_read norm_step o_split y_full y_read")
        qk_ins = (qk_in0, qk_in1)
        QK_LOADS = 9 * DMA
        PV_LAG = 5
        block = ctx.enter_context(nc.Block())

        @block.sync
        def _(sp):
            sp.dma_start(raw[:, :], c.ins["wo1"]).then_inc(w_in, DMA)
            sp.dma_start(mask_in[:, 0, :, :], c.ins["mask"].rearrange("(n p) k -> p n k", p=P)).then_inc(mask_loaded, DMA)
            sp.dma_start(mask_in[:, 1, :, :], c.ins["maskT"].rearrange("(n p) k -> p n k", p=P)).then_inc(mask_loaded, DMA)
            sp.wait_ge(const, 6)
            with sp.Fori(0, B) as b:
                for g in range(GROUPS):
                    sp.wait_ge(st_full, b * 2 * H1 + (g + 1) * 2 * GH)
                    rows = lambda part, l: part[bass.ds(b, 1), l, g * GH * DH1:(g + 1) * GH * DH1, :].rearrange("o (h d) t -> d (o h) t", d=DH1)
                    done = qk_ins[g % 2]
                    for r, (ql, kl) in enumerate(((0, 0), (1, 0), (0, 1), (1, 1))):
                        at = slice(r * DH1, (r + 1) * DH1)
                        sp.dma_start(q4[at, g % 2, :, :].bitcast(F32), rows(c.q_dram, ql)).then_inc(done, DMA)
                        sp.dma_start(k4[at, g % 2, :, :].bitcast(F32), rows(c.k_dram, kl)).then_inc(done, DMA)
                    sp.dma_start(q4[AUX:AUX + 1, g % 2, :, :].rearrange("p h s -> p (h s)").bitcast(F32), zeros[:, :]).then_inc(done, DMA)
                    if g == 0:
                        sp.wait_ge(pv_full, b * GROUPS + 2)
                        sp.dma_start(V[:, :, :, :].rearrange("p t h d -> p (t h d)"),
                                     c.v_dram[bass.ds(b, 1), :, :].rearrange("o p n -> (o p) n")).then_inc(v_in, DMA)

        @block.gpsimd
        def _(pool):
            nc.gpsimd.memset(zeros[:, :], 0.0).then_inc(const, 1)
            nc.gpsimd.memset(q4[AUX:P, :, :, :].bitcast(F32), 0.0).then_inc(const, 1)
            nc.gpsimd.memset(k4[AUX:P, :, :, :].bitcast(F32), 0.0).then_inc(const, 1)
            pool.wait_ge(const, 3)
            nc.gpsimd.memset(k4[AUX:AUX + 1, :, :, :].bitcast(F32), 1.0).then_inc(const, 1)
            pool.wait_ge(const, 4)
            nc.gpsimd.memset(select[:, :], 0.0).then_inc(const, 1)
            pool.wait_ge(const, 5)
            sel = select[:, :].rearrange("p (h r) -> p h r", r=R)
            nc.gpsimd.affine_select(out=sel, in_=sel, compare_op=ALU.not_equal, fill=1.0, base=-DH1,
                                    pattern=[[-R, GH], [0, R]], channel_multiplier=1).then_inc(const, 1)

        @block.scalar
        def _(act):
            act.wait_ge(w_in, DMA)
            nc.scalar.activation(woH[:, :], raw[:, :], ACT.Copy).then_inc(w_hi, 1)
            act.wait_ge(mask_loaded, 2 * DMA)
            nc.scalar.activation(by_key[:, :, :], mask_in[:, 1, :, :], ACT.Copy, scale=MASKED).then_inc(mask_done, 1)
            nc.scalar.activation(ident_bf[:, :], c.ident[:, :], ACT.Copy).then_inc(mask_done, 1)
            with act.Fori(0, B) as b:
                def keep_sums(g):
                    act.wait_ge(pv_full, b * GROUPS + g + 1 + 2)
                    act.wait_ge(o_split, b * GROUPS + g + 1)
                    nc.scalar.activation(osum[:, g % 2, :], c.pd[:, 2, :], ACT.Copy).then_inc(osum_done, 1)

                for n in range(H1):
                    g, i = n // GH, n % GH
                    act.wait_ge(row_full, b * H1 + n + 1)
                    nc.scalar.activation(q4[AUX:AUX + 1, g % 2, i, :], c.pd[0:1, 3, :], ACT.Copy, scale=-1.0).then_inc(row_done, 1)
                    if i == 0 and g >= 2:
                        keep_sums(g - 2)
                    for half in range(2):
                        act.wait_ge(st_full, (b * H1 + n) * 2 + half + 1 + 4 * GH)
                        act.wait_ge(pv_full, b * GROUPS + g + 1)
                        nc.scalar.activation(prob[:, g % 2, i, 2 * half:2 * half + 2, :], c.pa[:, 2 * half:2 * half + 2, :], ACT.Exp,
                                             scale=DH1 ** -0.5).then_inc(exp_done, 1)
                keep_sums(2)
                keep_sums(3)

        @block.vector
        def _(dve):
            dve.sem_inc(s_read, 2)
            dve.sem_inc(o_split, 2)
            dve.sem_inc(y_read, 2)
            dve.sem_inc(sel_read, 1)
            dve.wait_ge(w_hi, 1)
            nc.vector.tensor_tensor(woL[:, :], raw[:, :], woH[:, :].bitcast(F32), ALU.subtract).then_inc(w_lo, 1)
            dve.wait_ge(mask_loaded, 2 * DMA)
            nc.vector.tensor_scalar(by_query[:, :, :], mask_in[:, 0, :, :], MASKED, None, ALU.mult).then_inc(mask_done, 1)
            dve.wait_ge(mask_done, 3)
            with dve.Fori(0, B) as b:
                def normalise(g):
                    G = b * GROUPS + g
                    dve.wait_ge(sel_full, G + 1)
                    dve.wait_ge(o_split, G + 2)
                    nc.vector.tensor_scalar(inv[:, :], c.pd[:, 3, :], 1e-30, None, ALU.max).then_inc(sel_read, 1)
                    dve.wait_ge(sel_read, G + 2)
                    nc.vector.reciprocal(inv[:, :], inv[:, :]).then_inc(norm_step, 1)
                    dve.wait_ge(norm_step, 3 * G + 1)
                    nc.vector.tensor_tensor(inv[:, :], osum[:, g % 2, :], inv[:, :], ALU.mult).then_inc(norm_step, 1)
                    dve.wait_ge(norm_step, 3 * G + 2)
                    nc.vector.tensor_copy(oH[:, g, :], inv[:, :]).then_inc(norm_step, 1)
                    dve.wait_ge(norm_step, 3 * G + 3)
                    nc.vector.tensor_tensor(oL[:, g, :], inv[:, :], oH[:, g, :].bitcast(F32), ALU.subtract).then_inc(o_split, 1)

                for n in range(H1):
                    for t in range(TT):
                        dve.wait_ge(s_full, (b * H1 + n) * TT + t + 1)
                        dve.wait_ge(s_read, (b * H1 + n) * TT + t + 1)
                        apart(dve, c)
                        nc.vector.tensor_tensor_reduce(masked[:, t % 2, :], c.pd[:, t % 2, :], by_query[:, t, :], 1.0, LEAST_MAX, ALU.add, ALU.max,
                                                       accum_out=mx[:, n % 4, t:t + 1]).then_inc(s_read, 1)
                    if n >= 2 * GH and n % GH == 3:
                        normalise(n // GH - 2)
                normalise(2)
                normalise(3)
                for n in range(2):
                    dve.wait_ge(y_full, 2 * b + n + 1)
                    xb = c.X[:, bass.ds(b * TT + 2 * n, 2), :].rearrange("p n d -> p (n d)")
                    nc.vector.tensor_tensor(xb, c.pd[:, 2 + n, :], xb, ALU.add).then_inc(y_read, 1)

        @block.tensor
        def _(pe):
            pe.sem_inc(st_full, 4 * GH)
            pe.sem_inc(pv_full, 2)
            pe.sem_inc(row_done, 1)
            pe.sem_inc(osum_done, 1)
            pe.sem_inc(exp_done, 2)
            pe.wait_ge(const, 6)
            pe.wait_ge(w_lo, 1)
            pe.wait_ge(mask_done, 3)
            with pe.Fori(0, B) as b:
                def by_query_scores(n):
                    g, i = n // GH, n % GH
                    if i == 0:
                        pe.wait_ge(qk_ins[g % 2], (b * 2 + g // 2 + 1) * QK_LOADS)
                    for t in range(TT):
                        pe.wait_ge(s_read, (b * H1 + n) * TT + t + 1)
                        nc.tensor.matmul(c.pd[:, t % 2, :], q4[:, g % 2, i, t * P:(t + 1) * P], k4[:, g % 2, i, :],
                                         start=True, stop=True).then_inc(s_full, 1)

                def max_row(n):
                    pe.wait_ge(s_read, (b * H1 + n) * TT + TT + 2)
                    pe.wait_ge(row_done, b * H1 + n + 1)
                    pe.wait_ge(sel_read, b * GROUPS + 1 + max(0, (n - 6) // GH))
                    pe.wait_ge(y_read, 2 * b + 2)
                    for t in range(TT):
                        last = nc.tensor.transpose(c.pd[0:1, 3, t * P:(t + 1) * P], mx[:, n % 4, t:t + 1], c.ident[:, :])
                    last.then_inc(row_full, 1)

                def by_key_scores(n):
                    g, i = n // GH, n % GH
                    pe.wait_ge(row_done, b * H1 + n + 2)
                    for half in range(2):
                        pe.wait_ge(exp_done, (b * H1 + n) * 2 + half + 1)
                        for t in (2 * half, 2 * half + 1):
                            nc.tensor.matmul(c.pa[:, t, :], k4[:, g % 2, i, t * P:(t + 1) * P], q4[:, g % 2, i, :], start=True, stop=False)
                            last = nc.tensor.matmul(c.pa[:, t, :], ident_bf[:, :], by_key[:, t, :], start=False, stop=True)
                        last.then_inc(st_full, 1)

                def values(g, t):
                    if t == 0:
                        if g == 0:
                            pe.wait_ge(v_in, b * DMA + DMA)
                        pe.wait_ge(exp_done, (b * H1 + (g + 1) * GH) * 2 + 2)
                        pe.wait_ge(osum_done, b * GROUPS + g + 1)
                    for i in range(GH):
                        last = nc.tensor.matmul(c.pd[i * R:(i + 1) * R, 2, :], V[:, t, g * GH + i, :], prob[:, g % 2, i, t, :],
                                                start=t == 0, stop=t == TT - 1, tile_position=(0, i * R))
                    if t == TT - 1:
                        last.then_inc(pv_full, 1)

                def spread_sums(g, n):
                    pe.wait_ge(osum_done, b * GROUPS + g + 2)
                    pe.wait_ge(row_done, b * H1 + n + 2)
                    pe.wait_ge(sel_read, b * GROUPS + g + 1)
                    nc.tensor.matmul(c.pd[:, 3, :], select[:, :], osum[:, g % 2, :], start=True, stop=True).then_inc(sel_full, 1)

                by_query_scores(0)
                by_query_scores(1)
                for n in range(H1):
                    max_row(n)
                    if n + 2 < H1:
                        by_query_scores(n + 2)
                    if n >= PV_LAG:
                        values((n - PV_LAG) // GH, (n - PV_LAG) % GH)
                    if n >= PV_LAG + GH and n % GH == PV_LAG % GH:
                        spread_sums((n - PV_LAG) // GH - 1, n)
                    by_key_scores(n)
                for m in range(H1 - PV_LAG, H1):
                    if m % GH == 0:
                        spread_sums(m // GH - 1, H1 - 1)
                    values(m // GH, m % GH)
                spread_sums(3, H1 - 1)
                pe.wait_ge(o_split, b * GROUPS + GROUPS + 2)
                for n in range(2):
                    for t in (2 * n, 2 * n + 1):
                        for k in range(GROUPS):
                            last = hi_lo(pe, nc, c.pd[:, 2 + n, (t % 2) * D:(t % 2 + 1) * D], [x[:, k, t * P:(t + 1) * P] for x in (oH, oL)],
                                         [x[:, k * D:(k + 1) * D] for x in (woH, woL)], k == 0, k == GROUPS - 1)
                    last.then_inc(y_full, 1)


def first_ffn_phase(nc, c):
    CHUNK = HID
    CHUNKS = 2 * KT + HT
    with ExitStack() as ctx:
        sb = lambda n, s, d=F32: ctx.enter_context(nc.sbuf_tensor(f"f_{n}", s, d))
        raw = sb("raw", [P, 2, CHUNK])
        wH = sb("wH", [P, CHUNKS, CHUNK], F32R)
        wL = sb("wL", [P, CHUNKS, CHUNK], F32R)
        scales = sb("scales", [P, 3, HT])
        gate = sb("gate", [P, 2, S])
        h_raw = sb("h_raw", [P, 2, S])
        hH = sb("hH", [P, HT, S], F32R)
        hL = sb("hL", [P, HT, S], F32R)
        hidden = sb("hidden", [P, 2, S])
        (w_in0, w_in1, scales_in, w_hi, w_lo, gate_full, gate_done, up_full, h_done, hi_done, split, hid_full, hid_done, stored0,
         stored1) = semaphores(nc, ctx, "f", "w_in0 w_in1 scales_in w_hi w_lo gate_full gate_done up_full h_done hi_done split hid_full "
                               "hid_done stored0 stored1")
        w_ins, stores = (w_in0, w_in1), (stored0, stored1)
        weight = lambda w, m: [x[:, w, m * P:(m + 1) * P] for x in (wH, wL)]
        block = ctx.enter_context(nc.Block())

        @block.sync
        def _(sp):
            sp.dma_start(scales[:, :, :], c.ins["ffn_scales"]).then_inc(scales_in, DMA)
            for n in range(CHUNKS):
                if n >= 2:
                    sp.wait_ge(w_lo, n - 1)
                sp.dma_start(raw[:, n % 2, :], c.ins["ffn_w"][n]).then_inc(w_ins[n % 2], DMA)
            with sp.Fori(0, B) as b:
                for m in range(HT):
                    sp.wait_ge(hid_done, b * HT + m + 1)
                    sp.dma_start(c.hidden_dram[bass.ds(b, 1), :, m, :].rearrange("o p t -> (o p) t"),
                                 hidden[:, m % 2, :]).then_inc(stores[m % 2], DMA)
            for done in stores:
                sp.wait_ge(done, (B * HT // 2 + 1) * DMA)

        @block.gpsimd
        def _(pool):
            pass

        @block.scalar
        def _(act):
            act.sem_inc(stored0, DMA)
            act.sem_inc(stored1, DMA)
            for n in range(CHUNKS):
                act.wait_ge(w_ins[n % 2], (n // 2 + 1) * DMA)
                nc.scalar.activation(wH[:, n, :], raw[:, n % 2, :], ACT.Copy).then_inc(w_hi, 1)
            act.wait_ge(scales_in, DMA)
            with act.Fori(0, B) as b:
                for m in range(HT):
                    act.wait_ge(gate_full, b * HT + m + 1)
                    act.wait_ge(h_done, b * HT + m + 1)
                    nc.scalar.activation(gate[:, m % 2, :], c.pa[:, m % 2, :], ACT.Silu, scale=scales[:, 0, m:m + 1]).then_inc(gate_done, 1)
                for m in range(HT):
                    act.wait_ge(hid_full, b * HT + m + 2)
                    act.wait_ge(stores[m % 2], (b * HT // 2 + m // 2 + 1) * DMA)
                    nc.scalar.activation(hidden[:, m % 2, :], c.pa[:, 2 + m % 2, :], ACT.Gelu, scale=scales[:, 2, m:m + 1]).then_inc(hid_done, 1)

        @block.vector
        def _(dve):
            dve.sem_inc(h_done, 2)
            dve.sem_inc(split, 2)
            for n in range(CHUNKS):
                dve.wait_ge(w_hi, n + 1)
                nc.vector.tensor_tensor(wL[:, n, :], raw[:, n % 2, :], wH[:, n, :].bitcast(F32), ALU.subtract).then_inc(w_lo, 1)
            dve.wait_ge(scales_in, DMA)
            with dve.Fori(0, B) as b:
                for m in range(HT):
                    dve.wait_ge(up_full, b * HT + m + 1)
                    dve.wait_ge(gate_done, b * HT + m + 1)
                    dve.wait_ge(split, b * HT + m + 1)
                    nc.vector.scalar_tensor_tensor(h_raw[:, m % 2, :], c.pd[:, m % 2, :], scales[:, 1, m:m + 1], gate[:, m % 2, :],
                                                   ALU.mult, ALU.mult).then_inc(h_done, 1)
                    dve.wait_ge(h_done, b * HT + m + 3)
                    if m == 0:
                        dve.wait_ge(hid_full, b * HT + 1)
                    nc.vector.tensor_copy(hH[:, m, :], h_raw[:, m % 2, :]).then_inc(hi_done, 1)
                    dve.wait_ge(hi_done, b * HT + m + 1)
                    nc.vector.tensor_tensor(hL[:, m, :], h_raw[:, m % 2, :], hH[:, m, :].bitcast(F32), ALU.subtract).then_inc(split, 1)

        @block.tensor
        def _(pe):
            pe.sem_inc(hid_full, 1)
            pe.wait_ge(w_lo, CHUNKS)
            with pe.Fori(0, B) as b:
                xn = lambda k: [x[:, k, bass.ds(b * S, S)] for x in (c.xnH, c.xnL)]
                for m in range(HT):
                    pe.wait_ge(h_done, b * HT + m + 1)
                    for k in range(KT):
                        last = hi_lo(pe, nc, c.pa[:, m % 2, :], weight(k, m), xn(k), k == 0, k == KT - 1)
                    last.then_inc(gate_full, 1)
                    for k in range(KT):
                        last = hi_lo(pe, nc, c.pd[:, m % 2, :], weight(KT + k, m), xn(k), k == 0, k == KT - 1)
                    last.then_inc(up_full, 1)
                for m in range(HT):
                    if m >= 2:
                        pe.wait_ge(hid_done, b * HT + m - 1)
                    for k in range(HT):
                        if m == 0:
                            pe.wait_ge(split, b * HT + k + 3)
                        last = hi_lo(pe, nc, c.pa[:, 2 + m % 2, :], weight(2 * KT + k, m), [x[:, k, :] for x in (hH, hL)], k == 0, k == HT - 1)
                    last.then_inc(hid_full, 1)


def second_ffn_phase(nc, c):
    CHUNK = HID
    CHUNKS = HT + 2
    with ExitStack() as ctx:
        sb = lambda n, s, d=F32: ctx.enter_context(nc.sbuf_tensor(f"g_{n}", s, d))
        raw = sb("raw", [P, 2, CHUNK])
        wH = sb("wH", [P, CHUNKS, CHUNK], F32R)
        wL = sb("wL", [P, CHUNKS, CHUNK], F32R)
        scales = sb("scales", [P, HT])
        out_scale = sb("out_scale", [P, 2, D])
        hidden = sb("hidden", [P, HT, S])
        hH = sb("hH", [P, HT, S], F32R)
        hL = sb("hL", [P, HT, S], F32R)
        z_raw = sb("z_raw", [P, 2, S])
        zH = sb("zH", [P, HT, S], F32R)
        zL = sb("zL", [P, HT, S], F32R)
        y = sb("y", [P, 2, 2, D])
        (w_in0, w_in1, scales_in, w_hi, w_lo, hid_in, hid_hi, hid_lo, z_full, z_done, z_hi, z_split, y_full, y_scaled, y_done,
         stored) = semaphores(nc, ctx, "g", "w_in0 w_in1 scales_in w_hi w_lo hid_in hid_hi hid_lo z_full z_done z_hi z_split y_full "
                              "y_scaled y_done stored")
        w_ins = (w_in0, w_in1)
        weight = lambda k, m: [x[:, k, m * P:(m + 1) * P] for x in (wH, wL)]
        w3 = lambda k: [x[:, HT + k // 4, (k % 4) * D:(k % 4 + 1) * D] for x in (wH, wL)]
        out_rows = c.out.rearrange("(b n p) d -> p (b n) d", p=P, n=TT)
        block = ctx.enter_context(nc.Block())

        @block.sync
        def _(sp):
            sp.dma_start(scales[:, :], c.ins["h2_s"]).then_inc(scales_in, DMA)
            for n in range(2):
                sp.dma_start(out_scale[:, n, :], c.ins["w3_s"].partition_broadcast(P)).then_inc(scales_in, DMA)
            for n in range(CHUNKS):
                if n >= 2:
                    sp.wait_ge(w_lo, n - 1)
                sp.dma_start(raw[:, n % 2, :], c.ins["ffn_w"][2 * KT + HT + n]).then_inc(w_ins[n % 2], DMA)
            with sp.Fori(0, B) as b:
                sp.wait_ge(hid_lo, b * HT + HT)
                sp.dma_start(hidden[:, :, :], c.hidden_dram[bass.ds(b, 1), :, :, :].rearrange("o p m t -> p (o m) t")).then_inc(hid_in, DMA)
            with sp.Fori(0, B) as b:
                sp.wait_ge(y_done, 2 * b + 2 + 2)
                sp.dma_start(out_rows[:, bass.ds(b * TT, TT), :], c.X[:, bass.ds(b * TT, TT), :]).then_inc(stored, DMA)
            sp.wait_ge(stored, B * DMA)

        @block.gpsimd
        def _(pool):
            pass

        @block.scalar
        def _(act):
            for n in range(CHUNKS):
                act.wait_ge(w_ins[n % 2], (n // 2 + 1) * DMA)
                nc.scalar.activation(wH[:, n, :], raw[:, n % 2, :], ACT.Copy).then_inc(w_hi, 1)
            act.wait_ge(scales_in, 3 * DMA)
            with act.Fori(0, B) as b:
                act.wait_ge(hid_in, b * DMA + DMA)
                act.wait_ge(z_full, b * HT + 2)
                for k in range(HT):
                    nc.scalar.activation(hH[:, k, :], hidden[:, k, :], ACT.Copy).then_inc(hid_hi, 1)
                for m in range(HT):
                    act.wait_ge(z_full, b * HT + m + 1 + 2)
                    act.wait_ge(z_split, b * HT + m + 1)
                    nc.scalar.activation(z_raw[:, m % 2, :], c.pa[:, m % 2, :], ACT.Gelu, scale=scales[:, m:m + 1]).then_inc(z_done, 1)

        @block.vector
        def _(dve):
            dve.sem_inc(hid_lo, HT)
            dve.sem_inc(z_split, 2)
            dve.sem_inc(y_done, 2)
            for n in range(CHUNKS):
                dve.wait_ge(w_hi, n + 1)
                nc.vector.tensor_tensor(wL[:, n, :], raw[:, n % 2, :], wH[:, n, :].bitcast(F32), ALU.subtract).then_inc(w_lo, 1)
            dve.wait_ge(scales_in, 3 * DMA)
            with dve.Fori(0, B) as b:
                for k in range(HT):
                    dve.wait_ge(hid_hi, b * HT + k + 1)
                    nc.vector.tensor_tensor(hL[:, k, :], hidden[:, k, :], hH[:, k, :].bitcast(F32), ALU.subtract).then_inc(hid_lo, 1)
                for m in range(HT):
                    dve.wait_ge(z_done, b * HT + m + 1 + 2)
                    nc.vector.tensor_copy(zH[:, m, :], z_raw[:, m % 2, :]).then_inc(z_hi, 1)
                    dve.wait_ge(z_hi, b * HT + m + 1)
                    nc.vector.tensor_tensor(zL[:, m, :], z_raw[:, m % 2, :], zH[:, m, :].bitcast(F32), ALU.subtract).then_inc(z_split, 1)
                for n in range(2):
                    dve.wait_ge(y_full, 2 * b + n + 1)
                    nc.vector.tensor_tensor(y[:, n, :, :], c.pd[:, n, :].rearrange("p (t d) -> p t d", d=D), out_scale[:, :, :],
                                            ALU.mult).then_inc(y_scaled, 1)
                    dve.wait_ge(y_scaled, 2 * b + n + 1)
                    xb = c.X[:, bass.ds(b * TT + 2 * n, 2), :]
                    nc.vector.tensor_tensor(xb, y[:, n, :, :], xb, ALU.add).then_inc(y_done, 1)

        @block.tensor
        def _(pe):
            pe.sem_inc(z_full, 2)
            pe.sem_inc(z_done, 2)
            pe.wait_ge(w_lo, CHUNKS)
            with pe.Fori(0, B) as b:
                for m in range(HT):
                    pe.wait_ge(z_done, b * HT + m + 1)
                    for k in range(HT):
                        if m == 0:
                            pe.wait_ge(hid_lo, b * HT + k + 1 + HT)
                        last = hi_lo(pe, nc, c.pa[:, m % 2, :], weight(k, m), [x[:, k, :] for x in (hH, hL)], k == 0, k == HT - 1)
                    last.then_inc(z_full, 1)
                pe.wait_ge(z_split, b * HT + HT + 2)
                for n in range(2):
                    pe.wait_ge(y_done, 2 * b + n + 1)
                    for t in (2 * n, 2 * n + 1):
                        for k in range(HT):
                            last = hi_lo(pe, nc, c.pd[:, n, (t % 2) * D:(t % 2 + 1) * D], [x[:, k, t * P:(t + 1) * P] for x in (zH, zL)],
                                         w3(k), k == 0, k == HT - 1)
                    last.then_inc(y_full, 1)


def build_program(nc, ins, out):
    c = Core()
    c.ins, c.out = ins, out
    c.q_dram = nc.dram_tensor("q_dram", (B, 2, D, S), F32).ap()
    c.k_dram = nc.dram_tensor("k_dram", (B, 2, D, S), F32).ap()
    c.v_dram = nc.dram_tensor("v_dram", (B, P, TT * H1 * 2 * DH1), F32).ap()
    c.hidden_dram = nc.dram_tensor("hidden_dram", (B, P, HT, S), F32).ap()
    with ExitStack() as ctx:
        sb = lambda n, s, d=F32: ctx.enter_context(nc.sbuf_tensor(n, s, d))
        c.X = sb("X", [P, NT, D])
        c.ident = sb("ident", [P, P])
        c.bo = sb("bo", [P, D])
        c.pa = ctx.enter_context(nc.psum_tensor("pa", [P, 4, S], F32))
        c.pd = ctx.enter_context(nc.psum_tensor("pd", [P, 4, S], F32))
        c.ln_sems = semaphores(nc, ctx, "ln", "loaded const stat_done step var_done pow_done rstd_done xn_done tr_done hi_done lo_done")
        c.waited = ctx.enter_context(nc.semaphore("waited"))
        def normed(stack, part):
            c.xnH = stack.enter_context(nc.sbuf_tensor(f"xnH_{part}", [P, KT, T], F32R))
            c.xnL = stack.enter_context(nc.sbuf_tensor(f"xnL_{part}", [P, KT, T], F32R))

        with ExitStack() as stack:
            normed(stack, "a")
            layernorm_phase(nc, c, 0)
            first_attention_phase(nc, c)
            layernorm_phase(nc, c, 1)
            mixture_phase(nc, c)
            layernorm_phase(nc, c, 2)
            second_projection_phase(nc, c)
        second_attention_phase(nc, c)
        with ExitStack() as stack:
            normed(stack, "b")
            layernorm_phase(nc, c, 3)
            first_ffn_phase(nc, c)
        second_ffn_phase(nc, c)


def kernel(**inputs):
    import concourse.bacc as bacc
    from concourse.bass_utils import run_bass_kernel_spmd

    inp = {n: np.asarray(a) for n, a in inputs.items()}
    of = lambda part: {n[len(part):]: a for n, a in inp.items() if n.startswith(part)}
    a0, moe, a1, ffn = of("L0_xattn_"), of("L0_ffn_"), of("L1_xattn_"), of("L1_ffn_")

    def by_contraction(w):
        return w.reshape(-1, P, w.shape[1]).transpose(1, 0, 2).reshape(P, -1)

    def columns(v, *lead):
        return np.moveaxis(v.reshape(*lead, -1, P), -1, 0)

    mask = inp["mask_1x1xSxS2_bk1"].reshape(S, S)
    wo1 = np.zeros((GROUPS, GH, 2, DH1, D), np.float32)
    wo1[:, :, 0] = a1["Wo"].T.reshape(GROUPS, GH, DH1, D)
    expert = lambda e: np.concatenate([by_contraction(moe["fc1_w"][e].T), by_contraction(moe["fc2_w"][e].T)], 1)
    feature_tiles = lambda w: w.T.reshape(-1, P, HID)
    layout = {
        "x": inp["x"].reshape(T, D),
        "ctx": inp["ctx_1024"].reshape(T, KT, P).transpose(2, 1, 0),
        "bo": a0["bo"],
        "wq0": by_contraction(a0["Wq"]), "wk0": by_contraction(a0["Wk"]),
        "wv0": by_contraction(a0["Wv"]), "wo0": by_contraction(a0["Wo"]),
        "gate": by_contraction(np.concatenate([moe["gate_w"].T, np.zeros((D, 1), np.float32)], 1)),
        "b1": columns(moe["fc1_b"], E), "mult": columns(moe["geglu_mult"], E),
        "sb1": columns(moe["s_fc1_b"]), "smult": columns(moe["s_geglu_mult"]),
        "b2": np.concatenate([moe["fc2_b"], moe["s_fc2_b"][None]], 0),
        "sw": np.concatenate([by_contraction(moe["s_fc1_w"].T), by_contraction(moe["s_fc2_w"].T)], 1),
        "ew": np.stack([expert(e) for e in range(E)]),
        "wq1": by_contraction(a1["Wq"].T), "wk1": by_contraction(a1["Wk"].T), "wv1": by_contraction(a1["Wv"].T),
        "wo1": by_contraction(wo1.reshape(-1, D)),
        "mask": mask, "maskT": mask.T,
        "ffn_w": np.concatenate([feature_tiles(ffn["w1_w"]), feature_tiles(ffn["w2_w"]), feature_tiles(ffn["h1_w"]),
                                 feature_tiles(ffn["h2_w"]),
                                 ffn["w3_w"].T.reshape(2, 4, P, D).transpose(0, 2, 1, 3).reshape(2, P, HID)], 0),
        "ffn_scales": np.stack([columns(ffn[n]) for n in ("w1_s", "w2_s", "h1_s")], 1),
        "h2_s": columns(ffn["h2_s"]), "w3_s": ffn["w3_s"],
    }
    arrays = {f"in_{n}": np.ascontiguousarray(a) for n, a in layout.items()}
    nc = bacc.Bacc("TRN2", target_bir_lowering=False, num_devices=1)
    ins = {n[3:]: nc.dram_tensor(n, a.shape, mybir.dt.from_np(a.dtype), kind="ExternalInput").ap() for n, a in arrays.items()}
    out = nc.dram_tensor("out", (T, D), F32, kind="ExternalOutput").ap()
    build_program(nc, ins, out)
    return run_bass_kernel_spmd(nc, [arrays], core_ids=[0]).results[0]["out"].reshape(B, S, D)
```

```python
from contextlib import ExitStack

import numpy as np

import concourse.bass as bass
from concourse import mybir
from concourse.alu_op_type import AluOpType as ALU

F32 = mybir.dt.float32
F32R = mybir.dt.float32r
BF16 = mybir.dt.bfloat16
U8 = mybir.dt.uint8
I32 = mybir.dt.int32
U32 = mybir.dt.uint32
ACT = mybir.ActivationFunctionType
AX = mybir.AxisListType

P = 128
B, S, D = 4, 512, 256
KT = D // P
TT = S // P
T = B * S
NT = T // P
LN_EPS = 1e-5

H0, DH0 = 8, 64
INNER = H0 * DH0
PAIRS = H0 // 2
H1, DH1 = 16, 16
GROUPS, GH = 4, 4
E, TOPK, F, FS = 15, 3, 256, 512
FT, FST = F // P, FS // P
BLOCKS = (TOPK * T + E * (P - 1)) // P
RING = 4
BLOCKS += -BLOCKS % RING
HID = 1024
HT = HID // P
MASKED = -1.0e30
LEAST_MAX = -1.0e29
DMA = 16


def hi_lo(pe, nc, out, stat, move, first, last):
    (sh, sl), (mh, ml) = stat, move
    nc.tensor.matmul(out, sh, ml, start=first, stop=False)
    nc.tensor.matmul(out, sl, mh, start=False, stop=False)
    return nc.tensor.matmul(out, sh, mh, start=False, stop=last)


class Core:
    pass


def apart(engine, c):
    engine.sem_inc(c.waited, 1)


def semaphores(nc, ctx, phase, names, reuse=False):
    if not reuse:
        return [ctx.enter_context(nc.semaphore(f"{phase}_{n}")) for n in names.split()]
    handles = [nc.alloc_semaphore(name=f"{phase}_{n}") for n in names.split()]

    def free():
        nc.clear_and_free_semaphores(handles)
        nc.all_engine_barrier()

    ctx.callback(free)
    return handles


def layernorm_phase(nc, c, turn, prefetch=None, rows=None):
    setup = turn == 0
    with ExitStack() as ctx:
        sb = lambda n, s, d=F32: ctx.enter_context(nc.sbuf_tensor(f"ln{turn}_{n}", s, d))
        stats = sb("stats", [P, TT, 6])
        mean = sb("mean", [P, TT])
        diff = sb("diff", [P, TT])
        m2 = sb("m2", [P, TT])
        ve = sb("ve", [P, TT])
        y = sb("y", [P, TT])
        t1 = sb("t1", [P, TT])
        half = sb("half", [P, TT])
        rstd = sb("rstd", [P, TT])
        xn = sb("xn", [P, TT, D])
        (loaded, const, stat_done, step, var_done, pow_done, rstd_done, xn_done, tr_done, hi_done, lo_done) = c.ln_sems
        CONST = 3 + turn
        block = ctx.enter_context(nc.Block())

        @block.sync
        def _(sp):
            if setup:
                sp.dma_start(c.X[:, :, :], c.ins["x"].rearrange("(n p) d -> p n d", p=P)).then_inc(loaded, DMA)
                sp.dma_start(c.bo[:, :], c.ins["bo"].partition_broadcast(P)).then_inc(loaded, DMA)
            if prefetch:
                prefetch(sp)
            if rows:
                with sp.Fori(0, B) as b:
                    sp.wait_ge(xn_done, b + turn * B + 1)
                    sp.dma_start(rows[0].rearrange("(n p) d -> p n d", p=P)[:, bass.ds(b * TT, TT), :], xn[:, :, :]).then_inc(rows[1], DMA)
                sp.wait_ge(rows[1], (B + 1) * DMA)

        @block.gpsimd
        def _(pool):
            if setup:
                nc.gpsimd.memset(c.ident[:, :], 0.0).then_inc(const, 1)
                pool.wait_ge(const, 1)
                nc.gpsimd.affine_select(out=c.ident[:, :], in_=c.ident[:, :], compare_op=ALU.not_equal, fill=1.0,
                                        base=0, pattern=[[-1, P]], channel_multiplier=1).then_inc(const, 1)
            nc.gpsimd.memset(half[:, :], -0.5).then_inc(const, 1)
            pool.wait_ge(const, CONST)
            pool.wait_ge(loaded, 2 * DMA)
            with pool.Fori(0, B) as b:
                n = b + turn * B
                pool.wait_ge(var_done, n + 1)
                nc.gpsimd.tensor_tensor(y[:, :], ve[:, :], half[:, :], ALU.pow).then_inc(pow_done, 1)
                if setup:
                    pool.wait_ge(xn_done, n + 1)
                    xb = c.X[:, bass.ds(b * TT, TT), :]
                    nc.gpsimd.tensor_tensor(xb, xb, c.bo[:, :].unsqueeze(1).to_broadcast([P, TT, D]), ALU.add)

        @block.vector
        def _(dve):
            if setup:
                dve.wait_ge(loaded, 2 * DMA)
            if rows:
                dve.sem_inc(rows[1], DMA)
            with dve.Fori(0, B) as b:
                n = b + turn * B
                if rows:
                    dve.wait_ge(rows[1], b * DMA + DMA)
                for t in range(TT):
                    last = nc.vector.bn_stats(stats[:, t, :], c.X[:, bass.ds(b * TT + t, 1), :].rearrange("p o d -> p (o d)"))
                last.then_inc(stat_done, 1)
                dve.wait_ge(stat_done, n + 1)
                nc.vector.tensor_tensor(mean[:, :], stats[:, :, 1], stats[:, :, 4], ALU.add)
                nc.vector.tensor_tensor(diff[:, :], stats[:, :, 1], stats[:, :, 4], ALU.subtract)
                nc.vector.tensor_tensor(m2[:, :], stats[:, :, 2], stats[:, :, 5], ALU.add).then_inc(step, 1)
                dve.wait_ge(step, 5 * n + 1)
                nc.vector.tensor_scalar(mean[:, :], mean[:, :], 0.5, None, ALU.mult)
                nc.vector.tensor_tensor(diff[:, :], diff[:, :], diff[:, :], ALU.mult).then_inc(step, 1)
                dve.wait_ge(step, 5 * n + 2)
                nc.vector.scalar_tensor_tensor(m2[:, :], diff[:, :], D / 4.0, m2[:, :], ALU.mult, ALU.add).then_inc(step, 1)
                dve.wait_ge(step, 5 * n + 3)
                nc.vector.tensor_scalar(ve[:, :], m2[:, :], 1.0 / D, LN_EPS, ALU.mult, ALU.add).then_inc(var_done, 1)
                dve.wait_ge(pow_done, n + 1)
                nc.vector.scalar_tensor_tensor(t1[:, :], ve[:, :], -0.5, y[:, :], ALU.mult, ALU.mult).then_inc(step, 1)
                dve.wait_ge(step, 5 * n + 4)
                nc.vector.tensor_tensor(t1[:, :], t1[:, :], y[:, :], ALU.mult).then_inc(step, 1)
                dve.wait_ge(step, 5 * n + 5)
                nc.vector.scalar_tensor_tensor(rstd[:, :], t1[:, :], 1.5, y[:, :], ALU.add, ALU.mult).then_inc(rstd_done, 1)
                dve.wait_ge(rstd_done, n + 1)
                for t in range(TT):
                    last = nc.vector.tensor_scalar(xn[:, t, :], c.X[:, bass.ds(b * TT + t, 1), :].rearrange("p o d -> p (o d)"),
                                                   mean[:, t:t + 1], rstd[:, t:t + 1], ALU.subtract, ALU.mult)
                last.then_inc(xn_done, 1)
                for k in range(KT):
                    dve.wait_ge(hi_done, KT * n + k + 1)
                    tok = bass.ds(b * S, S)
                    nc.vector.tensor_tensor(c.xnL[:, k, tok], c.pd[:, k, :], c.xnH[:, k, tok].bitcast(F32),
                                            ALU.subtract).then_inc(lo_done, 1)

        @block.tensor
        def _(pe):
            pe.wait_ge(const, CONST)
            with pe.Fori(0, B) as b:
                n = b + turn * B
                pe.wait_ge(xn_done, n + 1)
                for k in range(KT):
                    for t in range(TT):
                        last = nc.tensor.transpose(c.pd[:, k, t * P:(t + 1) * P], xn[:, t, k * P:(k + 1) * P], c.ident[:, :])
                    last.then_inc(tr_done, 1)

        @block.scalar
        def _(act):
            with act.Fori(0, B) as b:
                n = b + turn * B
                for k in range(KT):
                    act.wait_ge(tr_done, KT * n + k + 1)
                    apart(act, c)
                    nc.scalar.activation(c.xnH[:, k, bass.ds(b * S, S)], c.pd[:, k, :], ACT.Copy).then_inc(hi_done, 1)


def first_attention_phase(nc, c):
    WORK = TT + PAIRS * (2 + 2 * TT) + 2
    with ExitStack() as ctx:
        sb = lambda n, s, d=F32: ctx.enter_context(nc.sbuf_tensor(f"a_{n}", s, d))
        raw = sb("raw", [P, 2, KT * INNER])
        wH = sb("wH", [P, 4, KT * INNER], F32R)
        wL = sb("wL", [P, 4, KT * INNER], F32R)
        ctx_raw = sb("ctx_raw", [P, KT, S])
        ctxH = sb("ctxH", [P, KT, S], F32R)
        ctxL = sb("ctxL", [P, KT, S], F32R)
        V = sb("V", [P, TT, INNER])
        qHL = sb("qHL", [P, 2, 2, S], F32R)
        kHH = sb("kHH", [P, 2, 2, S], F32R)
        kL1 = sb("kL1", [P, 2, 2, S], F32R)
        qHM = sb("qHM", [P, 2, 2, S], F32R)
        mx = sb("mx", [P, 2, 2, TT])
        prob = sb("prob", [P, 2, 2, TT, S])
        half_sum = sb("half_sum", [P, 2, S])
        prob_sum = sb("prob_sum", [P, 2, 2, S])
        ones = sb("ones", [P, DH0])
        inv = sb("inv", [P, S])
        o = sb("o", [P, S])
        oH = sb("oH", [P, PAIRS, S], F32R)
        oL = sb("oL", [P, PAIRS, S], F32R)
        (w_in0, w_in1, w_hi, w_lo, const, ctx_in, ctx_hi, ctx_lo, work_full, work_read, q_hi, k_hi, dup_done, row_full,
         row_done, st_full, exp_done, add_half, add_done, pv_done, norm_step, o_read, o_split, x_done) = semaphores(
            nc, ctx, "a", "w_in0 w_in1 w_hi w_lo const ctx_in ctx_hi ctx_lo work_full work_read q_hi k_hi dup_done row_full "
            "row_done st_full exp_done add_half add_done pv_done norm_step o_read o_split x_done", reuse=True)
        wq, wk, wv, wo = range(4)
        weight = lambda w, k, lo, n: [x[:, w, k * INNER + lo:k * INNER + lo + n] for x in (wH, wL)]
        wo_tile = lambda k: [x[:, wo, k * D:(k + 1) * D] for x in (wH, wL)]
        own = lambda h: slice(h * DH0, (h + 1) * DH0)
        other = lambda h: slice((1 - h) * DH0, (2 - h) * DH0)
        aux = lambda h: slice((1 - h) * DH0, (1 - h) * DH0 + 1)
        use_v = lambda t: t
        use_proj = lambda j, n: TT + n if j == 0 else TT + 2 + (j - 1) * (2 + 2 * TT) + n
        use_s = lambda j, h, t: TT + 2 + j * (2 + 2 * TT) + (2 if j < PAIRS - 1 else 0) + h * TT + t
        use_o = lambda n: WORK - 2 + n
        block = ctx.enter_context(nc.Block())

        @block.sync
        def _(sp):
            for n, name in enumerate(("wq0", "wk0", "wv0", "wo0")):
                if n >= 2:
                    sp.wait_ge(w_lo, n - 1)
                sp.dma_start(raw[:, n % 2, :], c.ins[name]).then_inc(w_in0 if n % 2 == 0 else w_in1, DMA)
            with sp.Fori(0, B) as b:
                sp.wait_ge(ctx_lo, b + 1)
                sp.dma_start(ctx_raw[:, :, :], c.ins["ctx"][:, :, bass.ds(b * S, S)]).then_inc(ctx_in, DMA)

        @block.gpsimd
        def _(pool):
            pool.sem_inc(add_done, 1)
            nc.gpsimd.memset(ones[:, :], 1.0).then_inc(const, 1)
            nc.gpsimd.memset(kL1[:, :, :, :].bitcast(F32), 0.0).then_inc(const, 1)
            nc.gpsimd.memset(qHM[:, :, :, :].bitcast(F32), 0.0).then_inc(const, 1)
            pool.wait_ge(const, 3)
            for h in range(2):
                nc.gpsimd.memset(kL1[aux(h), :, h, :].bitcast(F32), 1.0).then_inc(const, 1)

            with pool.Fori(0, B) as b:
                for j in range(PAIRS):
                    for h in range(2):
                        pool.wait_ge(exp_done, (b * PAIRS + j) * 4 + 3 + h)
                        pool.wait_ge(add_done, (b * PAIRS + j) * 2 + h + 1)
                        nc.gpsimd.tensor_tensor(half_sum[:, :, :], prob[:, j % 2, h, 0:2, :], prob[:, j % 2, h, 2:4, :],
                                                ALU.add).then_inc(add_half, 1)
                        pool.wait_ge(add_half, (b * PAIRS + j) * 2 + h + 1)
                        nc.gpsimd.tensor_tensor(prob_sum[:, j % 2, h, :], half_sum[:, 0, :], half_sum[:, 1, :],
                                                ALU.add).then_inc(add_done, 1)

        @block.scalar
        def _(act):
            for n in range(4):
                act.wait_ge(w_in0 if n % 2 == 0 else w_in1, DMA * (n // 2 + 1))
                nc.scalar.activation(wH[:, n, :], raw[:, n % 2, :], ACT.Copy).then_inc(w_hi, 1)

            def round_hi(b, j):
                act.wait_ge(work_full, b * WORK + use_proj(j, 0) + 1)
                for h in range(2):
                    last = nc.scalar.activation(qHL[own(h), j % 2, h, :], c.pd[own(h), use_proj(j, 0) % 2, :], ACT.Copy)
                last.then_inc(q_hi, 1)
                act.wait_ge(work_full, b * WORK + use_proj(j, 1) + 1)
                for h in range(2):
                    nc.scalar.activation(kHH[own(h), j % 2, h, :], c.pd[own(h), use_proj(j, 1) % 2, :], ACT.Copy)
                    last = nc.scalar.activation(kHH[other(h), j % 2, h, :], c.pd[own(h), use_proj(j, 1) % 2, :], ACT.Copy)
                last.then_inc(k_hi, 1)

            with act.Fori(0, B) as b:
                act.wait_ge(ctx_in, DMA * b + DMA)
                nc.scalar.activation(ctxH[:, :, :], ctx_raw[:, :, :], ACT.Copy).then_inc(ctx_hi, 1)
                round_hi(b, 0)
                for j in range(PAIRS):
                    if j + 1 < PAIRS:
                        round_hi(b, j + 1)
                    for h in range(2):
                        act.wait_ge(row_full, (b * PAIRS + j) * 2 + h + 1)
                        act.wait_ge(dup_done, b * PAIRS + j + 1)
                        nc.scalar.activation(qHM[aux(h), j % 2, h, :], c.pa[0:1, 2 * h, :], ACT.Copy,
                                             scale=-1.0).then_inc(row_done, 1)
                    for n in range(4):
                        h, k2 = n % 2, 2 * (n // 2)
                        act.wait_ge(st_full, (b * PAIRS + j) * 4 + n + 1)
                        act.wait_ge(pv_done, b * PAIRS + j + 1)
                        nc.scalar.activation(prob[:, j % 2, h, k2:k2 + 2, :], c.pa[:, 2 * h:2 * h + 2, :], ACT.Exp,
                                             scale=DH0 ** -0.5).then_inc(exp_done, 1)

        @block.vector
        def _(dve):
            dve.sem_inc(work_read, 2)
            dve.sem_inc(ctx_lo, 1)
            dve.sem_inc(o_read, 1)
            for n in range(4):
                dve.wait_ge(w_hi, n + 1)
                nc.vector.tensor_tensor(wL[:, n, :], raw[:, n % 2, :], wH[:, n, :].bitcast(F32), ALU.subtract).then_inc(w_lo, 1)

            def keep_lo(b, j):
                dve.wait_ge(q_hi, b * PAIRS + j + 1)
                for h in range(2):
                    last = nc.vector.tensor_tensor(qHL[other(h), j % 2, h, :], c.pd[own(h), use_proj(j, 0) % 2, :],
                                                   qHL[own(h), j % 2, h, :].bitcast(F32), ALU.subtract)
                last.then_inc(work_read, 1)
                for h in range(2):
                    last = nc.vector.tensor_copy(qHM[own(h), j % 2, h, :], qHL[own(h), j % 2, h, :].bitcast(F32))
                last.then_inc(dup_done, 1)
                dve.wait_ge(k_hi, b * PAIRS + j + 1)
                for h in range(2):
                    last = nc.vector.tensor_tensor(kL1[own(h), j % 2, h, :], c.pd[own(h), use_proj(j, 1) % 2, :],
                                                   kHH[own(h), j % 2, h, :].bitcast(F32), ALU.subtract)
                last.then_inc(work_read, 1)

            def normalise(b, j):
                dve.wait_ge(pv_done, b * PAIRS + j + 3)
                step = (b * PAIRS + j) * 2
                nc.vector.reciprocal(inv[:, :], c.pd[:, 3, :]).then_inc(norm_step, 1)
                dve.wait_ge(norm_step, step + 1)
                nc.vector.tensor_tensor(o[:, :], c.pd[:, 2, :], inv[:, :], ALU.mult).then_inc(o_read, 1)
                dve.wait_ge(o_read, b * PAIRS + j + 2)
                nc.vector.tensor_copy(oH[:, j, :], o[:, :]).then_inc(norm_step, 1)
                dve.wait_ge(norm_step, step + 2)
                nc.vector.tensor_tensor(oL[:, j, :], o[:, :], oH[:, j, :].bitcast(F32), ALU.subtract).then_inc(o_split, 1)

            with dve.Fori(0, B) as b:
                dve.wait_ge(ctx_hi, b + 1)
                nc.vector.tensor_tensor(ctxL[:, :, :], ctx_raw[:, :, :], ctxH[:, :, :].bitcast(F32),
                                        ALU.subtract).then_inc(ctx_lo, 1)
                for t in range(TT):
                    dve.wait_ge(work_full, b * WORK + use_v(t) + 1)
                    nc.vector.tensor_copy(V[:, t, :], c.pd[:, use_v(t) % 2, :]).then_inc(work_read, 1)
                keep_lo(b, 0)
                for j in range(PAIRS):
                    if j + 1 < PAIRS:
                        keep_lo(b, j + 1)
                    for h in range(2):
                        for t in range(TT):
                            u = use_s(j, h, t)
                            dve.wait_ge(work_full, b * WORK + u + 1)
                            nc.vector.reduce_max(mx[:, j % 2, h, t:t + 1], c.pd[:, u % 2, :], AX.X).then_inc(work_read, 1)
                    if j:
                        normalise(b, j - 1)
                normalise(b, PAIRS - 1)
                for n in range(2):
                    dve.wait_ge(work_full, b * WORK + use_o(n) + 1)
                    xb = c.X[:, bass.ds(b * TT + 2 * n, 2), :].rearrange("p n d -> p (n d)")
                    nc.vector.tensor_tensor(xb, c.pd[:, use_o(n) % 2, :], xb, ALU.add).then_inc(work_read, 1)

        @block.tensor
        def _(pe):
            pe.sem_inc(pv_done, 2)
            pe.wait_ge(w_lo, 4)
            pe.wait_ge(const, 5)

            def free_bank(b, u):
                pe.wait_ge(work_read, b * WORK + u + 1)
                return c.pd[:, u % 2, :]

            def project(b, j):
                out = free_bank(b, use_proj(j, 0))
                for k in range(KT):
                    last = hi_lo(pe, nc, out, weight(wq, k, j * P, P), [x[:, k, bass.ds(b * S, S)] for x in (c.xnH, c.xnL)],
                                 k == 0, k == KT - 1)
                last.then_inc(work_full, 1)
                out = free_bank(b, use_proj(j, 1))
                for k in range(KT):
                    last = hi_lo(pe, nc, out, weight(wk, k, j * P, P), [x[:, k, :] for x in (ctxH, ctxL)],
                                 k == 0, k == KT - 1)
                last.then_inc(work_full, 1)

            def weigh_values(b, j, k):
                if k == 0:
                    pe.wait_ge(o_read, b * PAIRS + j + 1)
                pe.wait_ge(exp_done, (b * PAIRS + j) * 4 + (2 if k < 2 else 4))
                for h in range(2):
                    head = 2 * j + h
                    nc.tensor.matmul(c.pd[own(h), 2, :], V[:, k, head * DH0:(head + 1) * DH0], prob[:, j % 2, h, k, :],
                                     start=k == 0, stop=k == TT - 1)

            def denominators(b, j):
                pe.wait_ge(add_done, (b * PAIRS + j) * 2 + 3)
                for h in range(2):
                    last = nc.tensor.matmul(c.pd[own(h), 3, :], ones[:, :], prob_sum[:, j % 2, h, :], start=True, stop=True)
                last.then_inc(pv_done, 1)

            with pe.Fori(0, B) as b:
                pe.wait_ge(ctx_lo, b + 2)
                for t in range(TT):
                    out = free_bank(b, use_v(t))
                    for k in range(KT):
                        last = hi_lo(pe, nc, out, [x[:, k, t * P:(t + 1) * P] for x in (ctxH, ctxL)],
                                     weight(wv, k, 0, INNER), k == 0, k == KT - 1)
                    last.then_inc(work_full, 1)
                project(b, 0)
                for j in range(PAIRS):
                    if j + 1 < PAIRS:
                        project(b, j + 1)
                    pe.wait_ge(dup_done, b * PAIRS + j + 1)
                    pe.wait_ge(work_read, b * WORK + use_proj(j, 1) + 3)
                    for h in range(2):
                        for t in range(TT):
                            out = free_bank(b, use_s(j, h, t))
                            nc.tensor.matmul(out, qHL[:, j % 2, h, t * P:(t + 1) * P], kHH[:, j % 2, h, :],
                                             start=True, stop=True).then_inc(work_full, 1)
                            if j and h * TT + t >= 2 and t % 2 == 1:
                                weigh_values(b, j - 1, (h * TT + t) // 2 - 1)
                    if j:
                        weigh_values(b, j - 1, TT - 1)
                        denominators(b, j - 1)
                    for h in range(2):
                        pe.wait_ge(work_read, b * WORK + use_s(j, h, TT - 1) + 3)
                        pe.wait_ge(exp_done, (b * PAIRS + j) * 4) if j else None
                        for t in range(TT):
                            last = nc.tensor.transpose(c.pa[0:1, 2 * h, t * P:(t + 1) * P], mx[:, j % 2, h, t:t + 1], c.ident[:, :])
                        last.then_inc(row_full, 1)
                    for n in range(4):
                        h = n % 2
                        if n < 2:
                            pe.wait_ge(row_done, (b * PAIRS + j) * 2 + h + 1)
                        else:
                            pe.wait_ge(exp_done, (b * PAIRS + j) * 4 + n - 1)
                        for k in range(2 * (n // 2), 2 * (n // 2) + 2):
                            out = c.pa[:, 2 * h + k % 2, :]
                            nc.tensor.matmul(out, kHH[:, j % 2, h, k * P:(k + 1) * P], qHL[:, j % 2, h, :], start=True, stop=False)
                            last = nc.tensor.matmul(out, kL1[:, j % 2, h, k * P:(k + 1) * P], qHM[:, j % 2, h, :],
                                                    start=False, stop=True)
                        last.then_inc(st_full, 1)
                for k in range(TT):
                    weigh_values(b, PAIRS - 1, k)
                denominators(b, PAIRS - 1)
                pe.wait_ge(o_split, b * PAIRS + PAIRS)
                for n in range(2):
                    bank = free_bank(b, use_o(n))
                    for t in (2 * n, 2 * n + 1):
                        out = bank[:, (t % 2) * D:(t % 2 + 1) * D]
                        for k in range(PAIRS):
                            last = hi_lo(pe, nc, out, [x[:, k, t * P:(t + 1) * P] for x in (oH, oL)], wo_tile(k),
                                         k == 0, k == PAIRS - 1)
                    last.then_inc(work_full, 1)


def mixture_phase(nc, c):
    EP = E + 1
    W1, W2 = KT * 2 * F, FT * D
    with ExitStack() as ctx:
        weights = ctx.enter_context(nc.sbuf_tensor("m_weights", [P, E, W1 + W2], F32))
        (w_loaded, rows_stored) = semaphores(nc, ctx, "m", "w_loaded rows_stored")

        def load_experts(sp):
            for e in range(E):
                sp.dma_start(weights[:, e, :], c.ins["ew"][e]).then_inc(w_loaded, DMA)

        sb = lambda n, s, d=F32: ctx.enter_context(nc.sbuf_tensor(f"m_{n}", s, d))
        SW = KT * 2 * FS + FST * D
        gate_raw = sb("gate_raw", [P, KT * EP])
        gateH = sb("gateH", [P, KT * EP], F32R)
        gateL = sb("gateL", [P, KT * EP], F32R)
        mult = sb("mult", [P, E, FT])
        sb1 = sb("sb1", [P, 2 * FST])
        smult = sb("smult", [P, FST])
        b2 = sb("b2", [EP, D])
        before = sb("before", [P, E, E])
        rank = sb("rank", [P, NT, E])
        comb = sb("comb", [P, NT, EP])
        combT = sb("combT", [EP, S])
        (w_in, gate_hi, gate_lo, const) = semaphores(nc, ctx, "m", "w_in gate_hi gate_lo const")

        with ExitStack() as inner:
            c.xnH = inner.enter_context(nc.sbuf_tensor("m_xnH", [P, KT, T], F32R))
            c.xnL = inner.enter_context(nc.sbuf_tensor("m_xnL", [P, KT, T], F32R))
            layernorm_phase(nc, c, 1, prefetch=load_experts, rows=(c.rows_dram, rows_stored))
            sb = lambda n, s, d=F32: inner.enter_context(nc.sbuf_tensor(f"ms_{n}", s, d))
            wH = sb("wH", [P, SW], F32R)
            wL = sb("wL", [P, SW], F32R)
            logT = sb("logT", [EP, S])
            lg = sb("lg", [P, TT, EP])
            peak = sb("peak", [P, TT])
            ex = sb("ex", [P, TT, EP])
            tot = sb("tot", [P, TT])
            score = sb("score", [P, TT, E])
            gt = sb("gt", [P, TT, E * E], BF16)
            eq = sb("eq", [P, TT, E * E], BF16)
            best = sb("best", [P, TT, E])
            gl = sb("gl", [P, 2, S])
            up = sb("up", [P, 2, S])
            aH = sb("aH", [P, FST, S], F32R)
            aL = sb("aL", [P, FST, S], F32R)
            (sw_in0, sw_in1, sw_hi, sw_lo, log_full, log_copied, logtok_full, shifted, exp_done, step, comb_done, combT_full,
             combT_done, g_full, g_done, x_full, x_read, araw_done, hi_done, a_split, y_full, y_read) = semaphores(
                nc, inner, "ms", "sw_in0 sw_in1 sw_hi sw_lo log_full log_copied logtok_full shifted exp_done step comb_done "
                "combT_full combT_done g_full g_done x_full x_read araw_done hi_done a_split y_full y_read")
            up_w = lambda m, k: [x[:, k * 2 * FS + m * P:k * 2 * FS + (m + 1) * P] for x in (wH, wL)]
            down_w = lambda k: [x[:, KT * 2 * FS + k * D:KT * 2 * FS + (k + 1) * D] for x in (wH, wL)]
            STEPS = 13
            CHUNK = 2 * S
            staged = lambda n: (gl, up)[n % 2][:, :, :].rearrange("p n s -> p (n s)")
            sw_ins = (sw_in0, sw_in1)
            block = inner.enter_context(nc.Block())

            @block.sync
            def _(sp):
                sp.dma_start(gate_raw[:, :], c.ins["gate"]).then_inc(w_in, DMA)
                for dst, name in ((mult[:, :, :], "mult"), (sb1[:, :], "sb1"), (smult[:, :], "smult"),
                                  (b2[:, :], "b2")):
                    sp.dma_start(dst, c.ins[name]).then_inc(w_in, DMA)
                for n in range(SW // CHUNK):
                    if n >= 2:
                        sp.wait_ge(sw_lo, n - 1)
                    sp.dma_start(staged(n), c.ins["sw"][:, n * CHUNK:(n + 1) * CHUNK]).then_inc(sw_ins[n % 2], DMA)

            @block.gpsimd
            def _(pool):
                nc.gpsimd.memset(before[:, :, :], 1.0).then_inc(const, 1)
                pool.wait_ge(const, 1)
                nc.gpsimd.affine_select(out=before[:, :, :], in_=before[:, :, :], compare_op=ALU.is_gt, fill=0.0, base=0,
                                        pattern=[[1, E], [-1, E]], channel_multiplier=0).then_inc(const, 1)

            @block.scalar
            def _(act):
                act.wait_ge(w_in, 5 * DMA)
                nc.scalar.activation(gateH[:, :], gate_raw[:, :], ACT.Copy).then_inc(gate_hi, 1)
                for n in range(SW // CHUNK):
                    act.wait_ge(sw_ins[n % 2], (n // 2 + 1) * DMA)
                    nc.scalar.activation(wH[:, n * CHUNK:(n + 1) * CHUNK], staged(n), ACT.Copy).then_inc(sw_hi, 1)
                with act.Fori(0, B) as b:
                    act.wait_ge(shifted, b + 1)
                    nc.scalar.activation(ex[:, :, :], lg[:, :, :], ACT.Exp).then_inc(exp_done, 1)
                    def keep_hi(m):
                        act.wait_ge(araw_done, b * FST + m + 1)
                        nc.scalar.activation(aH[:, m, :], up[:, m % 2, :], ACT.Copy).then_inc(hi_done, 1)

                    for m in range(FST):
                        act.wait_ge(g_full, b * FST + m + 1)
                        nc.scalar.activation(gl[:, m % 2, :], c.pa[:, m % 4, :], ACT.Gelu,
                                             bias=sb1[:, FST + m:FST + m + 1]).then_inc(g_done, 1)
                        if m:
                            keep_hi(m - 1)
                    keep_hi(FST - 1)

            @block.vector
            def _(dve):
                dve.sem_inc(x_read, 2)
                dve.sem_inc(a_split, 2)
                dve.sem_inc(y_read, 2)
                dve.wait_ge(gate_hi, 1)
                nc.vector.tensor_tensor(gateL[:, :], gate_raw[:, :], gateH[:, :].bitcast(F32), ALU.subtract).then_inc(gate_lo, 1)
                for n in range(SW // CHUNK):
                    dve.wait_ge(sw_hi, n + 1)
                    part = slice(n * CHUNK, (n + 1) * CHUNK)
                    nc.vector.tensor_tensor(wL[:, part], staged(n), wH[:, part].bitcast(F32), ALU.subtract).then_inc(sw_lo, 1)
                dve.wait_ge(const, 2)
                with dve.Fori(0, B) as b:
                    dve.wait_ge(log_full, b + 1)
                    nc.vector.tensor_copy(logT[:, :], c.pd[0:EP, 0, :]).then_inc(log_copied, 1)
                    dve.wait_ge(logtok_full, b + 1)
                    nc.vector.reduce_max(peak[:, :], c.pd[:, 1, 0:TT * EP].rearrange("p (t e) -> p t e", e=EP)[:, :, 0:E], AX.X).then_inc(step, 1)
                    dve.wait_ge(step, STEPS * b + 1)
                    nc.vector.tensor_tensor(lg[:, :, :], c.pd[:, 1, 0:TT * EP].rearrange("p (t e) -> p t e", e=EP),
                                            peak[:, :].unsqueeze(2).to_broadcast([P, TT, EP]), ALU.subtract).then_inc(shifted, 1)
                    dve.wait_ge(exp_done, b + 1)
                    nc.vector.reduce_sum(tot[:, :], ex[:, :, 0:E], AX.X).then_inc(step, 1)
                    dve.wait_ge(step, STEPS * b + 2)
                    nc.vector.reciprocal(tot[:, :], tot[:, :]).then_inc(step, 1)
                    dve.wait_ge(step, STEPS * b + 3)
                    nc.vector.tensor_tensor(score[:, :, :], ex[:, :, 0:E], tot[:, :].unsqueeze(2).to_broadcast([P, TT, E]),
                                            ALU.mult).then_inc(step, 1)
                    dve.wait_ge(step, STEPS * b + 4)
                    for t in range(TT):
                        others = score[:, t, :].unsqueeze(1).to_broadcast([P, E, E])
                        own = score[:, t, :].unsqueeze(2).to_broadcast([P, E, E])
                        nc.vector.tensor_tensor(gt[:, t, :].rearrange("p (e f) -> p e f", f=E), others, own, ALU.is_gt)
                        last = nc.vector.tensor_tensor(eq[:, t, :].rearrange("p (e f) -> p e f", f=E), others, own, ALU.is_equal)
                    last.then_inc(step, 1)
                    dve.wait_ge(step, STEPS * b + 5)
                    nc.vector.tensor_tensor(eq[:, :, :], eq[:, :, :], before[:, :, :].rearrange("p e f -> p (e f)").unsqueeze(1)
                                            .to_broadcast([P, TT, E * E]), ALU.mult).then_inc(step, 1)
                    dve.wait_ge(step, STEPS * b + 6)
                    nc.vector.tensor_tensor(gt[:, :, :], gt[:, :, :], eq[:, :, :], ALU.add).then_inc(step, 1)
                    dve.wait_ge(step, STEPS * b + 7)
                    rank_b = rank[:, bass.ds(b * TT, TT), :]
                    apart(dve, c)
                    nc.vector.reduce_sum(rank_b.rearrange("p t e -> p (t e)"),
                                         gt[:, :, :].rearrange("p t (e f) -> p (t e) f", f=E), AX.X).then_inc(step, 1)
                    dve.wait_ge(step, STEPS * b + 8)
                    nc.vector.scalar_tensor_tensor(best[:, :, :], rank_b, TOPK - 0.5, score[:, :, :], ALU.is_lt, ALU.mult).then_inc(step, 1)
                    dve.wait_ge(step, STEPS * b + 9)
                    nc.vector.reduce_sum(tot[:, :], best[:, :, :], AX.X).then_inc(step, 1)
                    dve.wait_ge(step, STEPS * b + 10)
                    nc.vector.tensor_scalar(tot[:, :], tot[:, :], 1e-20, None, ALU.add).then_inc(step, 1)
                    dve.wait_ge(step, STEPS * b + 11)
                    nc.vector.reciprocal(tot[:, :], tot[:, :]).then_inc(step, 1)
                    dve.wait_ge(step, STEPS * b + 12)
                    nc.vector.memset(lg[:, :, E:EP], 1.0)
                    nc.vector.tensor_tensor(lg[:, :, 0:E], best[:, :, :], tot[:, :].unsqueeze(2).to_broadcast([P, TT, E]),
                                            ALU.mult).then_inc(comb_done, 1)
                    dve.wait_ge(comb_done, b + 1)
                    apart(dve, c)
                    nc.vector.tensor_copy(comb[:, bass.ds(b * TT, TT), :], lg[:, :, :]).then_inc(step, 1)
                    dve.wait_ge(combT_full, b + 1)
                    nc.vector.tensor_copy(combT[:, :], c.pd[0:EP, 0, :]).then_inc(combT_done, 1)
                    def keep_lo(m):
                        dve.wait_ge(hi_done, b * FST + m + 1)
                        nc.vector.tensor_tensor(aL[:, m, :], up[:, m % 2, :], aH[:, m, :].bitcast(F32), ALU.subtract).then_inc(a_split, 1)

                    for m in range(FST):
                        dve.wait_ge(x_full, b * FST + m + 1)
                        dve.wait_ge(a_split, b * FST + m + 1)
                        nc.vector.tensor_scalar(up[:, m % 2, :], c.pd[:, 2 + m % 2, :], sb1[:, m:m + 1], smult[:, m:m + 1],
                                                ALU.add, ALU.mult).then_inc(x_read, 1)
                        dve.wait_ge(x_read, b * FST + m + 3)
                        dve.wait_ge(g_done, b * FST + m + 1)
                        nc.vector.tensor_tensor(up[:, m % 2, :], up[:, m % 2, :], gl[:, m % 2, :], ALU.mult).then_inc(araw_done, 1)
                        if m:
                            keep_lo(m - 1)
                    keep_lo(FST - 1)
                    for n in range(2):
                        dve.wait_ge(y_full, 2 * b + n + 1)
                        xb = c.X[:, bass.ds(b * TT + 2 * n, 2), :].rearrange("p n d -> p (n d)")
                        nc.vector.tensor_tensor(xb, c.pd[:, n, :], xb, ALU.add).then_inc(y_read, 1)

            @block.tensor
            def _(pe):
                pe.wait_ge(gate_lo, 1)
                pe.wait_ge(sw_lo, SW // CHUNK)
                with pe.Fori(0, B) as b:
                    xn = lambda k: [x[:, k, bass.ds(b * S, S)] for x in (c.xnH, c.xnL)]
                    pe.wait_ge(y_read, 2 * b + 2)
                    for k in range(KT):
                        last = hi_lo(pe, nc, c.pd[0:EP, 0, :], [x[:, k * EP:(k + 1) * EP] for x in (gateH, gateL)], xn(k),
                                     k == 0, k == KT - 1)
                    last.then_inc(log_full, 1)
                    pe.wait_ge(log_copied, b + 1)
                    apart(pe, c)
                    for t in range(TT):
                        last = nc.tensor.transpose(c.pd[:, 1, t * EP:(t + 1) * EP], logT[:, t * P:(t + 1) * P], c.ident[0:EP, 0:EP])
                    last.then_inc(logtok_full, 1)
                    for m in range(FST):
                        if m == 2:
                            pe.wait_ge(comb_done, b + 1)
                            for t in range(TT):
                                last = nc.tensor.transpose(c.pd[0:EP, 0, t * P:(t + 1) * P], lg[:, t, :], c.ident[:, :])
                            last.then_inc(combT_full, 1)
                        for k in range(KT):
                            last = hi_lo(pe, nc, c.pa[:, m % 4, :], up_w(FST + m, k), xn(k), k == 0, k == KT - 1)
                        last.then_inc(g_full, 1)
                        pe.wait_ge(x_read, b * FST + m + 1)
                        for k in range(KT):
                            last = hi_lo(pe, nc, c.pd[:, 2 + m % 2, :], up_w(m, k), xn(k), k == 0, k == KT - 1)
                        last.then_inc(x_full, 1)
                    pe.wait_ge(combT_done, b + 1)
                    pe.wait_ge(a_split, b * FST + FST + 2)
                    for n in range(2):
                        for t in (2 * n, 2 * n + 1):
                            out = c.pd[:, n, (t % 2) * D:(t % 2 + 1) * D]
                            nc.tensor.matmul(out, combT[:, t * P:(t + 1) * P], b2[:, :], start=True, stop=False)
                            for k in range(FST):
                                last = hi_lo(pe, nc, out, [x[:, k, t * P:(t + 1) * P] for x in (aH, aL)], down_w(k),
                                             False, k == FST - 1)
                        last.then_inc(y_full, 1)

        with ExitStack() as inner:
            sb = lambda n, s, d=F32: inner.enter_context(nc.sbuf_tensor(f"me_{n}", s, d))
            b1 = sb("b1", [P, E, 2 * F])
            lane_int = sb("lane_int", [P, P], I32)
            lane_of = sb("lane_of", [P, P])
            token_int = sb("token_int", [P, NT], I32)
            token_of = sb("token_of", [P, NT])
            ones = sb("ones", [P, P], BF16)
            earlier = sb("earlier", [P, P], BF16)
            chosen = sb("chosen", [P, NT + 1, E], BF16)
            count = sb("count", [P, E])
            full = sb("full", [P, E, NT])
            blocks = sb("blocks", [P, E])
            below = sb("below", [P, E, E])
            start = sb("start", [P, E])
            end = sb("end", [P, E])
            past = sb("past", [P, BLOCKS, E])
            expert = sb("expert", [P, BLOCKS])
            expert_id = sb("expert_id", [P, BLOCKS], I32)
            place = sb("place", [P, NT, E])
            match = sb("match", [P, 2, NT, E])
            slot = sb("slot", [P, TOPK, NT])
            weight = sb("weight", [P, TOPK, NT])
            slot_id = sb("slot_id", [P, TOPK, NT], I32)
            slot_block = sb("slot_block", [P, TOPK, NT], I32)
            block_f = sb("block_f", [P, TOPK, NT])
            lane_f = sb("lane_f", [P, TOPK, NT])
            lane_hot = sb("lane_hot", [P, NT, P])
            block_hot = sb("block_hot", [P, NT, BLOCKS])
            token_id = sb("token_id", [P, BLOCKS], I32)
            x_index = sb("x_index", [P, RING, 1], I32)
            rows = sb("rows", [P, RING, D])
            xT = sb("xT", [P, RING, KT, P])
            gate = sb("gate", [P, RING, F])
            gl = sb("gl", [P, RING, F])
            up = sb("up", [P, RING, F])
            aT = sb("aT", [P, RING, FT, P])
            y = sb("y", [P, RING, D])
            y_index = sb("y_index", [P, 2, TOPK, 1], I32)
            y_rows = sb("y_rows", [P, 2, TOPK, D])
            (const, b_loaded, step, sel_done, prefix_full, hot_done, hot_used, ids_full, ids_done, x_picked, xt_full, xt_done, h_full,
             g_ready, h_read, gelu_done, a_done, at_full, at_done, y_full, y_done, y_picked, add_step, added) = semaphores(
                nc, inner, "me", "const b_loaded step sel_done prefix_full hot_done hot_used ids_full ids_done x_picked xt_full xt_done "
                "h_full g_ready h_read gelu_done a_done at_full at_done y_full y_done y_picked add_step added")
            gathered = semaphores(nc, inner, "me", "gathered0 gathered1 gathered2 gathered3")
            y_stored = semaphores(nc, inner, "me", "y_stored0 y_stored1 y_stored2 y_stored3")
            y_in = semaphores(nc, inner, "me", "y_in0 y_in1")
            ROUNDS = BLOCKS // RING
            BANKS = 2
            half = lambda bank, h: bank[:, h * D:(h + 1) * D]
            xt_bank = lambda s: half(c.pa[:, s % BANKS, :], 0)
            at_bank = lambda s: half(c.pa[:, BANKS + s % BANKS, :], 0)
            h_bank = lambda s: c.pd[:, s % BANKS, :]
            y_bank = lambda s: half(c.pd[:, BANKS + s % BANKS, :], 0)
            block = inner.enter_context(nc.Block())

            def all_blocks(engine, work, flush=None):
                for s in range(RING):
                    work(0, s, s)
                with engine.Fori(1, ROUNDS - 1) as i:
                    for s in range(RING):
                        work(i, s, None)
                for s in range(RING):
                    work(ROUNDS - 1, s, BLOCKS - RING + s)

            def neighbour(i, s, n, by):
                to = s + by
                return i + to // RING, to % RING, None if n is None else n + by

            exists = lambda n: n is None or 0 <= n < BLOCKS
            at = lambda i, s: i * RING + s

            @block.sync
            def _(sp):
                third = E // 3
                for k in range(3):
                    part = c.ins["b1row"][k * third * 2 * F:(k + 1) * third * 2 * F]
                    sp.dma_start(b1[:, k * third:(k + 1) * third, :].rearrange("p e f -> p (e f)"), part.partition_broadcast(P)).then_inc(b_loaded, DMA)

                def work(i, s, n):
                    sp.wait_ge(y_done, at(i, s) + 1 + BANKS)
                    sp.dma_start(c.y_dram[bass.ds(at(i, s) * P, P), :], y[:, s, :]).then_inc(y_stored[s], DMA)

                all_blocks(sp, work)
                for s in range(RING):
                    sp.wait_ge(y_stored[s], (ROUNDS + 1) * DMA)

            @block.gpsimd
            def _(pool):
                nc.gpsimd.iota(lane_int[:, :], [[1, P]], base=0, channel_multiplier=0).then_inc(const, 1)
                nc.gpsimd.iota(token_int[:, :], [[P, NT]], base=0, channel_multiplier=1).then_inc(const, 1)
                nc.gpsimd.memset(ones[:, :], 1.0).then_inc(const, 1)
                nc.gpsimd.memset(earlier[:, :], 1.0).then_inc(const, 1)
                nc.gpsimd.memset(chosen[:, NT, :], 0.0).then_inc(const, 1)
                pool.wait_ge(const, 5)
                nc.gpsimd.affine_select(out=earlier[:, :], in_=earlier[:, :], compare_op=ALU.is_gt, fill=0.0, base=0,
                                        pattern=[[1, P]], channel_multiplier=-1).then_inc(const, 1)
                pool.wait_ge(ids_done, 2)

                def work(i, s, n):
                    pool.wait_ge(xt_full, at(i, s) + 1)
                    apart(pool, c)
                    nc.gpsimd.tensor_copy(x_index[:, s, :], token_id[:, bass.ds(at(i, s), 1)]).then_inc(x_picked, 1)
                    pool.wait_ge(x_picked, at(i, s) + 1)
                    apart(pool, c)
                    nc.gpsimd.indirect_dma_start(out=rows[:, s, :], out_offset=None, in_=c.rows_dram,
                                                 in_offset=bass.IndirectOffsetOnAxis(x_index[:, s, :].bitcast(U32), 0)).then_inc(gathered[s], DMA)

                all_blocks(pool, work)
                for s in range(RING):
                    pool.wait_ge(y_stored[s], (ROUNDS + 1) * DMA)
                with pool.Fori(0, NT // 2) as i:
                    for h in range(2):
                        pool.wait_ge(added, i * 2 + h + 1)
                        for k in range(TOPK):
                            if k == 0:
                                apart(pool, c)
                            last = nc.gpsimd.tensor_copy(y_index[:, h, k, :], slot_id[:, k, bass.ds(i * 2 + h, 1)])
                        last.then_inc(y_picked, 1)
                        pool.wait_ge(y_picked, i * 2 + h + 1)
                        apart(pool, c)
                        for k in range(TOPK):
                            nc.gpsimd.indirect_dma_start(out=y_rows[:, h, k, :], out_offset=None, in_=c.y_dram,
                                                         in_offset=bass.IndirectOffsetOnAxis(y_index[:, h, k, :].bitcast(U32), 0)).then_inc(y_in[h], DMA)

            @block.scalar
            def _(act):
                act.wait_ge(ids_done, 2)

                def turn_x(i, s):
                    act.wait_ge(xt_full, at(i, s) + 1 + RING)
                    nc.scalar.activation(xT[:, s, :, :].rearrange("p k t -> p (k t)"), xt_bank(s), ACT.Copy).then_inc(xt_done, 1)

                def work(i, s, n):
                    if n == 0:
                        turn_x(i, s)
                    i1, s1, n1 = neighbour(i, s, n, 1)
                    if exists(n1):
                        turn_x(i1, s1)
                    act.wait_ge(g_ready, at(i, s) + 1)
                    nc.scalar.activation(gl[:, s, :], gate[:, s, :], ACT.Gelu).then_inc(gelu_done, 1)
                    i0, s0, n0 = neighbour(i, s, n, -1)
                    if exists(n0):
                        scale_a(i0, s0)
                    if n == BLOCKS - 1:
                        scale_a(i, s)

                def scale_a(i, s):
                    e = act.value_load(expert_id[0:1, bass.ds(at(i, s), 1)], min_val=0, max_val=E - 1)
                    act.wait_ge(at_full, at(i, s) + 1)
                    apart(act, c)
                    for f in range(FT):
                        last = nc.scalar.activation(aT[:, s, f, :], at_bank(s)[:, f * P:(f + 1) * P], ACT.Copy,
                                                    scale=mult[:, bass.ds(e, 1), f:f + 1].rearrange("p o f -> p (o f)"))
                    last.then_inc(at_done, 1)

                all_blocks(act, work)

            @block.vector
            def _(dve):
                dve.sem_inc(h_read, BANKS)
                dve.sem_inc(y_done, BANKS)
                dve.sem_inc(added, 2)
                for s in range(RING):
                    dve.sem_inc(y_stored[s], DMA)
                steps = 0

                def done(instruction):
                    nonlocal steps
                    instruction.then_inc(step, 1)
                    steps += 1
                    dve.wait_ge(step, steps)

                V = nc.vector
                dve.wait_ge(const, 6)
                V.tensor_scalar(chosen[:, 0:NT, :], rank[:, :, :], TOPK - 0.5, None, ALU.is_lt).then_inc(sel_done, 1)
                V.tensor_copy(token_of[:, :], token_int[:, :])
                done(V.tensor_copy(lane_of[:, :], lane_int[:, :]))
                dve.wait_ge(prefix_full, 1)
                done(V.tensor_copy(count[:, :], c.pd[:, 0, NT * E:(NT + 1) * E]))
                done(V.tensor_scalar(blocks[:, :], count[:, :], 1.0 / P, None, ALU.mult))
                done(V.tensor_tensor(full[:, :, :], blocks[:, :].unsqueeze(2).to_broadcast([P, E, NT]),
                                     lane_of[:, 0:NT].unsqueeze(1).to_broadcast([P, E, NT]), ALU.is_gt))
                done(V.reduce_sum(blocks[:, :], full[:, :, :], AX.X))
                done(V.tensor_tensor(below[:, :, :], before[:, :, :], blocks[:, :].unsqueeze(1).to_broadcast([P, E, E]), ALU.mult))
                done(V.reduce_sum(start[:, :], below[:, :, :], AX.X))
                V.tensor_tensor(end[:, :], start[:, :], blocks[:, :], ALU.add)
                done(V.tensor_scalar(count[:, :], start[:, :], float(P), None, ALU.mult))
                done(V.tensor_tensor(place[:, :, :], c.pd[:, 0, 0:NT * E].rearrange("p (t e) -> p t e", e=E),
                                     count[:, :].unsqueeze(1).to_broadcast([P, NT, E]), ALU.add))
                for k in range(TOPK):
                    V.scalar_tensor_tensor(match[:, 0, :, :], rank[:, :, :], float(k), place[:, :, :], ALU.is_equal, ALU.mult)
                    done(V.scalar_tensor_tensor(match[:, 1, :, :], rank[:, :, :], float(k), comb[:, :, 0:E], ALU.is_equal, ALU.mult))
                    V.reduce_sum(slot[:, k, :], match[:, 0, :, :], AX.X)
                    done(V.reduce_sum(weight[:, k, :], match[:, 1, :, :], AX.X))
                done(V.tensor_copy(slot_id[:, :, :], slot[:, :, :]))
                done(V.tensor_scalar(slot_block[:, :, :], slot_id[:, :, :], 7, None, ALU.arith_shift_right))
                done(V.tensor_copy(block_f[:, :, :], slot_block[:, :, :]))
                done(V.scalar_tensor_tensor(lane_f[:, :, :], block_f[:, :, :], -float(P), slot[:, :, :], ALU.mult, ALU.add))
                for k in range(TOPK):
                    if k:
                        dve.wait_ge(hot_used, k)
                    V.tensor_tensor(lane_hot[:, :, :], lane_f[:, k, :].unsqueeze(2).to_broadcast([P, NT, P]),
                                    lane_of[:, :].unsqueeze(1).to_broadcast([P, NT, P]), ALU.is_equal)
                    done(V.tensor_tensor(block_hot[:, :, :], block_f[:, k, :].unsqueeze(2).to_broadcast([P, NT, BLOCKS]),
                                         lane_of[:, 0:BLOCKS].unsqueeze(1).to_broadcast([P, NT, BLOCKS]), ALU.is_equal))
                    V.tensor_tensor(block_hot[:, :, :], block_hot[:, :, :], token_of[:, :].unsqueeze(2).to_broadcast([P, NT, BLOCKS]),
                                    ALU.mult).then_inc(hot_done, 1)
                done(V.tensor_tensor(past[:, :, :], lane_of[:, 0:BLOCKS].unsqueeze(2).to_broadcast([P, BLOCKS, E]),
                                     end[:, :].unsqueeze(1).to_broadcast([P, BLOCKS, E]), ALU.is_ge))
                done(V.reduce_sum(expert[:, :], past[:, :, :], AX.X))
                done(V.tensor_scalar(expert[:, :], expert[:, :], float(E - 1), None, ALU.min))
                V.tensor_copy(expert_id[:, :], expert[:, :]).then_inc(ids_done, 1)
                dve.wait_ge(ids_full, 1)
                V.tensor_copy(token_id[:, :], c.pd[:, 1, 0:BLOCKS]).then_inc(ids_done, 1)
                dve.wait_ge(ids_done, 2)
                dve.wait_ge(b_loaded, 3 * DMA)

                def keep_y(i, s):
                    dve.wait_ge(y_full, at(i, s) + 1)
                    dve.wait_ge(y_stored[s], i * DMA + DMA)
                    V.tensor_copy(y[:, s, :], y_bank(s)).then_inc(y_done, 1)

                def work(i, s, n):
                    e = dve.value_load(expert_id[0:1, bass.ds(at(i, s), 1)], min_val=0, max_val=E - 1)
                    bias = lambda f: b1[:, bass.ds(e, 1), f:f + F].rearrange("p o f -> p (o f)")
                    dve.wait_ge(h_full, at(i, s) + 1)
                    V.tensor_tensor(gate[:, s, :], half(h_bank(s), 1), bias(F), ALU.add).then_inc(g_ready, 1)
                    V.tensor_tensor(up[:, s, :], half(h_bank(s), 0), bias(0), ALU.add).then_inc(h_read, 1)
                    i2, s2, n2 = neighbour(i, s, n, -2)
                    if exists(n2):
                        keep_y(i2, s2)
                    dve.wait_ge(gelu_done, at(i, s) + 1)
                    dve.wait_ge(h_read, at(i, s) + 1 + BANKS)
                    V.tensor_tensor(up[:, s, :], up[:, s, :], gl[:, s, :], ALU.mult).then_inc(a_done, 1)
                    if n == BLOCKS - 1:
                        keep_y(*neighbour(i, s, n, -1)[:2])
                        keep_y(i, s)

                all_blocks(dve, work)
                with dve.Fori(0, NT // 2) as i:
                    for h in range(2):
                        t = bass.ds(i * 2 + h, 1)
                        xt = c.X[:, t, :].rearrange("p o d -> p (o d)")
                        dve.wait_ge(y_in[h], (i + 1) * TOPK * DMA)
                        for k in range(TOPK):
                            if k:
                                dve.wait_ge(add_step, (i * 2 + h) * 2 + k)
                            last = V.scalar_tensor_tensor(xt, y_rows[:, h, k, :], weight[:, k, t], xt, ALU.mult, ALU.add)
                            last.then_inc(add_step if k < TOPK - 1 else added, 1)

            @block.tensor
            def _(pe):
                pe.sem_inc(xt_full, RING)
                pe.wait_ge(const, 6)
                pe.wait_ge(sel_done, 1)
                nc.tensor.matmul(c.pd[:, 0, 0:(NT + 1) * E], earlier[:, :], chosen[:, :, :].rearrange("p t e -> p (t e)"), start=True, stop=False)
                for t in range(NT):
                    later = NT - t
                    last = nc.tensor.matmul(c.pd[:, 0, (t + 1) * E:(NT + 1) * E], ones[:, :],
                                            chosen[:, t, :].unsqueeze(1).to_broadcast([P, later, E]), start=False, stop=t == NT - 1)
                last.then_inc(prefix_full, 1)
                for k in range(TOPK):
                    pe.wait_ge(hot_done, k + 1)
                    for t in range(NT):
                        last = nc.tensor.matmul(c.pd[:, 1, 0:BLOCKS], lane_hot[:, t, :], block_hot[:, t, :], start=k == 0 and t == 0,
                                                stop=k == TOPK - 1 and t == NT - 1)
                    last.then_inc(hot_used if k < TOPK - 1 else ids_full, 1)
                pe.wait_ge(ids_done, 2)
                pe.wait_ge(w_loaded, E * DMA)

                def turn_x(i, s):
                    pe.wait_ge(gathered[s], i * DMA + DMA)
                    for k in range(KT):
                        last = nc.tensor.transpose(xt_bank(s)[:, k * P:(k + 1) * P], rows[:, s, k * P:(k + 1) * P], c.ident[:, :])
                    last.then_inc(xt_full, 1)

                def turn_a(i, s):
                    pe.wait_ge(a_done, at(i, s) + 1)
                    for f in range(FT):
                        last = nc.tensor.transpose(at_bank(s)[:, f * P:(f + 1) * P], up[:, s, f * P:(f + 1) * P], c.ident[:, :])
                    last.then_inc(at_full, 1)

                def second_layer(i, s):
                    e = pe.value_load(expert_id[0:1, bass.ds(at(i, s), 1)], min_val=0, max_val=E - 1)
                    pe.wait_ge(at_done, at(i, s) + 1)
                    pe.wait_ge(y_done, at(i, s) + 1)
                    for f in range(FT):
                        move = weights[:, bass.ds(e, 1), W1 + f * D:W1 + (f + 1) * D].rearrange("p o n -> p (o n)")
                        last = nc.tensor.matmul(y_bank(s), aT[:, s, f, :], move, start=f == 0, stop=f == FT - 1)
                    last.then_inc(y_full, 1)

                def work(i, s, n):
                    if n == 0:
                        turn_x(i, s)
                    i1, s1, n1 = neighbour(i, s, n, 1)
                    if exists(n1):
                        turn_x(i1, s1)
                    e = pe.value_load(expert_id[0:1, bass.ds(at(i, s), 1)], min_val=0, max_val=E - 1)
                    pe.wait_ge(xt_done, at(i, s) + 1)
                    pe.wait_ge(h_read, at(i, s) + 1)
                    for k in range(KT):
                        move = weights[:, bass.ds(e, 1), k * 2 * F:(k + 1) * 2 * F].rearrange("p o n -> p (o n)")
                        last = nc.tensor.matmul(h_bank(s), xT[:, s, k, :], move, start=k == 0, stop=k == KT - 1)
                    last.then_inc(h_full, 1)
                    i0, s0, n0 = neighbour(i, s, n, -1)
                    if exists(n0):
                        turn_a(i0, s0)
                    i2, s2, n2 = neighbour(i, s, n, -2)
                    if exists(n2):
                        second_layer(i2, s2)
                    if n == BLOCKS - 1:
                        turn_a(i, s)
                        second_layer(*neighbour(i, s, n, -1)[:2])
                        second_layer(i, s)

                all_blocks(pe, work)


def second_projection_phase(nc, c):
    USES = 6
    with ExitStack() as ctx:
        sb = lambda n, s, d=F32: ctx.enter_context(nc.sbuf_tensor(f"p_{n}", s, d))
        raw = sb("raw", [P, 3, KT * D])
        wH = sb("wH", [P, 3, KT * D], F32R)
        wL = sb("wL", [P, 3, KT * D], F32R)
        ctx_raw = sb("ctx_raw", [P, KT, S])
        ctxH = sb("ctxH", [P, KT, S], F32R)
        ctxL = sb("ctxL", [P, KT, S], F32R)
        qkH = sb("qkH", [P, 2 * KT, S], F32R)
        qkL = sb("qkL", [P, 2 * KT, S], F32R)
        V = sb("V", [P, TT, H1, 2 * DH1])
        (w_in, w_hi, w_lo, const, ctx_in, ctx_hi, ctx_lo, use_full, hi_done, use_read, stored) = semaphores(
            nc, ctx, "p", "w_in w_hi w_lo const ctx_in ctx_hi ctx_lo use_full hi_done use_read stored")
        STORES = 5 * DMA
        block = ctx.enter_context(nc.Block())

        @block.sync
        def _(sp):
            for n, name in enumerate(("wq1", "wk1", "wv1")):
                sp.dma_start(raw[:, n, :], c.ins[name]).then_inc(w_in, DMA)
            with sp.Fori(0, B) as b:
                sp.wait_ge(ctx_lo, b + 1)
                sp.dma_start(ctx_raw[:, :, :], c.ins["ctx"][:, :, bass.ds(b * S, S)]).then_inc(ctx_in, DMA)
                for n, part in enumerate((c.q_dram, c.k_dram)):
                    sp.wait_ge(use_read, b * USES + 2 * n + 2 + 3)
                    for l, src in enumerate((qkH, qkL)):
                        sp.dma_start(part[bass.ds(b, 1), l, :, :].rearrange("o (m p) t -> p (o m) t", p=P),
                                     src[:, n * KT:(n + 1) * KT, :].bitcast(F32)).then_inc(stored, DMA)
                sp.wait_ge(use_read, b * USES + USES + 3)
                sp.dma_start(c.v_dram[bass.ds(b, 1), :, :].rearrange("o p n -> (o p) n"),
                             V[:, :, :, :].rearrange("p t h d -> p (t h d)")).then_inc(stored, DMA)
            sp.wait_ge(stored, (B + 1) * STORES)

        @block.gpsimd
        def _(pool):
            nc.gpsimd.memset(V[:, :, :, :], 1.0).then_inc(const, 1)

        @block.scalar
        def _(act):
            act.sem_inc(stored, STORES)
            act.wait_ge(w_in, 3 * DMA)
            nc.scalar.activation(wH[:, :, :], raw[:, :, :], ACT.Copy).then_inc(w_hi, 1)
            with act.Fori(0, B) as b:
                act.wait_ge(ctx_in, b * DMA + DMA)
                nc.scalar.activation(ctxH[:, :, :], ctx_raw[:, :, :], ACT.Copy).then_inc(ctx_hi, 1)
                act.wait_ge(stored, b * STORES + STORES)
                for u in range(2 * KT):
                    act.wait_ge(use_full, b * USES + u + 1)
                    nc.scalar.activation(qkH[:, u, :], c.pd[:, u % 3, :], ACT.Copy).then_inc(hi_done, 1)

        @block.vector
        def _(dve):
            dve.sem_inc(use_read, 3)
            dve.sem_inc(ctx_lo, 1)
            dve.wait_ge(w_hi, 1)
            nc.vector.tensor_tensor(wL[:, :, :], raw[:, :, :], wH[:, :, :].bitcast(F32), ALU.subtract).then_inc(w_lo, 1)
            dve.wait_ge(const, 1)
            with dve.Fori(0, B) as b:
                dve.wait_ge(ctx_hi, b + 1)
                nc.vector.tensor_tensor(ctxL[:, :, :], ctx_raw[:, :, :], ctxH[:, :, :].bitcast(F32), ALU.subtract).then_inc(ctx_lo, 1)
                for u in range(2 * KT):
                    dve.wait_ge(hi_done, b * 2 * KT + u + 1)
                    nc.vector.tensor_tensor(qkL[:, u, :], c.pd[:, u % 3, :], qkH[:, u, :].bitcast(F32), ALU.subtract).then_inc(use_read, 1)
                for n in range(2):
                    u = 2 * KT + n
                    dve.wait_ge(use_full, b * USES + u + 1)
                    dve.wait_ge(stored, b * STORES + STORES)
                    nc.vector.tensor_copy(V[:, 2 * n:2 * n + 2, :, 0:DH1],
                                          c.pd[:, u % 3, :].rearrange("p (t h d) -> p t h d", t=2, d=DH1)).then_inc(use_read, 1)

        @block.tensor
        def _(pe):
            pe.wait_ge(w_lo, 1)
            weight = lambda w, k, lo, n: [x[:, w, k * D + lo:k * D + lo + n] for x in (wH, wL)]
            with pe.Fori(0, B) as b:
                for u in range(2 * KT):
                    if u == KT:
                        pe.wait_ge(ctx_lo, b + 2)
                    pe.wait_ge(use_read, b * USES + u + 1)
                    for k in range(KT):
                        move = [x[:, k, bass.ds(b * S, S)] for x in (c.xnH, c.xnL)] if u < KT else [x[:, k, :] for x in (ctxH, ctxL)]
                        last = hi_lo(pe, nc, c.pd[:, u % 3, :], weight(u // KT, k, (u % KT) * P, P), move, k == 0, k == KT - 1)
                    last.then_inc(use_full, 1)
                for n in range(2):
                    u = 2 * KT + n
                    pe.wait_ge(use_read, b * USES + u + 1)
                    for t in (2 * n, 2 * n + 1):
                        for k in range(KT):
                            last = hi_lo(pe, nc, c.pd[:, u % 3, (t % 2) * D:(t % 2 + 1) * D],
                                         [x[:, k, t * P:(t + 1) * P] for x in (ctxH, ctxL)], weight(2, k, 0, D), k == 0, k == KT - 1)
                    last.then_inc(use_full, 1)


def second_attention_phase(nc, c):
    R = 2 * DH1
    with ExitStack() as ctx:
        sb = lambda n, s, d=F32: ctx.enter_context(nc.sbuf_tensor(f"b_{n}", s, d))
        q4 = sb("q4", [P, 2, GH, S], F32R)
        k4 = sb("k4", [P, 2, GH, S], F32R)
        AUX = 4 * DH1
        V = sb("V", [P, TT, H1, R])
        zeros = sb("zeros", [1, GH * S])
        mask_in = sb("mask_in", [P, 2, TT, S], U8)
        by_query = sb("by_query", [P, TT, S])
        by_key = sb("by_key", [P, TT, S], BF16)
        ident_bf = sb("ident_bf", [P, P], BF16)
        select = sb("select", [P, P])
        masked = sb("masked", [P, 2, S], BF16)
        mx = sb("mx", [P, 4, TT])
        prob = sb("prob", [P, 2, GH, TT, S])
        raw = sb("raw", [P, GROUPS * D])
        woH = sb("woH", [P, GROUPS * D], F32R)
        woL = sb("woL", [P, GROUPS * D], F32R)
        osum = sb("osum", [P, 2, S])
        inv = sb("inv", [P, S])
        oH = sb("oH", [P, GROUPS, S], F32R)
        oL = sb("oL", [P, GROUPS, S], F32R)
        (const, w_in, mask_loaded, w_hi, w_lo, mask_done, v_in, qk_in0, qk_in1, s_full, s_read, row_full, row_done, st_full,
         exp_done, pv_full, osum_done, sel_full, sel_read, norm_step, o_split, y_full, y_read) = semaphores(
            nc, ctx, "b", "const w_in mask_loaded w_hi w_lo mask_done v_in qk_in0 qk_in1 s_full s_read row_full row_done st_full "
            "exp_done pv_full osum_done sel_full sel_read norm_step o_split y_full y_read")
        qk_ins = (qk_in0, qk_in1)
        QK_LOADS = 9 * DMA
        PV_LAG = 5
        block = ctx.enter_context(nc.Block())

        @block.sync
        def _(sp):
            sp.dma_start(raw[:, :], c.ins["wo1"]).then_inc(w_in, DMA)
            sp.dma_start(mask_in[:, 0, :, :], c.ins["mask"].rearrange("(n p) k -> p n k", p=P)).then_inc(mask_loaded, DMA)
            sp.dma_start(mask_in[:, 1, :, :], c.ins["maskT"].rearrange("(n p) k -> p n k", p=P)).then_inc(mask_loaded, DMA)
            sp.wait_ge(const, 6)
            with sp.Fori(0, B) as b:
                for g in range(GROUPS):
                    sp.wait_ge(st_full, b * 2 * H1 + (g + 1) * 2 * GH)
                    rows = lambda part, l: part[bass.ds(b, 1), l, g * GH * DH1:(g + 1) * GH * DH1, :].rearrange("o (h d) t -> d (o h) t", d=DH1)
                    done = qk_ins[g % 2]
                    for r, (ql, kl) in enumerate(((0, 0), (1, 0), (0, 1), (1, 1))):
                        at = slice(r * DH1, (r + 1) * DH1)
                        sp.dma_start(q4[at, g % 2, :, :].bitcast(F32), rows(c.q_dram, ql)).then_inc(done, DMA)
                        sp.dma_start(k4[at, g % 2, :, :].bitcast(F32), rows(c.k_dram, kl)).then_inc(done, DMA)
                    sp.dma_start(q4[AUX:AUX + 1, g % 2, :, :].rearrange("p h s -> p (h s)").bitcast(F32), zeros[:, :]).then_inc(done, DMA)
                    if g == 0:
                        sp.wait_ge(pv_full, b * GROUPS + 2)
                        sp.dma_start(V[:, :, :, :].rearrange("p t h d -> p (t h d)"),
                                     c.v_dram[bass.ds(b, 1), :, :].rearrange("o p n -> (o p) n")).then_inc(v_in, DMA)

        @block.gpsimd
        def _(pool):
            nc.gpsimd.memset(zeros[:, :], 0.0).then_inc(const, 1)
            nc.gpsimd.memset(q4[AUX:P, :, :, :].bitcast(F32), 0.0).then_inc(const, 1)
            nc.gpsimd.memset(k4[AUX:P, :, :, :].bitcast(F32), 0.0).then_inc(const, 1)
            pool.wait_ge(const, 3)
            nc.gpsimd.memset(k4[AUX:AUX + 1, :, :, :].bitcast(F32), 1.0).then_inc(const, 1)
            pool.wait_ge(const, 4)
            nc.gpsimd.memset(select[:, :], 0.0).then_inc(const, 1)
            pool.wait_ge(const, 5)
            sel = select[:, :].rearrange("p (h r) -> p h r", r=R)
            nc.gpsimd.affine_select(out=sel, in_=sel, compare_op=ALU.not_equal, fill=1.0, base=-DH1,
                                    pattern=[[-R, GH], [0, R]], channel_multiplier=1).then_inc(const, 1)

        @block.scalar
        def _(act):
            act.wait_ge(w_in, DMA)
            nc.scalar.activation(woH[:, :], raw[:, :], ACT.Copy).then_inc(w_hi, 1)
            act.wait_ge(mask_loaded, 2 * DMA)
            nc.scalar.activation(by_key[:, :, :], mask_in[:, 1, :, :], ACT.Copy, scale=MASKED).then_inc(mask_done, 1)
            nc.scalar.activation(ident_bf[:, :], c.ident[:, :], ACT.Copy).then_inc(mask_done, 1)
            with act.Fori(0, B) as b:
                def keep_sums(g):
                    act.wait_ge(pv_full, b * GROUPS + g + 1 + 2)
                    act.wait_ge(o_split, b * GROUPS + g + 1)
                    nc.scalar.activation(osum[:, g % 2, :], c.pd[:, 2, :], ACT.Copy).then_inc(osum_done, 1)

                for n in range(H1):
                    g, i = n // GH, n % GH
                    act.wait_ge(row_full, b * H1 + n + 1)
                    nc.scalar.activation(q4[AUX:AUX + 1, g % 2, i, :], c.pd[0:1, 3, :], ACT.Copy, scale=-1.0).then_inc(row_done, 1)
                    if i == 0 and g >= 2:
                        keep_sums(g - 2)
                    for half in range(2):
                        act.wait_ge(st_full, (b * H1 + n) * 2 + half + 1 + 4 * GH)
                        act.wait_ge(pv_full, b * GROUPS + g + 1)
                        nc.scalar.activation(prob[:, g % 2, i, 2 * half:2 * half + 2, :], c.pa[:, 2 * half:2 * half + 2, :], ACT.Exp,
                                             scale=DH1 ** -0.5).then_inc(exp_done, 1)
                keep_sums(2)
                keep_sums(3)

        @block.vector
        def _(dve):
            dve.sem_inc(s_read, 2)
            dve.sem_inc(o_split, 2)
            dve.sem_inc(y_read, 2)
            dve.sem_inc(sel_read, 1)
            dve.wait_ge(w_hi, 1)
            nc.vector.tensor_tensor(woL[:, :], raw[:, :], woH[:, :].bitcast(F32), ALU.subtract).then_inc(w_lo, 1)
            dve.wait_ge(mask_loaded, 2 * DMA)
            nc.vector.tensor_scalar(by_query[:, :, :], mask_in[:, 0, :, :], MASKED, None, ALU.mult).then_inc(mask_done, 1)
            dve.wait_ge(mask_done, 3)
            with dve.Fori(0, B) as b:
                def normalise(g):
                    G = b * GROUPS + g
                    dve.wait_ge(sel_full, G + 1)
                    dve.wait_ge(o_split, G + 2)
                    nc.vector.tensor_scalar(inv[:, :], c.pd[:, 3, :], 1e-30, None, ALU.max).then_inc(sel_read, 1)
                    dve.wait_ge(sel_read, G + 2)
                    nc.vector.reciprocal(inv[:, :], inv[:, :]).then_inc(norm_step, 1)
                    dve.wait_ge(norm_step, 3 * G + 1)
                    nc.vector.tensor_tensor(inv[:, :], osum[:, g % 2, :], inv[:, :], ALU.mult).then_inc(norm_step, 1)
                    dve.wait_ge(norm_step, 3 * G + 2)
                    nc.vector.tensor_copy(oH[:, g, :], inv[:, :]).then_inc(norm_step, 1)
                    dve.wait_ge(norm_step, 3 * G + 3)
                    nc.vector.tensor_tensor(oL[:, g, :], inv[:, :], oH[:, g, :].bitcast(F32), ALU.subtract).then_inc(o_split, 1)

                for n in range(H1):
                    for t in range(TT):
                        dve.wait_ge(s_full, (b * H1 + n) * TT + t + 1)
                        dve.wait_ge(s_read, (b * H1 + n) * TT + t + 1)
                        apart(dve, c)
                        nc.vector.tensor_tensor_reduce(masked[:, t % 2, :], c.pd[:, t % 2, :], by_query[:, t, :], 1.0, LEAST_MAX, ALU.add, ALU.max,
                                                       accum_out=mx[:, n % 4, t:t + 1]).then_inc(s_read, 1)
                    if n >= 2 * GH and n % GH == 3:
                        normalise(n // GH - 2)
                normalise(2)
                normalise(3)
                for n in range(2):
                    dve.wait_ge(y_full, 2 * b + n + 1)
                    xb = c.X[:, bass.ds(b * TT + 2 * n, 2), :].rearrange("p n d -> p (n d)")
                    nc.vector.tensor_tensor(xb, c.pd[:, 2 + n, :], xb, ALU.add).then_inc(y_read, 1)

        @block.tensor
        def _(pe):
            pe.sem_inc(st_full, 4 * GH)
            pe.sem_inc(pv_full, 2)
            pe.sem_inc(row_done, 1)
            pe.sem_inc(osum_done, 1)
            pe.sem_inc(exp_done, 2)
            pe.wait_ge(const, 6)
            pe.wait_ge(w_lo, 1)
            pe.wait_ge(mask_done, 3)
            with pe.Fori(0, B) as b:
                def by_query_scores(n):
                    g, i = n // GH, n % GH
                    if i == 0:
                        pe.wait_ge(qk_ins[g % 2], (b * 2 + g // 2 + 1) * QK_LOADS)
                    for t in range(TT):
                        pe.wait_ge(s_read, (b * H1 + n) * TT + t + 1)
                        nc.tensor.matmul(c.pd[:, t % 2, :], q4[:, g % 2, i, t * P:(t + 1) * P], k4[:, g % 2, i, :],
                                         start=True, stop=True).then_inc(s_full, 1)

                def max_row(n):
                    pe.wait_ge(s_read, (b * H1 + n) * TT + TT + 2)
                    pe.wait_ge(row_done, b * H1 + n + 1)
                    pe.wait_ge(sel_read, b * GROUPS + 1 + max(0, (n - 6) // GH))
                    pe.wait_ge(y_read, 2 * b + 2)
                    for t in range(TT):
                        last = nc.tensor.transpose(c.pd[0:1, 3, t * P:(t + 1) * P], mx[:, n % 4, t:t + 1], c.ident[:, :])
                    last.then_inc(row_full, 1)

                def by_key_scores(n):
                    g, i = n // GH, n % GH
                    pe.wait_ge(row_done, b * H1 + n + 2)
                    for half in range(2):
                        pe.wait_ge(exp_done, (b * H1 + n) * 2 + half + 1)
                        for t in (2 * half, 2 * half + 1):
                            nc.tensor.matmul(c.pa[:, t, :], k4[:, g % 2, i, t * P:(t + 1) * P], q4[:, g % 2, i, :], start=True, stop=False)
                            last = nc.tensor.matmul(c.pa[:, t, :], ident_bf[:, :], by_key[:, t, :], start=False, stop=True)
                        last.then_inc(st_full, 1)

                def values(g, t):
                    if t == 0:
                        if g == 0:
                            pe.wait_ge(v_in, b * DMA + DMA)
                        pe.wait_ge(exp_done, (b * H1 + (g + 1) * GH) * 2 + 2)
                        pe.wait_ge(osum_done, b * GROUPS + g + 1)
                    for i in range(GH):
                        last = nc.tensor.matmul(c.pd[i * R:(i + 1) * R, 2, :], V[:, t, g * GH + i, :], prob[:, g % 2, i, t, :],
                                                start=t == 0, stop=t == TT - 1, tile_position=(0, i * R))
                    if t == TT - 1:
                        last.then_inc(pv_full, 1)

                def spread_sums(g, n):
                    pe.wait_ge(osum_done, b * GROUPS + g + 2)
                    pe.wait_ge(row_done, b * H1 + n + 2)
                    pe.wait_ge(sel_read, b * GROUPS + g + 1)
                    nc.tensor.matmul(c.pd[:, 3, :], select[:, :], osum[:, g % 2, :], start=True, stop=True).then_inc(sel_full, 1)

                by_query_scores(0)
                by_query_scores(1)
                for n in range(H1):
                    max_row(n)
                    if n + 2 < H1:
                        by_query_scores(n + 2)
                    if n >= PV_LAG:
                        values((n - PV_LAG) // GH, (n - PV_LAG) % GH)
                    if n >= PV_LAG + GH and n % GH == PV_LAG % GH:
                        spread_sums((n - PV_LAG) // GH - 1, n)
                    by_key_scores(n)
                for m in range(H1 - PV_LAG, H1):
                    if m % GH == 0:
                        spread_sums(m // GH - 1, H1 - 1)
                    values(m // GH, m % GH)
                spread_sums(3, H1 - 1)
                pe.wait_ge(o_split, b * GROUPS + GROUPS + 2)
                for n in range(2):
                    for t in (2 * n, 2 * n + 1):
                        for k in range(GROUPS):
                            last = hi_lo(pe, nc, c.pd[:, 2 + n, (t % 2) * D:(t % 2 + 1) * D], [x[:, k, t * P:(t + 1) * P] for x in (oH, oL)],
                                         [x[:, k * D:(k + 1) * D] for x in (woH, woL)], k == 0, k == GROUPS - 1)
                    last.then_inc(y_full, 1)


def first_ffn_phase(nc, c):
    CHUNK = HID
    CHUNKS = 2 * KT + HT
    with ExitStack() as ctx:
        sb = lambda n, s, d=F32: ctx.enter_context(nc.sbuf_tensor(f"f_{n}", s, d))
        raw = sb("raw", [P, 2, CHUNK])
        wH = sb("wH", [P, CHUNKS, CHUNK], F32R)
        wL = sb("wL", [P, CHUNKS, CHUNK], F32R)
        scales = sb("scales", [P, 3, HT])
        gate = sb("gate", [P, 2, S])
        h_raw = sb("h_raw", [P, 2, S])
        hH = sb("hH", [P, HT, S], F32R)
        hL = sb("hL", [P, HT, S], F32R)
        hidden = sb("hidden", [P, 2, S])
        (w_in0, w_in1, scales_in, w_hi, w_lo, gate_full, gate_done, up_full, h_done, hi_done, split, hid_full, hid_done, stored0,
         stored1) = semaphores(nc, ctx, "f", "w_in0 w_in1 scales_in w_hi w_lo gate_full gate_done up_full h_done hi_done split hid_full "
                               "hid_done stored0 stored1")
        w_ins, stores = (w_in0, w_in1), (stored0, stored1)
        weight = lambda w, m: [x[:, w, m * P:(m + 1) * P] for x in (wH, wL)]
        block = ctx.enter_context(nc.Block())

        @block.sync
        def _(sp):
            sp.dma_start(scales[:, :, :], c.ins["ffn_scales"]).then_inc(scales_in, DMA)
            for n in range(CHUNKS):
                if n >= 2:
                    sp.wait_ge(w_lo, n - 1)
                sp.dma_start(raw[:, n % 2, :], c.ins["ffn_w"][n]).then_inc(w_ins[n % 2], DMA)
            with sp.Fori(0, B) as b:
                for m in range(HT):
                    sp.wait_ge(hid_done, b * HT + m + 1)
                    sp.dma_start(c.hidden_dram[bass.ds(b, 1), :, m, :].rearrange("o p t -> (o p) t"),
                                 hidden[:, m % 2, :]).then_inc(stores[m % 2], DMA)
            for done in stores:
                sp.wait_ge(done, (B * HT // 2 + 1) * DMA)

        @block.gpsimd
        def _(pool):
            pass

        @block.scalar
        def _(act):
            act.sem_inc(stored0, DMA)
            act.sem_inc(stored1, DMA)
            for n in range(CHUNKS):
                act.wait_ge(w_ins[n % 2], (n // 2 + 1) * DMA)
                nc.scalar.activation(wH[:, n, :], raw[:, n % 2, :], ACT.Copy).then_inc(w_hi, 1)
            act.wait_ge(scales_in, DMA)
            with act.Fori(0, B) as b:
                for m in range(HT):
                    act.wait_ge(gate_full, b * HT + m + 1)
                    act.wait_ge(h_done, b * HT + m + 1)
                    nc.scalar.activation(gate[:, m % 2, :], c.pa[:, m % 2, :], ACT.Silu, scale=scales[:, 0, m:m + 1]).then_inc(gate_done, 1)
                for m in range(HT):
                    act.wait_ge(hid_full, b * HT + m + 2)
                    act.wait_ge(stores[m % 2], (b * HT // 2 + m // 2 + 1) * DMA)
                    nc.scalar.activation(hidden[:, m % 2, :], c.pa[:, 2 + m % 2, :], ACT.Gelu, scale=scales[:, 2, m:m + 1]).then_inc(hid_done, 1)

        @block.vector
        def _(dve):
            dve.sem_inc(h_done, 2)
            dve.sem_inc(split, 2)
            for n in range(CHUNKS):
                dve.wait_ge(w_hi, n + 1)
                nc.vector.tensor_tensor(wL[:, n, :], raw[:, n % 2, :], wH[:, n, :].bitcast(F32), ALU.subtract).then_inc(w_lo, 1)
            dve.wait_ge(scales_in, DMA)
            with dve.Fori(0, B) as b:
                for m in range(HT):
                    dve.wait_ge(up_full, b * HT + m + 1)
                    dve.wait_ge(gate_done, b * HT + m + 1)
                    dve.wait_ge(split, b * HT + m + 1)
                    nc.vector.scalar_tensor_tensor(h_raw[:, m % 2, :], c.pd[:, m % 2, :], scales[:, 1, m:m + 1], gate[:, m % 2, :],
                                                   ALU.mult, ALU.mult).then_inc(h_done, 1)
                    dve.wait_ge(h_done, b * HT + m + 3)
                    if m == 0:
                        dve.wait_ge(hid_full, b * HT + 1)
                    nc.vector.tensor_copy(hH[:, m, :], h_raw[:, m % 2, :]).then_inc(hi_done, 1)
                    dve.wait_ge(hi_done, b * HT + m + 1)
                    nc.vector.tensor_tensor(hL[:, m, :], h_raw[:, m % 2, :], hH[:, m, :].bitcast(F32), ALU.subtract).then_inc(split, 1)

        @block.tensor
        def _(pe):
            pe.sem_inc(hid_full, 1)
            pe.wait_ge(w_lo, CHUNKS)
            with pe.Fori(0, B) as b:
                xn = lambda k: [x[:, k, bass.ds(b * S, S)] for x in (c.xnH, c.xnL)]
                for m in range(HT):
                    pe.wait_ge(h_done, b * HT + m + 1)
                    for k in range(KT):
                        last = hi_lo(pe, nc, c.pa[:, m % 2, :], weight(k, m), xn(k), k == 0, k == KT - 1)
                    last.then_inc(gate_full, 1)
                    for k in range(KT):
                        last = hi_lo(pe, nc, c.pd[:, m % 2, :], weight(KT + k, m), xn(k), k == 0, k == KT - 1)
                    last.then_inc(up_full, 1)
                for m in range(HT):
                    if m >= 2:
                        pe.wait_ge(hid_done, b * HT + m - 1)
                    for k in range(HT):
                        if m == 0:
                            pe.wait_ge(split, b * HT + k + 3)
                        last = hi_lo(pe, nc, c.pa[:, 2 + m % 2, :], weight(2 * KT + k, m), [x[:, k, :] for x in (hH, hL)], k == 0, k == HT - 1)
                    last.then_inc(hid_full, 1)


def second_ffn_phase(nc, c):
    CHUNK = HID
    CHUNKS = HT + 2
    with ExitStack() as ctx:
        sb = lambda n, s, d=F32: ctx.enter_context(nc.sbuf_tensor(f"g_{n}", s, d))
        raw = sb("raw", [P, 2, CHUNK])
        wH = sb("wH", [P, CHUNKS, CHUNK], F32R)
        wL = sb("wL", [P, CHUNKS, CHUNK], F32R)
        scales = sb("scales", [P, HT])
        out_scale = sb("out_scale", [P, 2, D])
        hidden = sb("hidden", [P, HT, S])
        hH = sb("hH", [P, HT, S], F32R)
        hL = sb("hL", [P, HT, S], F32R)
        z_raw = sb("z_raw", [P, 2, S])
        zH = sb("zH", [P, HT, S], F32R)
        zL = sb("zL", [P, HT, S], F32R)
        y = sb("y", [P, 2, 2, D])
        (w_in0, w_in1, scales_in, w_hi, w_lo, hid_in, hid_hi, hid_lo, z_full, z_done, z_hi, z_split, y_full, y_scaled, y_done,
         stored) = semaphores(nc, ctx, "g", "w_in0 w_in1 scales_in w_hi w_lo hid_in hid_hi hid_lo z_full z_done z_hi z_split y_full "
                              "y_scaled y_done stored")
        w_ins = (w_in0, w_in1)
        weight = lambda k, m: [x[:, k, m * P:(m + 1) * P] for x in (wH, wL)]
        w3 = lambda k: [x[:, HT + k // 4, (k % 4) * D:(k % 4 + 1) * D] for x in (wH, wL)]
        out_rows = c.out.rearrange("(b n p) d -> p (b n) d", p=P, n=TT)
        block = ctx.enter_context(nc.Block())

        @block.sync
        def _(sp):
            sp.dma_start(scales[:, :], c.ins["h2_s"]).then_inc(scales_in, DMA)
            for n in range(2):
                sp.dma_start(out_scale[:, n, :], c.ins["w3_s"].partition_broadcast(P)).then_inc(scales_in, DMA)
            for n in range(CHUNKS):
                if n >= 2:
                    sp.wait_ge(w_lo, n - 1)
                sp.dma_start(raw[:, n % 2, :], c.ins["ffn_w"][2 * KT + HT + n]).then_inc(w_ins[n % 2], DMA)
            with sp.Fori(0, B) as b:
                sp.wait_ge(hid_lo, b * HT + HT)
                sp.dma_start(hidden[:, :, :], c.hidden_dram[bass.ds(b, 1), :, :, :].rearrange("o p m t -> p (o m) t")).then_inc(hid_in, DMA)
            with sp.Fori(0, B) as b:
                sp.wait_ge(y_done, 2 * b + 2 + 2)
                sp.dma_start(out_rows[:, bass.ds(b * TT, TT), :], c.X[:, bass.ds(b * TT, TT), :]).then_inc(stored, DMA)
            sp.wait_ge(stored, B * DMA)

        @block.gpsimd
        def _(pool):
            pass

        @block.scalar
        def _(act):
            for n in range(CHUNKS):
                act.wait_ge(w_ins[n % 2], (n // 2 + 1) * DMA)
                nc.scalar.activation(wH[:, n, :], raw[:, n % 2, :], ACT.Copy).then_inc(w_hi, 1)
            act.wait_ge(scales_in, 3 * DMA)
            with act.Fori(0, B) as b:
                act.wait_ge(hid_in, b * DMA + DMA)
                act.wait_ge(z_full, b * HT + 2)
                for k in range(HT):
                    nc.scalar.activation(hH[:, k, :], hidden[:, k, :], ACT.Copy).then_inc(hid_hi, 1)
                for m in range(HT):
                    act.wait_ge(z_full, b * HT + m + 1 + 2)
                    act.wait_ge(z_split, b * HT + m + 1)
                    nc.scalar.activation(z_raw[:, m % 2, :], c.pa[:, m % 2, :], ACT.Gelu, scale=scales[:, m:m + 1]).then_inc(z_done, 1)

        @block.vector
        def _(dve):
            dve.sem_inc(hid_lo, HT)
            dve.sem_inc(z_split, 2)
            dve.sem_inc(y_done, 2)
            for n in range(CHUNKS):
                dve.wait_ge(w_hi, n + 1)
                nc.vector.tensor_tensor(wL[:, n, :], raw[:, n % 2, :], wH[:, n, :].bitcast(F32), ALU.subtract).then_inc(w_lo, 1)
            dve.wait_ge(scales_in, 3 * DMA)
            with dve.Fori(0, B) as b:
                for k in range(HT):
                    dve.wait_ge(hid_hi, b * HT + k + 1)
                    nc.vector.tensor_tensor(hL[:, k, :], hidden[:, k, :], hH[:, k, :].bitcast(F32), ALU.subtract).then_inc(hid_lo, 1)
                for m in range(HT):
                    dve.wait_ge(z_done, b * HT + m + 1 + 2)
                    nc.vector.tensor_copy(zH[:, m, :], z_raw[:, m % 2, :]).then_inc(z_hi, 1)
                    dve.wait_ge(z_hi, b * HT + m + 1)
                    nc.vector.tensor_tensor(zL[:, m, :], z_raw[:, m % 2, :], zH[:, m, :].bitcast(F32), ALU.subtract).then_inc(z_split, 1)
                for n in range(2):
                    dve.wait_ge(y_full, 2 * b + n + 1)
                    nc.vector.tensor_tensor(y[:, n, :, :], c.pd[:, n, :].rearrange("p (t d) -> p t d", d=D), out_scale[:, :, :],
                                            ALU.mult).then_inc(y_scaled, 1)
                    dve.wait_ge(y_scaled, 2 * b + n + 1)
                    xb = c.X[:, bass.ds(b * TT + 2 * n, 2), :]
                    nc.vector.tensor_tensor(xb, y[:, n, :, :], xb, ALU.add).then_inc(y_done, 1)

        @block.tensor
        def _(pe):
            pe.sem_inc(z_full, 2)
            pe.sem_inc(z_done, 2)
            pe.wait_ge(w_lo, CHUNKS)
            with pe.Fori(0, B) as b:
                for m in range(HT):
                    pe.wait_ge(z_done, b * HT + m + 1)
                    for k in range(HT):
                        if m == 0:
                            pe.wait_ge(hid_lo, b * HT + k + 1 + HT)
                        last = hi_lo(pe, nc, c.pa[:, m % 2, :], weight(k, m), [x[:, k, :] for x in (hH, hL)], k == 0, k == HT - 1)
                    last.then_inc(z_full, 1)
                pe.wait_ge(z_split, b * HT + HT + 2)
                for n in range(2):
                    pe.wait_ge(y_done, 2 * b + n + 1)
                    for t in (2 * n, 2 * n + 1):
                        for k in range(HT):
                            last = hi_lo(pe, nc, c.pd[:, n, (t % 2) * D:(t % 2 + 1) * D], [x[:, k, t * P:(t + 1) * P] for x in (zH, zL)],
                                         w3(k), k == 0, k == HT - 1)
                    last.then_inc(y_full, 1)


def build_program(nc, ins, out):
    c = Core()
    c.ins, c.out = ins, out
    c.q_dram = nc.dram_tensor("q_dram", (B, 2, D, S), F32).ap()
    c.k_dram = nc.dram_tensor("k_dram", (B, 2, D, S), F32).ap()
    c.v_dram = nc.dram_tensor("v_dram", (B, P, TT * H1 * 2 * DH1), F32).ap()
    c.rows_dram = nc.dram_tensor("rows_dram", (T, D), F32).ap()
    c.y_dram = nc.dram_tensor("y_dram", (BLOCKS * P, D), F32).ap()
    c.hidden_dram = nc.dram_tensor("hidden_dram", (B, P, HT, S), F32).ap()
    with ExitStack() as ctx:
        sb = lambda n, s, d=F32: ctx.enter_context(nc.sbuf_tensor(n, s, d))
        c.X = sb("X", [P, NT, D])
        c.ident = sb("ident", [P, P])
        c.bo = sb("bo", [P, D])
        c.pa = ctx.enter_context(nc.psum_tensor("pa", [P, 4, S], F32))
        c.pd = ctx.enter_context(nc.psum_tensor("pd", [P, 4, S], F32))
        c.ln_sems = semaphores(nc, ctx, "ln", "loaded const stat_done step var_done pow_done rstd_done xn_done tr_done hi_done lo_done")
        c.waited = ctx.enter_context(nc.semaphore("waited"))
        def normed(stack, part):
            c.xnH = stack.enter_context(nc.sbuf_tensor(f"xnH_{part}", [P, KT, T], F32R))
            c.xnL = stack.enter_context(nc.sbuf_tensor(f"xnL_{part}", [P, KT, T], F32R))

        with ExitStack() as stack:
            normed(stack, "a")
            layernorm_phase(nc, c, 0)
            first_attention_phase(nc, c)
        mixture_phase(nc, c)
        with ExitStack() as stack:
            normed(stack, "c")
            layernorm_phase(nc, c, 2)
            second_projection_phase(nc, c)
        second_attention_phase(nc, c)
        with ExitStack() as stack:
            normed(stack, "b")
            layernorm_phase(nc, c, 3)
            first_ffn_phase(nc, c)
        second_ffn_phase(nc, c)


def kernel(**inputs):
    import concourse.bacc as bacc
    from concourse.bass_utils import run_bass_kernel_spmd

    inp = {n: np.asarray(a) for n, a in inputs.items()}
    of = lambda part: {n[len(part):]: a for n, a in inp.items() if n.startswith(part)}
    a0, moe, a1, ffn = of("L0_xattn_"), of("L0_ffn_"), of("L1_xattn_"), of("L1_ffn_")

    def by_contraction(w):
        return w.reshape(-1, P, w.shape[1]).transpose(1, 0, 2).reshape(P, -1)

    def columns(v, *lead):
        return np.moveaxis(v.reshape(*lead, -1, P), -1, 0)

    mask = inp["mask_1x1xSxS2_bk1"].reshape(S, S)
    wo1 = np.zeros((GROUPS, GH, 2, DH1, D), np.float32)
    wo1[:, :, 0] = a1["Wo"].T.reshape(GROUPS, GH, DH1, D)
    expert = lambda e: np.concatenate([by_contraction(moe["fc1_w"][e].T), by_contraction(moe["fc2_w"][e].T)], 1)
    feature_tiles = lambda w: w.T.reshape(-1, P, HID)
    layout = {
        "x": inp["x"].reshape(T, D),
        "ctx": inp["ctx_1024"].reshape(T, KT, P).transpose(2, 1, 0),
        "bo": a0["bo"],
        "wq0": by_contraction(a0["Wq"]), "wk0": by_contraction(a0["Wk"]),
        "wv0": by_contraction(a0["Wv"]), "wo0": by_contraction(a0["Wo"]),
        "gate": by_contraction(np.concatenate([moe["gate_w"].T, np.zeros((D, 1), np.float32)], 1)),
        "b1row": moe["fc1_b"].reshape(-1), "mult": columns(moe["geglu_mult"], E),
        "sb1": columns(moe["s_fc1_b"]), "smult": columns(moe["s_geglu_mult"]),
        "b2": np.concatenate([moe["fc2_b"], moe["s_fc2_b"][None]], 0),
        "sw": np.concatenate([by_contraction(moe["s_fc1_w"].T), by_contraction(moe["s_fc2_w"].T)], 1),
        "ew": np.stack([expert(e) for e in range(E)]),
        "wq1": by_contraction(a1["Wq"].T), "wk1": by_contraction(a1["Wk"].T), "wv1": by_contraction(a1["Wv"].T),
        "wo1": by_contraction(wo1.reshape(-1, D)),
        "mask": mask, "maskT": mask.T,
        "ffn_w": np.concatenate([feature_tiles(ffn["w1_w"]), feature_tiles(ffn["w2_w"]), feature_tiles(ffn["h1_w"]),
                                 feature_tiles(ffn["h2_w"]),
                                 ffn["w3_w"].T.reshape(2, 4, P, D).transpose(0, 2, 1, 3).reshape(2, P, HID)], 0),
        "ffn_scales": np.stack([columns(ffn[n]) for n in ("w1_s", "w2_s", "h1_s")], 1),
        "h2_s": columns(ffn["h2_s"]), "w3_s": ffn["w3_s"],
    }
    arrays = {f"in_{n}": np.ascontiguousarray(a) for n, a in layout.items()}
    nc = bacc.Bacc("TRN2", target_bir_lowering=False, num_devices=1)
    ins = {n[3:]: nc.dram_tensor(n, a.shape, mybir.dt.from_np(a.dtype), kind="ExternalInput").ap() for n, a in arrays.items()}
    out = nc.dram_tensor("out", (T, D), F32, kind="ExternalOutput").ap()
    build_program(nc, ins, out)
    return run_bass_kernel_spmd(nc, [arrays], core_ids=[0]).results[0]["out"].reshape(B, S, D)
```

```python
from contextlib import ExitStack

import numpy as np

import concourse.bass as bass
from concourse import mybir
from concourse.alu_op_type import AluOpType as ALU

F32 = mybir.dt.float32
F32R = mybir.dt.float32r
BF16 = mybir.dt.bfloat16
U8 = mybir.dt.uint8
I32 = mybir.dt.int32
U32 = mybir.dt.uint32
ACT = mybir.ActivationFunctionType
AX = mybir.AxisListType

P = 128
B, S, D = 4, 512, 256
KT = D // P
TT = S // P
T = B * S
NT = T // P
LN_EPS = 1e-5

H0, DH0 = 8, 64
INNER = H0 * DH0
PAIRS = H0 // 2
H1, DH1 = 16, 16
GROUPS, GH = 4, 4
E, TOPK, F, FS = 15, 3, 256, 512
FT, FST = F // P, FS // P
BLOCKS = (TOPK * T + E * (P - 1)) // P
RING = 4
ROUNDS = -(-BLOCKS // RING)
LAST_ROUND = BLOCKS - (ROUNDS - 1) * RING
HID = 1024
HT = HID // P
MASKED = -1.0e30
LEAST_MAX = -1.0e29
DMA = 16


def hi_lo(pe, nc, out, stat, move, first, last):
    (sh, sl), (mh, ml) = stat, move
    nc.tensor.matmul(out, sh, ml, start=first, stop=False)
    nc.tensor.matmul(out, sl, mh, start=False, stop=False)
    return nc.tensor.matmul(out, sh, mh, start=False, stop=last)


class Core:
    pass


def apart(engine, c):
    engine.sem_inc(c.waited, 1)


def semaphores(nc, ctx, phase, names, reuse=False):
    if not reuse:
        return [ctx.enter_context(nc.semaphore(f"{phase}_{n}")) for n in names.split()]
    handles = [nc.alloc_semaphore(name=f"{phase}_{n}") for n in names.split()]

    def free():
        nc.clear_and_free_semaphores(handles)
        nc.all_engine_barrier()

    ctx.callback(free)
    return handles


def token_stats(nc, c, n):
    flat = lambda x: x[:, bass.ds(n, 1), :].rearrange("p o d -> p (o d)")
    return nc.vector.bn_stats(flat(c.stats), flat(c.X))


def layernorm_phase(nc, c, turn, prefetch=None, split_hi=None, split_lo=None, rows=None, xn=None):
    setup = turn == 0
    with ExitStack() as ctx:
        sb = lambda n, s, d=F32: ctx.enter_context(nc.sbuf_tensor(f"ln{turn}_{n}", s, d))
        stats = c.stats
        mean = sb("mean", [P, NT])
        diff = sb("diff", [P, NT])
        m2 = sb("m2", [P, NT])
        ve = sb("ve", [P, NT])
        y = sb("y", [P, NT])
        t1 = sb("t1", [P, NT])
        half = sb("half", [P, NT])
        rstd = sb("rstd", [P, NT])
        xn = sb("xn", [P, 2, TT, D]) if xn is None else xn
        (loaded, loaded2, const, stat_done, step, var_done, pow_done, rstd_done, xn_done, tr_done, hi_done, lo_done) = c.ln_sems
        CONST = 3 + turn
        before = turn * B
        block = ctx.enter_context(nc.Block())

        @block.sync
        def _(sp):
            if setup:
                for part, done in enumerate((loaded, loaded2)):
                    half_x = slice(part * NT // 2, (part + 1) * NT // 2)
                    sp.dma_start(c.X[:, half_x, :], c.ins["x"].rearrange("(n p) d -> p n d", p=P)[:, half_x, :]).then_inc(done, DMA)
            if prefetch:
                prefetch(sp)
            if rows:
                with sp.Fori(0, B // 2) as i:
                    for par in range(2):
                        sp.wait_ge(xn_done, i * 2 + par + before + 1)
                        sp.dma_start(rows[0].rearrange("(n p) d -> p n d", p=P)[:, bass.ds(i * 2 * TT + par * TT, TT), :],
                                     xn[:, par, :, :]).then_inc(rows[1][par], DMA)
                for par in range(2):
                    sp.wait_ge(rows[1][par], (B // 2 + 1) * DMA)

        @block.gpsimd
        def _(pool):
            if setup:
                nc.gpsimd.memset(c.ident[:, :], 0.0).then_inc(const, 1)
                pool.wait_ge(const, 1)
                nc.gpsimd.affine_select(out=c.ident[:, :], in_=c.ident[:, :], compare_op=ALU.not_equal, fill=1.0,
                                        base=0, pattern=[[-1, P]], channel_multiplier=1).then_inc(const, 1)
            nc.gpsimd.memset(half[:, :], -0.5).then_inc(const, 1)
            pool.wait_ge(const, CONST)
            pool.wait_ge(var_done, turn + 1)
            nc.gpsimd.tensor_tensor(y[:, :], ve[:, :], half[:, :], ALU.pow).then_inc(pow_done, 1)
            if split_lo:
                split_lo(pool)

        @block.vector
        def _(dve):
            if setup:
                for part, done in enumerate((loaded, loaded2)):
                    dve.wait_ge(done, DMA)
                    with dve.Fori(part * B // 2, (part + 1) * B // 2) as b:
                        for t in range(TT):
                            last = token_stats(nc, c, b * TT + t)
                        last.then_inc(stat_done, 1)
                dve.wait_ge(stat_done, B)
            tile = lambda n: c.X[:, bass.ds(n, 1), :].rearrange("p o d -> p (o d)")
            nc.vector.tensor_tensor(mean[:, :], stats[:, :, 1], stats[:, :, 4], ALU.add)
            nc.vector.tensor_tensor(diff[:, :], stats[:, :, 1], stats[:, :, 4], ALU.subtract)
            nc.vector.tensor_tensor(m2[:, :], stats[:, :, 2], stats[:, :, 5], ALU.add).then_inc(step, 1)
            dve.wait_ge(step, 5 * turn + 1)
            nc.vector.tensor_scalar(mean[:, :], mean[:, :], 0.5, None, ALU.mult)
            nc.vector.tensor_tensor(diff[:, :], diff[:, :], diff[:, :], ALU.mult).then_inc(step, 1)
            dve.wait_ge(step, 5 * turn + 2)
            nc.vector.scalar_tensor_tensor(m2[:, :], diff[:, :], D / 4.0, m2[:, :], ALU.mult, ALU.add).then_inc(step, 1)
            dve.wait_ge(step, 5 * turn + 3)
            nc.vector.tensor_scalar(ve[:, :], m2[:, :], 1.0 / D, LN_EPS, ALU.mult, ALU.add).then_inc(var_done, 1)
            dve.wait_ge(pow_done, turn + 1)
            nc.vector.scalar_tensor_tensor(t1[:, :], ve[:, :], -0.5, y[:, :], ALU.mult, ALU.mult).then_inc(step, 1)
            dve.wait_ge(step, 5 * turn + 4)
            nc.vector.tensor_tensor(t1[:, :], t1[:, :], y[:, :], ALU.mult).then_inc(step, 1)
            dve.wait_ge(step, 5 * turn + 5)
            nc.vector.scalar_tensor_tensor(rstd[:, :], t1[:, :], 1.5, y[:, :], ALU.add, ALU.mult).then_inc(rstd_done, 1)
            dve.wait_ge(rstd_done, turn + 1)
            if rows:
                for par in range(2):
                    dve.sem_inc(rows[1][par], DMA)

            def normalise(i, par):
                n = i * 2 + par
                if rows:
                    dve.wait_ge(rows[1][par], i * DMA + DMA)
                    apart(dve, c)
                for t in range(TT):
                    at = bass.ds(n * TT + t, 1)
                    last = nc.vector.tensor_scalar(xn[:, par, t, :], tile(n * TT + t), mean[:, at], rstd[:, at], ALU.subtract, ALU.mult)
                last.then_inc(xn_done, 1)

            def keep_lo(i, par):
                n = i * 2 + par
                for k in range(KT):
                    dve.wait_ge(hi_done, KT * (n + before) + k + 1)
                    tok = bass.ds(n * S, S)
                    nc.vector.tensor_tensor(c.xnL[:, k, tok], c.pd[:, 2 * par + k, :], c.xnH[:, k, tok].bitcast(F32),
                                            ALU.subtract).then_inc(lo_done, 1)

            for par in range(2):
                normalise(0, par)
            with dve.Fori(0, B // 2 - 1) as i:
                for par in range(2):
                    keep_lo(i, par)
                    normalise(i + 1, par)
            for par in range(2):
                keep_lo(B // 2 - 1, par)

        @block.tensor
        def _(pe):
            pe.wait_ge(const, CONST)
            with pe.Fori(0, B // 2) as i:
                for par in range(2):
                    pe.wait_ge(xn_done, i * 2 + par + before + 1)
                    for k in range(KT):
                        for t in range(TT):
                            last = nc.tensor.transpose(c.pd[:, 2 * par + k, t * P:(t + 1) * P], xn[:, par, t, k * P:(k + 1) * P], c.ident[:, :])
                        last.then_inc(tr_done, 1)

        @block.scalar
        def _(act):
            if split_hi:
                split_hi(act)
            with act.Fori(0, B // 2) as i:
                for par in range(2):
                    n = i * 2 + par
                    for k in range(KT):
                        act.wait_ge(tr_done, KT * (n + before) + k + 1)
                        apart(act, c)
                        nc.scalar.activation(c.xnH[:, k, bass.ds(n * S, S)], c.pd[:, 2 * par + k, :], ACT.Copy).then_inc(hi_done, 1)


def all_batches(engine, work):
    work(0, True, False)
    with engine.Fori(1, B - 1) as b:
        work(b, False, False)
    work(B - 1, False, True)


def first_attention_phase(nc, c):
    with ExitStack() as ctx:
        sb = lambda n, s, d=F32: ctx.enter_context(nc.sbuf_tensor(f"a_{n}", s, d))
        wH = sb("wH", [P, 4, KT * INNER], F32R)
        wL = sb("wL", [P, 4, KT * INNER], F32R)
        ctx_raw = sb("ctx_raw", [P, KT, S])
        ctxH = sb("ctxH", [P, KT, S], F32R)
        ctxL = sb("ctxL", [P, KT, S], F32R)
        V = sb("V", [P, TT, INNER])
        qHL = sb("qHL", [P, 2, 2, S], F32R)
        kHH = sb("kHH", [P, 2, 2, S], F32R)
        kL1 = sb("kL1", [P, 2, 2, S], F32R)
        qHM = sb("qHM", [P, 2, 2, S], F32R)
        mx = sb("mx", [P, 2, TT])
        prob = sb("prob", [P, 2, 2, TT, S])
        half_sum = sb("half_sum", [P, 2, S])
        prob_sum = sb("prob_sum", [P, 2, 2, S])
        ones = sb("ones", [P, DH0])
        inv = sb("inv", [P, S])
        o = sb("o", [P, 2, S])
        oH = sb("oH", [P, PAIRS, S], F32R)
        oL = sb("oL", [P, PAIRS, S], F32R)
        (w_hi, w_lo, const, ctx_in, ctx_hi, ctx_lo, work_full, work_read, q_hi, k_hi, copied, row_full, row_done, st_full,
         exp_done, add_half, add_done, pv_full, o_copied, den_full, den_read, inv_left, norm_step, o_split) = semaphores(
            nc, ctx, "a", "w_hi w_lo const ctx_in ctx_hi ctx_lo work_full work_read q_hi k_hi copied row_full row_done st_full "
            "exp_done add_half add_done pv_full o_copied den_full den_read inv_left norm_step o_split", reuse=True)
        w_ins = semaphores(nc, ctx, "a", "wq_in wk_in wv_in wo_in")
        bias_in, bias_done = semaphores(nc, ctx, "a", "bias_in bias_done")
        wq, wk, wv, wo = range(4)
        weight = lambda w, k, lo, n: [x[:, w, k * INNER + lo:k * INNER + lo + n] for x in (wH, wL)]
        wo_tile = lambda k: [x[:, wo, k * D:(k + 1) * D] for x in (wH, wL)]
        staged = lambda n: prob[:, n // 2, n % 2, 0:2, :].rearrange("p t s -> p (t s)")
        own = lambda h: slice(h * DH0, (h + 1) * DH0)
        other = lambda h: slice((1 - h) * DH0, (2 - h) * DH0)
        aux = lambda h: slice((1 - h) * DH0, (1 - h) * DH0 + 1)
        V_AT, WO_AT, CTX_AT = 1, 3, 5
        AHEAD = 2 + TT

        def uses(first):
            order = []
            for n in range(H0):
                if n == V_AT:
                    order += [("v", t) for t in range(TT)]
                order += [("s", n + 1, t) for t in range(TT)]
                if n % 2 == 0:
                    order += [("q", n // 2 + 1), ("k", n // 2 + 1)]
                if n == WO_AT and not first:
                    order += [("o", 0), ("o", 1)]
            return {what: at for at, what in enumerate(order)}

        WORK = len(uses(False))

        def use(b, first, *what):
            return AHEAD + uses(True)[what] if first else AHEAD - 2 + b * WORK + uses(False)[what]

        early = {("q", 0): 0, ("k", 0): 1, **{("s", 0, t): 2 + t for t in range(TT)}}
        bank = lambda what: c.pd[:, (early[what] if what in early else uses(False)[what]) % 2, :]

        def pair_before(b, j, by, first):
            return (b, j - by) if j >= by else None if first else (b - 1, j - by + PAIRS)

        def load_first(sp):
            sp.dma_start(c.bias[:, :], c.ins["bo"].partition_broadcast(P)).then_inc(bias_in, DMA)
            sp.dma_start(ctx_raw[:, :, :], c.ins["ctx"][:, :, 0:S]).then_inc(ctx_in, DMA)
            for n, name in enumerate(("wq0", "wk0", "wv0", "wo0")):
                sp.dma_start(staged(n), c.ins[name]).then_inc(w_ins[n], DMA)

        rows_room = prob[:, :, 0, 2:4, :].rearrange("p n t s -> p n (t s)").rearrange("p n (t d) -> p n t d", d=D)
        def context_hi(act, b):
            act.wait_ge(ctx_in, DMA * b + DMA)
            nc.scalar.activation(ctxH[:, :, :], ctx_raw[:, :, :], ACT.Copy).then_inc(ctx_hi, 1)

        def first_hi(act):
            context_hi(act, 0)
            for n in range(4):
                act.wait_ge(w_ins[n], DMA)
                nc.scalar.activation(wH[:, n, :], staged(n), ACT.Copy).then_inc(w_hi, 1)

        def first_lo(pool):
            pool.wait_ge(ctx_hi, 1)
            nc.gpsimd.tensor_tensor(ctxL[:, :, :], ctx_raw[:, :, :], ctxH[:, :, :].bitcast(F32), ALU.subtract).then_inc(ctx_lo, 1)
            for n in range(4):
                pool.wait_ge(w_hi, n + 1)
                nc.gpsimd.tensor_tensor(wL[:, n, :], staged(n), wH[:, n, :].bitcast(F32), ALU.subtract).then_inc(w_lo, 1)

        layernorm_phase(nc, c, 0, prefetch=load_first, split_hi=first_hi, split_lo=first_lo, xn=rows_room)
        block = ctx.enter_context(nc.Block())

        @block.sync
        def _(sp):
            with sp.Fori(1, B) as b:
                sp.wait_ge(ctx_lo, b)
                sp.dma_start(ctx_raw[:, :, :], c.ins["ctx"][:, :, bass.ds(b * S, S)]).then_inc(ctx_in, DMA)

        @block.gpsimd
        def _(pool):
            pool.sem_inc(add_done, 1)
            nc.gpsimd.memset(ones[:, :], 1.0).then_inc(const, 1)
            nc.gpsimd.memset(kL1[:, :, :, :].bitcast(F32), 0.0).then_inc(const, 1)
            nc.gpsimd.memset(qHM[:, :, :, :].bitcast(F32), 0.0).then_inc(const, 1)
            pool.wait_ge(const, 3)
            for h in range(2):
                nc.gpsimd.memset(kL1[aux(h), :, h, :].bitcast(F32), 1.0).then_inc(const, 1)
            pool.wait_ge(bias_in, DMA)
            pool.wait_ge(const, 5)
            with pool.Fori(0, B) as b:
                xb = c.X[:, bass.ds(b * TT, TT), :]
                nc.gpsimd.tensor_tensor(xb, xb, c.bias[:, :].unsqueeze(1).to_broadcast([P, TT, D]), ALU.add).then_inc(bias_done, 1)

            with pool.Fori(0, B) as b:
                for j in range(PAIRS):
                    for h in range(2):
                        head = (b * PAIRS + j) * 2 + h
                        pool.wait_ge(exp_done, head * 2 + 3)
                        pool.wait_ge(add_done, head + 1)
                        nc.gpsimd.tensor_tensor(half_sum[:, :, :], prob[:, j % 2, h, 0:2, :], prob[:, j % 2, h, 2:4, :],
                                                ALU.add).then_inc(add_half, 1)
                        pool.wait_ge(add_half, head + 1)
                        nc.gpsimd.tensor_tensor(prob_sum[:, j % 2, h, :], half_sum[:, 0, :], half_sum[:, 1, :],
                                                ALU.add).then_inc(add_done, 1)

        @block.scalar
        def _(act):
            act.sem_inc(exp_done, 1)
            def queries_hi(at, pair, j):
                act.wait_ge(work_full, at + 1)
                for h in range(2):
                    last = nc.scalar.activation(qHL[own(h), j % 2, h, :], bank(("q", j))[own(h), :], ACT.Copy)
                last.then_inc(q_hi, 1)
                act.wait_ge(q_hi, pair + 1)
                for h in range(2):
                    last = nc.scalar.activation(qHM[own(h), j % 2, h, :], qHL[own(h), j % 2, h, :].bitcast(F32), ACT.Copy)
                last.then_inc(copied, 1)

            def keys_hi(at, pair, j):
                act.wait_ge(work_full, at + 1)
                for h in range(2):
                    last = nc.scalar.activation(kHH[own(h), j % 2, h, :], bank(("k", j))[own(h), :], ACT.Copy)
                last.then_inc(k_hi, 1)
                act.wait_ge(k_hi, pair + 1)
                for h in range(2):
                    last = nc.scalar.activation(kHH[other(h), j % 2, h, :], kHH[own(h), j % 2, h, :].bitcast(F32), ACT.Copy)
                last.then_inc(copied, 1)

            act.wait_ge(const, 5)
            queries_hi(early["q", 0], 0, 0)
            keys_hi(early["k", 0], 0, 0)

            def batch(b, first, last):
                for n in range(H0):
                    j, h = n // 2, n % 2
                    N = b * H0 + n
                    act.wait_ge(row_full, N + 1)
                    nc.scalar.activation(qHM[aux(h), j % 2, h, :], c.pa[0:1, 0, :], ACT.Copy, scale=-1.0).then_inc(row_done, 1)
                    before = pair_before(b, j, 1, first)
                    if h == 1 and before:
                        G = before[0] * PAIRS + before[1]
                        act.wait_ge(pv_full, G + 1)
                        act.wait_ge(o_split, G + 1)
                        nc.scalar.activation(o[:, before[1] % 2, :], c.pd[:, 2, :], ACT.Copy).then_inc(o_copied, 1)
                    for half in range(2):
                        act.wait_ge(st_full, N * 2 + half + 1)
                        act.wait_ge(den_full, b * PAIRS + j + 1)
                        nc.scalar.activation(prob[:, j % 2, h, 2 * half:2 * half + 2, :], c.pa[:, 2 * half:2 * half + 2, :], ACT.Exp,
                                             scale=DH0 ** -0.5).then_inc(exp_done, 1)
                        if h == 0 and not (last and j == PAIRS - 1):
                            if half == 0:
                                queries_hi(use(b, first, "q", j + 1), b * PAIRS + j + 1, j + 1)
                            else:
                                keys_hi(use(b, first, "k", j + 1), b * PAIRS + j + 1, j + 1)
                    if n == CTX_AT and not last:
                        context_hi(act, b + 1)
                if last:
                    G = b * PAIRS + PAIRS - 1
                    act.wait_ge(pv_full, G + 1)
                    act.wait_ge(o_split, G + 1)
                    nc.scalar.activation(o[:, 1, :], c.pd[:, 2, :], ACT.Copy).then_inc(o_copied, 1)

            all_batches(act, batch)

        @block.vector
        def _(dve):
            dve.sem_inc(work_read, 2)
            dve.sem_inc(o_split, 2)
            dve.sem_inc(den_read, 1)
            dve.sem_inc(o_copied, 1)
            def context_lo(b):
                dve.wait_ge(ctx_hi, b + 1)
                nc.vector.tensor_tensor(ctxL[:, :, :], ctx_raw[:, :, :], ctxH[:, :, :].bitcast(F32), ALU.subtract).then_inc(ctx_lo, 1)

            def queries_lo(pair, j):
                dve.wait_ge(q_hi, pair + 1)
                for h in range(2):
                    last = nc.vector.tensor_tensor(qHL[other(h), j % 2, h, :], bank(("q", j))[own(h), :],
                                                   qHL[own(h), j % 2, h, :].bitcast(F32), ALU.subtract)
                last.then_inc(work_read, 1)

            def keys_lo(pair, j):
                dve.wait_ge(k_hi, pair + 1)
                for h in range(2):
                    last = nc.vector.tensor_tensor(kL1[own(h), j % 2, h, :], bank(("k", j))[own(h), :],
                                                   kHH[own(h), j % 2, h, :].bitcast(F32), ALU.subtract)
                last.then_inc(work_read, 1)

            def maxima(at, n):
                for t in range(TT):
                    dve.wait_ge(work_full, at + t + 1)
                    nc.vector.reduce_max(mx[:, n % 2, t:t + 1], bank(("s", n, t)), AX.X).then_inc(work_read, 1)

            def invert(b, j, right):
                G = b * PAIRS + j
                part = slice(right * (S // 2), (right + 1) * (S // 2))
                if not right:
                    dve.wait_ge(den_full, G + 3)
                    dve.wait_ge(o_split, G + 2)
                nc.vector.reciprocal(inv[:, part], c.pd[:, 3, part]).then_inc(den_read if right else inv_left, 1)

            def normalise(b, j):
                G = b * PAIRS + j
                dve.wait_ge(inv_left, G + 1)
                dve.wait_ge(den_read, G + 2)
                dve.wait_ge(o_copied, G + 2)
                nc.vector.tensor_tensor(o[:, j % 2, :], o[:, j % 2, :], inv[:, :], ALU.mult).then_inc(norm_step, 1)
                dve.wait_ge(norm_step, 2 * G + 1)
                nc.vector.tensor_copy(oH[:, j, :], o[:, j % 2, :]).then_inc(norm_step, 1)
                dve.wait_ge(norm_step, 2 * G + 2)
                nc.vector.tensor_tensor(oL[:, j, :], o[:, j % 2, :], oH[:, j, :].bitcast(F32), ALU.subtract).then_inc(o_split, 1)

            def add_output(b, n, at, source):
                dve.wait_ge(work_full, at + 1)
                dve.wait_ge(bias_done, B)
                xb = c.X[:, bass.ds(b * TT + 2 * n, 2), :].rearrange("p n d -> p (n d)")
                nc.vector.tensor_tensor(xb, source, xb, ALU.add).then_inc(work_read, 1)
                dve.wait_ge(work_read, at + 3)
                apart(dve, c)
                for t in (2 * n, 2 * n + 1):
                    token_stats(nc, c, b * TT + t)

            queries_lo(0, 0)
            keys_lo(0, 0)
            maxima(early["s", 0, 0], 0)

            def batch(b, first, last):
                for n in range(H0):
                    j, h = n // 2, n % 2
                    if n == WO_AT + 1 and not first:
                        for m in range(2):
                            add_output(b - 1, m, use(b, first, "o", m), bank(("o", m)))
                    if n == V_AT:
                        for t in range(TT):
                            dve.wait_ge(work_full, use(b, first, "v", t) + 1)
                            nc.vector.tensor_copy(V[:, t, :], bank(("v", t))).then_inc(work_read, 1)
                    if not (last and n == H0 - 1):
                        maxima(use(b, first, "s", n + 1, 0), n + 1)
                    before = pair_before(b, j, 2, first)
                    ahead = h == 0 and not (last and j == PAIRS - 1)
                    if h == 0 and before:
                        invert(*before, False)
                        invert(*before, True)
                    if ahead:
                        queries_lo(b * PAIRS + j + 1, j + 1)
                        keys_lo(b * PAIRS + j + 1, j + 1)
                    if h == 1 and before:
                        normalise(*before)
                    if n == CTX_AT and not last:
                        context_lo(b + 1)
                if last:
                    for j in (PAIRS - 2, PAIRS - 1):
                        invert(b, j, False)
                        invert(b, j, True)
                        normalise(b, j)
                    for m in range(2):
                        add_output(b, m, use(b, first, "s", H0, 0) - 2 + m, c.pd[:, m, :])

            all_batches(dve, batch)

        @block.tensor
        def _(pe):
            pe.sem_inc(den_full, 2)
            pe.wait_ge(w_lo, 4)
            pe.wait_ge(const, 5)
            pe.wait_ge(ctx_lo, 1)

            def project(b, at, kind, j):
                pe.wait_ge(work_read, at + 1)
                if kind == "k":
                    pe.wait_ge(ctx_lo, b + 1)
                for k in range(KT):
                    move = [x[:, k, bass.ds(b * S, S)] for x in (c.xnH, c.xnL)] if kind == "q" else [x[:, k, :] for x in (ctxH, ctxL)]
                    last = hi_lo(pe, nc, bank((kind, j)), weight(wq if kind == "q" else wk, k, j % PAIRS * P, P), move, k == 0, k == KT - 1)
                last.then_inc(work_full, 1)

            def by_query_scores(at, n, tiles, keys=None):
                if keys is not None:
                    pe.wait_ge(copied, keys[0] * 2 + 2)
                    pe.wait_ge(work_read, keys[1] + 3)
                j, h = n // 2, n % 2
                for t in tiles:
                    pe.wait_ge(work_read, at + t + 1)
                    nc.tensor.matmul(bank(("s", n, t)), qHL[:, j % 2, h, t * P:(t + 1) * P], kHH[:, j % 2, h, :],
                                     start=True, stop=True).then_inc(work_full, 1)

            def max_row(N, at, n):
                pe.wait_ge(work_read, at + TT + 2)
                if not (isinstance(N, int) and N == 0):
                    pe.wait_ge(exp_done, 2 * N)
                for t in range(TT):
                    last = nc.tensor.transpose(c.pa[0:1, 0, t * P:(t + 1) * P], mx[:, n % 2, t:t + 1], c.ident[:, :])
                last.then_inc(row_full, 1)

            def by_key_scores(N, n, half):
                j, h = n // 2, n % 2
                if half == 0:
                    pe.wait_ge(row_done, N + 1)
                else:
                    pe.wait_ge(exp_done, 2 * N + 1)
                for k in (2 * half, 2 * half + 1):
                    nc.tensor.matmul(c.pa[:, k, :], kHH[:, j % 2, h, k * P:(k + 1) * P], qHL[:, j % 2, h, :], start=True, stop=False)
                    last = nc.tensor.matmul(c.pa[:, k, :], kL1[:, j % 2, h, k * P:(k + 1) * P], qHM[:, j % 2, h, :],
                                            start=False, stop=True)
                last.then_inc(st_full, 1)

            def weigh_values(b, j, k, values=None):
                G = b * PAIRS + j
                if k == 0:
                    if values is not None:
                        pe.wait_ge(work_read, values + 3)
                    pe.wait_ge(o_copied, G + 1)
                    pe.wait_ge(exp_done, G * 4 + 5)
                for h in range(2):
                    head = 2 * j + h
                    last = nc.tensor.matmul(c.pd[own(h), 2, :], V[:, k, head * DH0:(head + 1) * DH0], prob[:, j % 2, h, k, :],
                                            start=k == 0, stop=k == TT - 1)
                if k == TT - 1:
                    last.then_inc(pv_full, 1)

            def denominators(b, j):
                G = b * PAIRS + j
                pe.wait_ge(add_done, G * 2 + 3)
                pe.wait_ge(den_read, G + 1)
                for h in range(2):
                    last = nc.tensor.matmul(c.pd[own(h), 3, :], ones[:, :], prob_sum[:, j % 2, h, :], start=True, stop=True)
                last.then_inc(den_full, 1)

            def output(b, n, at, out):
                pe.wait_ge(work_read, at + 1)
                pe.wait_ge(o_split, b * PAIRS + PAIRS + 2)
                for t in (2 * n, 2 * n + 1):
                    for k in range(PAIRS):
                        last = hi_lo(pe, nc, out[:, (t % 2) * D:(t % 2 + 1) * D], [x[:, k, t * P:(t + 1) * P] for x in (oH, oL)],
                                     wo_tile(k), k == 0, k == PAIRS - 1)
                last.then_inc(work_full, 1)

            project(0, early["q", 0], "q", 0)
            project(0, early["k", 0], "k", 0)
            by_query_scores(early["s", 0, 0], 0, range(TT), (0, early["k", 0]))
            max_row(0, early["s", 0, 0], 0)

            def batch(b, first, last):
                for n in range(H0):
                    j, h = n // 2, n % 2
                    N = b * H0 + n
                    before = pair_before(b, j, 1, first)
                    next_head = not (last and n == H0 - 1)
                    next_pair = h == 0 and not (last and j == PAIRS - 1)
                    to = b if j + 1 < PAIRS else b + 1
                    scores = use(b, first, "s", n + 1, 0)
                    values = use(b, first, "v", TT - 1) if before and before[1] == 0 else None
                    if h == 1 and before:
                        weigh_values(*before, 2)
                        weigh_values(*before, 3)
                    if n == V_AT:
                        for t in range(TT):
                            pe.wait_ge(work_read, use(b, first, "v", t) + 1)
                            for k in range(KT):
                                ready = hi_lo(pe, nc, bank(("v", t)), [x[:, k, t * P:(t + 1) * P] for x in (ctxH, ctxL)],
                                              weight(wv, k, 0, INNER), k == 0, k == KT - 1)
                            ready.then_inc(work_full, 1)
                    if next_head:
                        by_query_scores(scores, n + 1, (0, 1), (b * PAIRS + j + 1, use(b, first, "k", j + 1)) if h == 1 else None)
                    by_key_scores(N, n, 0)
                    if next_head:
                        by_query_scores(scores, n + 1, (2, 3))
                    if next_pair:
                        project(to, use(b, first, "q", j + 1), "q", j + 1)
                    if h == 0 and before:
                        weigh_values(*before, 0, values)
                    by_key_scores(N, n, 1)
                    if next_pair:
                        project(to, use(b, first, "k", j + 1), "k", j + 1)
                    if h == 0 and before:
                        weigh_values(*before, 1)
                    if next_head:
                        max_row(N + 1, scores, n + 1)
                    if h == 1 and before:
                        denominators(*before)
                    if n == WO_AT and not first:
                        for m in range(2):
                            output(b - 1, m, use(b, first, "o", m), bank(("o", m)))
                if last:
                    for k in range(TT):
                        weigh_values(b, PAIRS - 1, k)
                    denominators(b, PAIRS - 1)
                    for m in range(2):
                        output(b, m, use(b, first, "s", H0, 0) - 2 + m, c.pd[:, m, :])


            all_batches(pe, batch)


def mixture_phase(nc, c):
    EP = E + 1
    W1, W2 = KT * 2 * F, FT * D
    with ExitStack() as ctx:
        weights = ctx.enter_context(nc.sbuf_tensor("m_weights", [P, E, W1 + W2], F32))
        (w_loaded, rows_stored0, rows_stored1) = semaphores(nc, ctx, "m", "w_loaded rows_stored0 rows_stored1")

        sb = lambda n, s, d=F32: ctx.enter_context(nc.sbuf_tensor(f"m_{n}", s, d))
        SW = KT * 2 * FS + FST * D
        gate_raw = sb("gate_raw", [P, KT * EP])
        gateH = sb("gateH", [P, KT * EP], F32R)
        gateL = sb("gateL", [P, KT * EP], F32R)
        mult = sb("mult", [P, E, FT])
        sb1 = sb("sb1", [P, 2 * FST])
        smult = sb("smult", [P, FST])
        before = sb("before", [P, E, E])
        rank = sb("rank", [P, NT, E])
        comb = sb("comb", [P, NT, E])
        (w_in, gate_hi, gate_lo, const) = semaphores(nc, ctx, "m", "w_in gate_hi gate_lo const")

        with ExitStack() as inner:
            c.xnH = inner.enter_context(nc.sbuf_tensor("m_xnH", [P, KT, T], F32R))
            c.xnL = inner.enter_context(nc.sbuf_tensor("m_xnL", [P, KT, T], F32R))
            sb = lambda n, s, d=F32: inner.enter_context(nc.sbuf_tensor(f"ms_{n}", s, d))
            wH = sb("wH", [P, SW], F32R)
            wL = sb("wL", [P, SW], F32R)
            logT = sb("logT", [EP, S])
            lg = sb("lg", [P, TT, EP])
            peak = sb("peak", [P, TT])
            ex = sb("ex", [P, TT, EP])
            tot = sb("tot", [P, TT])
            score = sb("score", [P, TT, E])
            gt = sb("gt", [P, TT, E * E], BF16)
            eq = sb("eq", [P, TT, E * E], BF16)
            best = sb("best", [P, TT, E])
            gl = sb("gl", [P, 2, S])
            up = sb("up", [P, 2, S])
            aH = sb("aH", [P, FST, S], F32R)
            aL = sb("aL", [P, FST, S], F32R)
            (sw_in0, sw_in1, sw_in2, bias_in, bias_done, sw_hi, sw_lo, log_full, log_copied, logtok_full, shifted, exp_done, step, comb_done,
             g_full, g_done, x_full, x_read, araw_done, hi_done, a_split, y_full, y_read) = semaphores(
                nc, inner, "ms", "sw_in0 sw_in1 sw_in2 bias_in bias_done sw_hi sw_lo log_full log_copied logtok_full shifted exp_done step comb_done "
                "g_full g_done x_full x_read araw_done hi_done a_split y_full y_read")
            up_w = lambda m, k: [x[:, k * 2 * FS + m * P:k * 2 * FS + (m + 1) * P] for x in (wH, wL)]
            down_w = lambda k: [x[:, KT * 2 * FS + k * D:KT * 2 * FS + (k + 1) * D] for x in (wH, wL)]
            STEPS = 13
            PARTS = 3
            part = lambda n: slice(n * SW // PARTS, (n + 1) * SW // PARTS)
            staged = weights[:, 0:SW // (W1 + W2), :].rearrange("p e f -> p (e f)")
            sw_ins = (sw_in0, sw_in1, sw_in2)

            def load_first(sp):
                for dst, name in ((gate_raw[:, :], "gate"), (mult[:, :, :], "mult"), (sb1[:, :], "sb1"), (smult[:, :], "smult")):
                    sp.dma_start(dst, c.ins[name]).then_inc(w_in, DMA)
                for n in range(PARTS):
                    sp.dma_start(staged[:, part(n)], c.ins["sw"][:, part(n)]).then_inc(sw_ins[n], DMA)
                sp.dma_start(c.bias[:, :], c.ins["s_b2"].partition_broadcast(P)).then_inc(bias_in, DMA)

            def weights_hi(act):
                act.wait_ge(w_in, 4 * DMA)
                nc.scalar.activation(gateH[:, :], gate_raw[:, :], ACT.Copy).then_inc(gate_hi, 1)
                for n in range(PARTS):
                    act.wait_ge(sw_ins[n], DMA)
                    nc.scalar.activation(wH[:, part(n)], staged[:, part(n)], ACT.Copy).then_inc(sw_hi, 1)

            def weights_lo(pool):
                pool.wait_ge(gate_hi, 1)
                nc.gpsimd.tensor_tensor(gateL[:, :], gate_raw[:, :], gateH[:, :].bitcast(F32), ALU.subtract).then_inc(gate_lo, 1)
                for n in range(PARTS):
                    pool.wait_ge(sw_hi, n + 1)
                    nc.gpsimd.tensor_tensor(wL[:, part(n)], staged[:, part(n)], wH[:, part(n)].bitcast(F32), ALU.subtract).then_inc(sw_lo, 1)

            def load_experts(sp):
                for e in range(E):
                    sp.dma_start(weights[:, e, :], c.ins["ew"][e]).then_inc(w_loaded, DMA)

            layernorm_phase(nc, c, 1, prefetch=load_first, split_hi=weights_hi, split_lo=weights_lo,
                            rows=(c.rows_dram, (rows_stored0, rows_stored1)))
            block = inner.enter_context(nc.Block())

            @block.sync
            def _(sp):
                sp.wait_ge(sw_lo, PARTS)
                load_experts(sp)

            @block.gpsimd
            def _(pool):
                nc.gpsimd.memset(before[:, :, :], 1.0).then_inc(const, 1)
                pool.wait_ge(const, 1)
                nc.gpsimd.affine_select(out=before[:, :, :], in_=before[:, :, :], compare_op=ALU.is_gt, fill=0.0, base=0,
                                        pattern=[[1, E], [-1, E]], channel_multiplier=0).then_inc(const, 1)
                pool.wait_ge(bias_in, DMA)
                pool.wait_ge(const, 2)
                with pool.Fori(0, B) as b:
                    xb = c.X[:, bass.ds(b * TT, TT), :]
                    nc.gpsimd.tensor_tensor(xb, xb, c.bias[:, :].unsqueeze(1).to_broadcast([P, TT, D]), ALU.add).then_inc(bias_done, 1)

            @block.scalar
            def _(act):
                act.sem_inc(g_done, 2)

                def copy_logits(b):
                    act.wait_ge(log_full, b + 1)
                    nc.scalar.activation(logT[:, :], c.pd[0:EP, 0, :], ACT.Copy).then_inc(log_copied, 1)

                def batch(b, first, last):
                    if first:
                        copy_logits(b)

                    def keep_hi(m):
                        act.wait_ge(araw_done, b * FST + m + 1)
                        nc.scalar.activation(aH[:, m, :], up[:, m % 2, :], ACT.Copy).then_inc(hi_done, 1)

                    for m in range(FST):
                        act.wait_ge(g_full, b * FST + m + 1)
                        nc.scalar.activation(gl[:, m % 2, :], c.pa[:, m % 2, :], ACT.Gelu,
                                             bias=sb1[:, FST + m:FST + m + 1]).then_inc(g_done, 1)
                        if m:
                            keep_hi(m - 1)
                    keep_hi(FST - 1)
                    if not last:
                        copy_logits(b + 1)
                    act.wait_ge(shifted, b + 1)
                    nc.scalar.activation(ex[:, :, :], lg[:, :, :], ACT.Exp).then_inc(exp_done, 1)

                all_batches(act, batch)

            @block.vector
            def _(dve):
                dve.sem_inc(x_read, 2)
                dve.sem_inc(a_split, 2)
                dve.sem_inc(y_read, 2)
                dve.wait_ge(const, 2)
                with dve.Fori(0, B) as b:
                    def shift_logits():
                        dve.wait_ge(logtok_full, b + 1)
                        nc.vector.reduce_max(peak[:, :], c.pd[:, 1, 0:TT * EP].rearrange("p (t e) -> p t e", e=EP)[:, :, 0:E], AX.X).then_inc(step, 1)
                        dve.wait_ge(step, STEPS * b + 1)
                        nc.vector.tensor_tensor(lg[:, :, :], c.pd[:, 1, 0:TT * EP].rearrange("p (t e) -> p t e", e=EP),
                                                peak[:, :].unsqueeze(2).to_broadcast([P, TT, EP]), ALU.subtract).then_inc(shifted, 1)

                    def keep_lo(m):
                        dve.wait_ge(hi_done, b * FST + m + 1)
                        nc.vector.tensor_tensor(aL[:, m, :], up[:, m % 2, :], aH[:, m, :].bitcast(F32), ALU.subtract).then_inc(a_split, 1)

                    for m in range(FST):
                        dve.wait_ge(x_full, b * FST + m + 1)
                        dve.wait_ge(a_split, b * FST + m + 1)
                        nc.vector.tensor_scalar(up[:, m % 2, :], c.pd[:, 2 + m % 2, :], sb1[:, m:m + 1], smult[:, m:m + 1],
                                                ALU.add, ALU.mult).then_inc(x_read, 1)
                        dve.wait_ge(x_read, b * FST + m + 3)
                        dve.wait_ge(g_done, b * FST + m + 1 + 2)
                        nc.vector.tensor_tensor(up[:, m % 2, :], up[:, m % 2, :], gl[:, m % 2, :], ALU.mult).then_inc(araw_done, 1)
                        if m:
                            keep_lo(m - 1)
                        if m == 0:
                            shift_logits()
                    keep_lo(FST - 1)
                    dve.wait_ge(exp_done, b + 1)
                    nc.vector.reduce_sum(tot[:, :], ex[:, :, 0:E], AX.X).then_inc(step, 1)
                    dve.wait_ge(step, STEPS * b + 2)
                    nc.vector.reciprocal(tot[:, :], tot[:, :]).then_inc(step, 1)
                    dve.wait_ge(step, STEPS * b + 3)
                    nc.vector.tensor_tensor(score[:, :, :], ex[:, :, 0:E], tot[:, :].unsqueeze(2).to_broadcast([P, TT, E]),
                                            ALU.mult).then_inc(step, 1)
                    dve.wait_ge(step, STEPS * b + 4)
                    for t in range(TT):
                        others = score[:, t, :].unsqueeze(1).to_broadcast([P, E, E])
                        own = score[:, t, :].unsqueeze(2).to_broadcast([P, E, E])
                        nc.vector.tensor_tensor(gt[:, t, :].rearrange("p (e f) -> p e f", f=E), others, own, ALU.is_gt)
                        last = nc.vector.tensor_tensor(eq[:, t, :].rearrange("p (e f) -> p e f", f=E), others, own, ALU.is_equal)
                    last.then_inc(step, 1)
                    for n in range(2):
                        dve.wait_ge(y_full, 2 * b + n + 1)
                        dve.wait_ge(bias_done, B)
                        xb = c.X[:, bass.ds(b * TT + 2 * n, 2), :].rearrange("p n d -> p (n d)")
                        nc.vector.tensor_tensor(xb, c.pa[:, 2 + n, :], xb, ALU.add).then_inc(y_read, 1)
                    dve.wait_ge(step, STEPS * b + 5)
                    nc.vector.tensor_tensor(eq[:, :, :], eq[:, :, :], before[:, :, :].rearrange("p e f -> p (e f)").unsqueeze(1)
                                            .to_broadcast([P, TT, E * E]), ALU.mult).then_inc(step, 1)
                    dve.wait_ge(step, STEPS * b + 6)
                    nc.vector.tensor_tensor(gt[:, :, :], gt[:, :, :], eq[:, :, :], ALU.add).then_inc(step, 1)
                    dve.wait_ge(step, STEPS * b + 7)
                    rank_b = rank[:, bass.ds(b * TT, TT), :]
                    apart(dve, c)
                    nc.vector.reduce_sum(rank_b.rearrange("p t e -> p (t e)"),
                                         gt[:, :, :].rearrange("p t (e f) -> p (t e) f", f=E), AX.X).then_inc(step, 1)
                    dve.wait_ge(step, STEPS * b + 8)
                    nc.vector.scalar_tensor_tensor(best[:, :, :], rank_b, TOPK - 0.5, score[:, :, :], ALU.is_lt, ALU.mult).then_inc(step, 1)
                    dve.wait_ge(step, STEPS * b + 9)
                    nc.vector.reduce_sum(tot[:, :], best[:, :, :], AX.X).then_inc(step, 1)
                    dve.wait_ge(step, STEPS * b + 10)
                    nc.vector.tensor_scalar(tot[:, :], tot[:, :], 1e-20, None, ALU.add).then_inc(step, 1)
                    dve.wait_ge(step, STEPS * b + 11)
                    nc.vector.reciprocal(tot[:, :], tot[:, :]).then_inc(step, 1)
                    dve.wait_ge(step, STEPS * b + 12)
                    nc.vector.tensor_tensor(best[:, :, :], best[:, :, :], tot[:, :].unsqueeze(2).to_broadcast([P, TT, E]),
                                            ALU.mult).then_inc(comb_done, 1)
                    dve.wait_ge(comb_done, b + 1)
                    apart(dve, c)
                    nc.vector.tensor_copy(comb[:, bass.ds(b * TT, TT), :], best[:, :, :]).then_inc(step, 1)

            @block.tensor
            def _(pe):
                pe.wait_ge(gate_lo, 1)
                pe.wait_ge(sw_lo, PARTS)
                xn = lambda b, k: [x[:, k, bass.ds(b * S, S)] for x in (c.xnH, c.xnL)]

                def logits(b, first):
                    if not first:
                        pe.wait_ge(shifted, b)
                    for k in range(KT):
                        last = hi_lo(pe, nc, c.pd[0:EP, 0, :], [x[:, k * EP:(k + 1) * EP] for x in (gateH, gateL)], xn(b, k),
                                     k == 0, k == KT - 1)
                    last.then_inc(log_full, 1)

                def turn_logits(b):
                    pe.wait_ge(log_copied, b + 1)
                    apart(pe, c)
                    for t in range(TT):
                        last = nc.tensor.transpose(c.pd[:, 1, t * EP:(t + 1) * EP], logT[:, t * P:(t + 1) * P], c.ident[0:EP, 0:EP])
                    last.then_inc(logtok_full, 1)

                def batch(b, first, last):
                    if first:
                        logits(b, True)
                        turn_logits(b)
                    for m in range(FST):
                        pe.wait_ge(g_done, b * FST + m + 1)
                        for k in range(KT):
                            done = hi_lo(pe, nc, c.pa[:, m % 2, :], up_w(FST + m, k), xn(b, k), k == 0, k == KT - 1)
                        done.then_inc(g_full, 1)
                        pe.wait_ge(x_read, b * FST + m + 1)
                        for k in range(KT):
                            done = hi_lo(pe, nc, c.pd[:, 2 + m % 2, :], up_w(m, k), xn(b, k), k == 0, k == KT - 1)
                        done.then_inc(x_full, 1)
                    if not last:
                        logits(b + 1, False)
                    pe.wait_ge(a_split, b * FST + FST + 2)
                    for n in range(2):
                        if n and not last:
                            turn_logits(b + 1)
                        pe.wait_ge(y_read, 2 * b + n + 1)
                        for t in (2 * n, 2 * n + 1):
                            out = c.pa[:, 2 + n, (t % 2) * D:(t % 2 + 1) * D]
                            for k in range(FST):
                                done = hi_lo(pe, nc, out, [x[:, k, t * P:(t + 1) * P] for x in (aH, aL)], down_w(k),
                                             k == 0, k == FST - 1)
                        done.then_inc(y_full, 1)

                all_batches(pe, batch)

        with ExitStack() as inner:
            sb = lambda n, s, d=F32: inner.enter_context(nc.sbuf_tensor(f"me_{n}", s, d))
            b1 = sb("b1", [P, E, 2 * F])
            b2 = sb("b2", [P, E, D])
            lane_int = sb("lane_int", [P, P], I32)
            lane_of = sb("lane_of", [P, P])
            token_int = sb("token_int", [P, NT], I32)
            token_of = sb("token_of", [P, NT])
            ones = sb("ones", [P, P], BF16)
            earlier = sb("earlier", [P, P], BF16)
            chosen = sb("chosen", [P, NT + 1, E], BF16)
            count = sb("count", [P, E])
            full = sb("full", [P, E, NT])
            blocks = sb("blocks", [P, E])
            below = sb("below", [P, E, E])
            start = sb("start", [P, E])
            end = sb("end", [P, E])
            past = sb("past", [P, BLOCKS, E])
            expert = sb("expert", [P, BLOCKS])
            expert_id = sb("expert_id", [P, BLOCKS], I32)
            place = sb("place", [P, NT, E])
            match = sb("match", [P, 2, NT, E])
            slot = sb("slot", [P, TOPK, NT])
            weight, slot_id = c.weight, c.slot_id
            slot_block = sb("slot_block", [P, TOPK, NT], I32)
            block_f = sb("block_f", [P, TOPK, NT])
            lane_f = sb("lane_f", [P, TOPK, NT])
            token_id = sb("token_id", [P, BLOCKS], I32)
            x_index = sb("x_index", [P, RING, 1], I32)
            rows = sb("rows", [P, RING, D])
            xT = sb("xT", [P, RING, KT, P])
            passing = sb("passing", [P, 3 * RING * F])
            gate, gl, up = (passing[:, k * RING * F:(k + 1) * RING * F].rearrange("p (s f) -> p s f", f=F) for k in range(3))
            lane_hot = passing[:, 0:NT * P].rearrange("p (t l) -> p t l", l=P)
            block_hot = passing[:, NT * P:NT * (P + BLOCKS)].rearrange("p (t b) -> p t b", b=BLOCKS)
            aT = sb("aT", [P, RING, FT, P])
            y = sb("y", [P, RING, D])
            (const, b_loaded, step, sel_done, prefix_full, hot_done, hot_used, ids_full, ids_done, x_picked, xt_full, xt_done, h_full,
             g_ready, h_read, gelu_done, a_done, at_full, at_done, y_full, y_done) = semaphores(
                nc, inner, "me", "const b_loaded step sel_done prefix_full hot_done hot_used ids_full ids_done x_picked xt_full xt_done "
                "h_full g_ready h_read gelu_done a_done at_full at_done y_full y_done")
            gathered = semaphores(nc, inner, "me", "gathered0 gathered1 gathered2 gathered3")
            y_stored = semaphores(nc, inner, "me", "y_stored0 y_stored1 y_stored2 y_stored3")
            BANKS = 2
            half = lambda bank, h: bank[:, h * D:(h + 1) * D]
            xt_bank = lambda s: half(c.pa[:, s % BANKS, :], 0)
            at_bank = lambda s: half(c.pa[:, BANKS + s % BANKS, :], 0)
            h_bank = lambda s: c.pd[:, s % BANKS, :]
            y_bank = lambda s: half(c.pd[:, BANKS + s % BANKS, :], 0)
            block = inner.enter_context(nc.Block())

            def all_blocks(engine, work, flush=None):
                for s in range(RING):
                    work(0, s, s)
                with engine.Fori(1, ROUNDS - 1) as i:
                    for s in range(RING):
                        work(i, s, None)
                for s in range(LAST_ROUND):
                    work(ROUNDS - 1, s, (ROUNDS - 1) * RING + s)

            def neighbour(i, s, n, by):
                to = s + by
                return i + to // RING, to % RING, None if n is None else n + by

            exists = lambda n: n is None or 0 <= n < BLOCKS
            at = lambda i, s: i * RING + s

            @block.sync
            def _(sp):
                third = E // 3
                for k in range(3):
                    part = c.ins["b1row"][k * third * 2 * F:(k + 1) * third * 2 * F]
                    sp.dma_start(b1[:, k * third:(k + 1) * third, :].rearrange("p e f -> p (e f)"), part.partition_broadcast(P)).then_inc(b_loaded, DMA)
                sp.dma_start(b2[:, :, :].rearrange("p e f -> p (e f)"), c.ins["b2row"].partition_broadcast(P)).then_inc(b_loaded, DMA)

                def work(i, s, n):
                    sp.wait_ge(y_done, at(i, s) + 1 + BANKS)
                    sp.dma_start(c.y_dram[bass.ds(at(i, s) * P, P), :], y[:, s, :]).then_inc(y_stored[s], DMA)

                all_blocks(sp, work)
                for s in range(RING):
                    sp.wait_ge(y_stored[s], (ROUNDS + (s < LAST_ROUND)) * DMA)

            @block.gpsimd
            def _(pool):
                nc.gpsimd.iota(lane_int[:, :], [[1, P]], base=0, channel_multiplier=0).then_inc(const, 1)
                nc.gpsimd.iota(token_int[:, :], [[P, NT]], base=0, channel_multiplier=1).then_inc(const, 1)
                nc.gpsimd.memset(ones[:, :], 1.0).then_inc(const, 1)
                nc.gpsimd.memset(earlier[:, :], 1.0).then_inc(const, 1)
                nc.gpsimd.memset(chosen[:, NT, :], 0.0).then_inc(const, 1)
                pool.wait_ge(const, 5)
                nc.gpsimd.affine_select(out=earlier[:, :], in_=earlier[:, :], compare_op=ALU.is_gt, fill=0.0, base=0,
                                        pattern=[[1, P]], channel_multiplier=-1).then_inc(const, 1)
                pool.wait_ge(ids_done, 2)

                def work(i, s, n):
                    pool.wait_ge(xt_full, at(i, s) + 1)
                    apart(pool, c)
                    nc.gpsimd.tensor_copy(x_index[:, s, :], token_id[:, bass.ds(at(i, s), 1)]).then_inc(x_picked, 1)
                    pool.wait_ge(x_picked, at(i, s) + 1)
                    apart(pool, c)
                    nc.gpsimd.indirect_dma_start(out=rows[:, s, :], out_offset=None, in_=c.rows_dram,
                                                 in_offset=bass.IndirectOffsetOnAxis(x_index[:, s, :].bitcast(U32), 0)).then_inc(gathered[s], DMA)

                all_blocks(pool, work)

            @block.scalar
            def _(act):
                act.wait_ge(ids_done, 2)

                def turn_x(i, s):
                    act.wait_ge(xt_full, at(i, s) + 1 + RING)
                    nc.scalar.activation(xT[:, s, :, :].rearrange("p k t -> p (k t)"), xt_bank(s), ACT.Copy).then_inc(xt_done, 1)

                def work(i, s, n):
                    if n == 0:
                        turn_x(i, s)
                    i1, s1, n1 = neighbour(i, s, n, 1)
                    if exists(n1):
                        turn_x(i1, s1)
                    act.wait_ge(g_ready, at(i, s) + 1)
                    nc.scalar.activation(gl[:, s, :], gate[:, s, :], ACT.Gelu).then_inc(gelu_done, 1)
                    i0, s0, n0 = neighbour(i, s, n, -1)
                    if exists(n0):
                        scale_a(i0, s0)
                    if n == BLOCKS - 1:
                        scale_a(i, s)

                def scale_a(i, s):
                    e = act.value_load(expert_id[0:1, bass.ds(at(i, s), 1)], min_val=0, max_val=E - 1)
                    act.wait_ge(at_full, at(i, s) + 1)
                    apart(act, c)
                    for f in range(FT):
                        last = nc.scalar.activation(aT[:, s, f, :], at_bank(s)[:, f * P:(f + 1) * P], ACT.Copy,
                                                    scale=mult[:, bass.ds(e, 1), f:f + 1].rearrange("p o f -> p (o f)"))
                    last.then_inc(at_done, 1)

                all_blocks(act, work)

            @block.vector
            def _(dve):
                dve.sem_inc(h_read, BANKS)
                dve.sem_inc(y_done, BANKS)
                for s in range(RING):
                    dve.sem_inc(y_stored[s], DMA)
                steps = 0

                def done(instruction):
                    nonlocal steps
                    instruction.then_inc(step, 1)
                    steps += 1
                    dve.wait_ge(step, steps)

                V = nc.vector
                dve.wait_ge(const, 6)
                V.tensor_scalar(chosen[:, 0:NT, :], rank[:, :, :], TOPK - 0.5, None, ALU.is_lt).then_inc(sel_done, 1)
                V.tensor_copy(token_of[:, :], token_int[:, :])
                done(V.tensor_copy(lane_of[:, :], lane_int[:, :]))
                dve.wait_ge(prefix_full, 1)
                done(V.tensor_copy(count[:, :], c.pd[:, 0, NT * E:(NT + 1) * E]))
                done(V.tensor_scalar(blocks[:, :], count[:, :], 1.0 / P, None, ALU.mult))
                done(V.tensor_tensor(full[:, :, :], blocks[:, :].unsqueeze(2).to_broadcast([P, E, NT]),
                                     lane_of[:, 0:NT].unsqueeze(1).to_broadcast([P, E, NT]), ALU.is_gt))
                done(V.reduce_sum(blocks[:, :], full[:, :, :], AX.X))
                done(V.tensor_tensor(below[:, :, :], before[:, :, :], blocks[:, :].unsqueeze(1).to_broadcast([P, E, E]), ALU.mult))
                done(V.reduce_sum(start[:, :], below[:, :, :], AX.X))
                V.tensor_tensor(end[:, :], start[:, :], blocks[:, :], ALU.add)
                done(V.tensor_scalar(count[:, :], start[:, :], float(P), None, ALU.mult))
                done(V.tensor_tensor(place[:, :, :], c.pd[:, 0, 0:NT * E].rearrange("p (t e) -> p t e", e=E),
                                     count[:, :].unsqueeze(1).to_broadcast([P, NT, E]), ALU.add))
                for k in range(TOPK):
                    V.scalar_tensor_tensor(match[:, 0, :, :], rank[:, :, :], float(k), place[:, :, :], ALU.is_equal, ALU.mult)
                    done(V.scalar_tensor_tensor(match[:, 1, :, :], rank[:, :, :], float(k), comb[:, :, :], ALU.is_equal, ALU.mult))
                    V.reduce_sum(slot[:, k, :], match[:, 0, :, :], AX.X)
                    done(V.reduce_sum(weight[:, k, :], match[:, 1, :, :], AX.X))
                done(V.tensor_copy(slot_id[:, :, :], slot[:, :, :]))
                done(V.tensor_scalar(slot_block[:, :, :], slot_id[:, :, :], 7, None, ALU.arith_shift_right))
                done(V.tensor_copy(block_f[:, :, :], slot_block[:, :, :]))
                done(V.scalar_tensor_tensor(lane_f[:, :, :], block_f[:, :, :], -float(P), slot[:, :, :], ALU.mult, ALU.add))
                for k in range(TOPK):
                    if k:
                        dve.wait_ge(hot_used, k)
                    V.tensor_tensor(lane_hot[:, :, :], lane_f[:, k, :].unsqueeze(2).to_broadcast([P, NT, P]),
                                    lane_of[:, :].unsqueeze(1).to_broadcast([P, NT, P]), ALU.is_equal)
                    done(V.tensor_tensor(block_hot[:, :, :], block_f[:, k, :].unsqueeze(2).to_broadcast([P, NT, BLOCKS]),
                                         lane_of[:, 0:BLOCKS].unsqueeze(1).to_broadcast([P, NT, BLOCKS]), ALU.is_equal))
                    V.tensor_tensor(block_hot[:, :, :], block_hot[:, :, :], token_of[:, :].unsqueeze(2).to_broadcast([P, NT, BLOCKS]),
                                    ALU.mult).then_inc(hot_done, 1)
                done(V.tensor_tensor(past[:, :, :], lane_of[:, 0:BLOCKS].unsqueeze(2).to_broadcast([P, BLOCKS, E]),
                                     end[:, :].unsqueeze(1).to_broadcast([P, BLOCKS, E]), ALU.is_ge))
                done(V.reduce_sum(expert[:, :], past[:, :, :], AX.X))
                done(V.tensor_scalar(expert[:, :], expert[:, :], float(E - 1), None, ALU.min))
                V.tensor_copy(expert_id[:, :], expert[:, :]).then_inc(ids_done, 1)
                dve.wait_ge(ids_full, 1)
                V.tensor_copy(token_id[:, :], c.pd[:, 1, 0:BLOCKS]).then_inc(ids_done, 1)
                dve.wait_ge(ids_done, 2)
                dve.wait_ge(b_loaded, 4 * DMA)

                def keep_y(i, s):
                    e = dve.value_load(expert_id[0:1, bass.ds(at(i, s), 1)], min_val=0, max_val=E - 1)
                    dve.wait_ge(y_full, at(i, s) + 1)
                    dve.wait_ge(y_stored[s], i * DMA + DMA)
                    V.tensor_tensor(y[:, s, :], y_bank(s), b2[:, bass.ds(e, 1), :].rearrange("p o f -> p (o f)"), ALU.add).then_inc(y_done, 1)

                def work(i, s, n):
                    e = dve.value_load(expert_id[0:1, bass.ds(at(i, s), 1)], min_val=0, max_val=E - 1)
                    bias = lambda f: b1[:, bass.ds(e, 1), f:f + F].rearrange("p o f -> p (o f)")
                    dve.wait_ge(h_full, at(i, s) + 1)
                    V.tensor_tensor(gate[:, s, :], half(h_bank(s), 1), bias(F), ALU.add).then_inc(g_ready, 1)
                    V.tensor_tensor(up[:, s, :], half(h_bank(s), 0), bias(0), ALU.add).then_inc(h_read, 1)
                    i2, s2, n2 = neighbour(i, s, n, -2)
                    if exists(n2):
                        keep_y(i2, s2)
                    dve.wait_ge(gelu_done, at(i, s) + 1)
                    dve.wait_ge(h_read, at(i, s) + 1 + BANKS)
                    V.tensor_tensor(up[:, s, :], up[:, s, :], gl[:, s, :], ALU.mult).then_inc(a_done, 1)
                    if n == BLOCKS - 1:
                        keep_y(*neighbour(i, s, n, -1)[:2])
                        keep_y(i, s)

                all_blocks(dve, work)

            @block.tensor
            def _(pe):
                pe.sem_inc(xt_full, RING)
                pe.wait_ge(const, 6)
                pe.wait_ge(sel_done, 1)
                nc.tensor.matmul(c.pd[:, 0, 0:(NT + 1) * E], earlier[:, :], chosen[:, :, :].rearrange("p t e -> p (t e)"), start=True, stop=False)
                for t in range(NT):
                    later = NT - t
                    last = nc.tensor.matmul(c.pd[:, 0, (t + 1) * E:(NT + 1) * E], ones[:, :],
                                            chosen[:, t, :].unsqueeze(1).to_broadcast([P, later, E]), start=False, stop=t == NT - 1)
                last.then_inc(prefix_full, 1)
                for k in range(TOPK):
                    pe.wait_ge(hot_done, k + 1)
                    for t in range(NT):
                        last = nc.tensor.matmul(c.pd[:, 1, 0:BLOCKS], lane_hot[:, t, :], block_hot[:, t, :], start=k == 0 and t == 0,
                                                stop=k == TOPK - 1 and t == NT - 1)
                    last.then_inc(hot_used if k < TOPK - 1 else ids_full, 1)
                pe.wait_ge(ids_done, 2)
                pe.wait_ge(w_loaded, E * DMA)

                def turn_x(i, s):
                    pe.wait_ge(gathered[s], i * DMA + DMA)
                    for k in range(KT):
                        last = nc.tensor.transpose(xt_bank(s)[:, k * P:(k + 1) * P], rows[:, s, k * P:(k + 1) * P], c.ident[:, :])
                    last.then_inc(xt_full, 1)

                def turn_a(i, s):
                    pe.wait_ge(a_done, at(i, s) + 1)
                    for f in range(FT):
                        last = nc.tensor.transpose(at_bank(s)[:, f * P:(f + 1) * P], up[:, s, f * P:(f + 1) * P], c.ident[:, :])
                    last.then_inc(at_full, 1)

                def second_layer(i, s):
                    e = pe.value_load(expert_id[0:1, bass.ds(at(i, s), 1)], min_val=0, max_val=E - 1)
                    pe.wait_ge(at_done, at(i, s) + 1)
                    pe.wait_ge(y_done, at(i, s) + 1)
                    for f in range(FT):
                        move = weights[:, bass.ds(e, 1), W1 + f * D:W1 + (f + 1) * D].rearrange("p o n -> p (o n)")
                        last = nc.tensor.matmul(y_bank(s), aT[:, s, f, :], move, start=f == 0, stop=f == FT - 1)
                    last.then_inc(y_full, 1)

                def work(i, s, n):
                    if n == 0:
                        turn_x(i, s)
                    i1, s1, n1 = neighbour(i, s, n, 1)
                    if exists(n1):
                        turn_x(i1, s1)
                    e = pe.value_load(expert_id[0:1, bass.ds(at(i, s), 1)], min_val=0, max_val=E - 1)
                    pe.wait_ge(xt_done, at(i, s) + 1)
                    pe.wait_ge(h_read, at(i, s) + 1)
                    for k in range(KT):
                        move = weights[:, bass.ds(e, 1), k * 2 * F:(k + 1) * 2 * F].rearrange("p o n -> p (o n)")
                        last = nc.tensor.matmul(h_bank(s), xT[:, s, k, :], move, start=k == 0, stop=k == KT - 1)
                    last.then_inc(h_full, 1)
                    i0, s0, n0 = neighbour(i, s, n, -1)
                    if exists(n0):
                        turn_a(i0, s0)
                    i2, s2, n2 = neighbour(i, s, n, -2)
                    if exists(n2):
                        second_layer(i2, s2)
                    if n == BLOCKS - 1:
                        turn_a(i, s)
                        second_layer(*neighbour(i, s, n, -1)[:2])
                        second_layer(i, s)

                all_blocks(pe, work)


class SecondAttention:
    AUX = 4 * DH1
    R = 2 * DH1
    QK_LOADS = 9 * DMA
    STORES = 2 * DMA

    def __init__(self, nc, c, ctx):
        sb = lambda n, s, d=F32: ctx.enter_context(nc.sbuf_tensor(f"b_{n}", s, d))
        self.c = c
        self.q4 = sb("q4", [P, 2, GH, S], F32R)
        self.k4 = sb("k4", [P, 2, GH, S], F32R)
        self.V_all = sb("V_all", [P, B, TT, H1, self.R])
        self.V = sb("V", [P, 2, TT, GH, self.R])
        self.qH = sb("qH", [P, 2, KT, S], F32R)
        self.qL = sb("qL", [P, 2, KT, S], F32R)
        self.mask_in = sb("mask_in", [P, 2, TT, S], U8)
        self.by_query = sb("by_query", [P, TT, S])
        self.by_key = sb("by_key", [P, TT, S], BF16)
        self.ident_bf = sb("ident_bf", [P, P], BF16)
        self.select = sb("select", [P, P])
        self.wo_raw = sb("wo_raw", [P, GROUPS * D])
        self.woH = sb("woH", [P, GROUPS * D], F32R)
        self.woL = sb("woL", [P, GROUPS * D], F32R)
        qk_in0, qk_in1, v_in0, v_in1, q_stored0, q_stored1 = semaphores(nc, ctx, "b", "qk_in0 qk_in1 v_in0 v_in1 q_stored0 q_stored1")
        self.q_stored = (q_stored0, q_stored1)
        self.qk_ins, self.v_ins = (qk_in0, qk_in1), (v_in0, v_in1)

    def rows(self, part, l, b, g):
        return part[bass.ds(b, 1), l, g * GH * DH1:(g + 1) * GH * DH1, :].rearrange("o (h d) t -> d (o h) t", d=DH1)

    def load_keys(self, engine, b, g):
        for r, l in enumerate((0, 0, 1, 1)):
            engine.dma_start(self.k4[r * DH1:(r + 1) * DH1, g % 2, :, :].bitcast(F32),
                             self.rows(self.c.k_dram, l, b, g)).then_inc(self.qk_ins[g % 2], DMA)

    def load_queries(self, engine, b, g):
        for r, l in enumerate((0, 1, 0, 1)):
            engine.dma_start(self.q4[r * DH1:(r + 1) * DH1, g % 2, :, :].bitcast(F32),
                             self.rows(self.c.q_dram, l, b, g)).then_inc(self.qk_ins[g % 2], DMA)
        aux = slice(self.AUX, self.AUX + 1)
        engine.dma_start(self.q4[aux, g % 2, :, :].bitcast(F32),
                         self.k4[self.AUX + 1:self.AUX + 2, g % 2, :, :].bitcast(F32)).then_inc(self.qk_ins[g % 2], DMA)

    def load_values(self, engine, b, g):
        engine.dma_start(self.V[:, g % 2, :, :, :].rearrange("p t h r -> p t (h r)"),
                         self.V_all[:, bass.ds(b, 1), :, g * GH:(g + 1) * GH, :].rearrange("p o t h r -> p (o t) (h r)")
                         ).then_inc(self.v_ins[g % 2], DMA)


def combination_phase(nc, c, att):
    AHEAD = NT // 2
    USES = 4
    assert NT == 2 * AHEAD and AHEAD == 2 * TT
    with ExitStack() as ctx:
        sb = lambda n, s, d=F32: ctx.enter_context(nc.sbuf_tensor(f"c_{n}", s, d))
        raw = sb("raw", [P, 2, KT * D])
        wH = sb("wH", [P, 2, KT * D], F32R)
        wL = sb("wL", [P, 2, KT * D], F32R)
        ctxH = sb("ctxH", [P, 2, KT, S], F32R)
        ctxL = sb("ctxL", [P, 2, KT, S], F32R)
        ctx_raw = sb("ctx_raw", [P, 2, KT, S])
        kH = sb("kH", [P, 2, KT, S], F32R)
        kL = sb("kL", [P, 2, KT, S], F32R)
        y_index = sb("y_index", [P, AHEAD, TOPK, 1], I32)
        y_rows = sb("y_rows", [P, AHEAD, TOPK, D])
        (w_in, w_hi, w_lo, ctx_in0, ctx_in1, ctx_hi, ctx_lo, use_full, hi_done, use_read, stored0, stored1,
         y_picked, add_step, added) = semaphores(
            nc, ctx, "c", "w_in w_hi w_lo ctx_in0 ctx_in1 ctx_hi ctx_lo use_full hi_done use_read stored0 stored1 "
            "y_picked add_step added", reuse=True)
        y_in = semaphores(nc, ctx, "c", " ".join(f"y_in{h}" for h in range(AHEAD)), reuse=True)
        ctx_ins, stored = (ctx_in0, ctx_in1), (stored0, stored1)
        STORES = 2 * DMA
        block = ctx.enter_context(nc.Block())

        @block.sync
        def _(sp):
            for n, name in enumerate(("wk1", "wv1")):
                sp.dma_start(raw[:, n, :], c.ins[name]).then_inc(w_in, DMA)
            for par in range(2):
                sp.dma_start(ctx_raw[:, par, :, :], c.ins["ctx"][:, :, par * S:(par + 1) * S]).then_inc(ctx_ins[par], DMA)

            def store(b, par):
                sp.wait_ge(use_read, b * USES + KT + USES)
                for l, src in enumerate((kH, kL)):
                    sp.dma_start(c.k_dram[bass.ds(b, 1), l, :, :].rearrange("o (m p) t -> p (o m) t", p=P),
                                 src[:, par, :, :].bitcast(F32)).then_inc(stored[par], DMA)

            with sp.Fori(0, B // 2 - 1) as i:
                for par in range(2):
                    b = i * 2 + par
                    sp.wait_ge(ctx_lo, b + 1)
                    sp.dma_start(ctx_raw[:, par, :, :], c.ins["ctx"][:, :, bass.ds((b + 2) * S, S)]).then_inc(ctx_ins[par], DMA)
                    store(b, par)
            for par in range(2):
                store(B - 2 + par, par)
            for par in range(2):
                sp.wait_ge(stored[par], (B // 2 + 1) * STORES)

        @block.gpsimd
        def _(pool):
            with pool.Fori(0, 2) as i:
                for h in range(AHEAD):
                    pool.wait_ge(y_picked, i * AHEAD + h + 1)
                    apart(pool, c)
                    for k in range(TOPK):
                        nc.gpsimd.indirect_dma_start(out=y_rows[:, h, k, :], out_offset=None, in_=c.y_dram,
                                                     in_offset=bass.IndirectOffsetOnAxis(y_index[:, h, k, :].bitcast(U32), 0)).then_inc(y_in[h], DMA)

        @block.scalar
        def _(act):
            def pick(n, to):
                nc.scalar.activation(y_index[:, bass.ds(to, 1), :, 0].rearrange("p o k -> p (o k)"),
                                     c.slot_id[:, :, bass.ds(n, 1)].rearrange("p k o -> p (k o)"), ACT.Copy).then_inc(y_picked, 1)

            for h in range(AHEAD):
                pick(h, h)
            for par in range(2):
                act.sem_inc(stored[par], STORES)
            act.wait_ge(w_in, 2 * DMA)
            nc.scalar.activation(wH[:, :, :], raw[:, :, :], ACT.Copy).then_inc(w_hi, 1)

            def context_hi(par, round):
                act.wait_ge(ctx_ins[par], round * DMA + DMA)
                apart(act, c)
                nc.scalar.activation(ctxH[:, par, :, :], ctx_raw[:, par, :, :], ACT.Copy).then_inc(ctx_hi, 1)

            def keys_hi(i, par, last=False):
                b = i * 2 + par
                act.wait_ge(use_read, b * USES + USES)
                if not last:
                    context_hi(1 - par, i + par)
                act.wait_ge(stored[par], i * STORES + STORES)
                for u in range(KT):
                    act.wait_ge(use_full, b * USES + u + 1)
                    nc.scalar.activation(kH[:, par, u, :], c.pd[:, u, :], ACT.Copy).then_inc(hi_done, 1)

            context_hi(0, 0)
            for par in range(2):
                keys_hi(0, par)
                for t in range(TT):
                    n = par * TT + t
                    act.wait_ge(added, n + 1)
                    pick(n + AHEAD, n)
            for par in range(2):
                keys_hi(B // 2 - 1, par, par == 1)

        @block.vector
        def _(dve):
            dve.sem_inc(use_read, USES)
            dve.wait_ge(w_hi, 1)
            nc.vector.tensor_tensor(wL[:, :, :], raw[:, :, :], wH[:, :, :].bitcast(F32), ALU.subtract).then_inc(w_lo, 1)

            def context_lo(b, par):
                dve.wait_ge(ctx_hi, b + 1)
                nc.vector.tensor_tensor(ctxL[:, par, :, :], ctx_raw[:, par, :, :], ctxH[:, par, :, :].bitcast(F32),
                                        ALU.subtract).then_inc(ctx_lo, 1)

            def batch(i, par, last=False):
                b = i * 2 + par
                if not last:
                    context_lo(b + 1, 1 - par)
                for u in range(KT):
                    dve.wait_ge(hi_done, b * KT + u + 1)
                    nc.vector.tensor_tensor(kL[:, par, u, :], c.pd[:, u, :], kH[:, par, u, :].bitcast(F32),
                                            ALU.subtract).then_inc(use_read, 1)
                for n in range(2):
                    dve.wait_ge(use_full, b * USES + KT + n + 1)
                    apart(dve, c)
                    nc.vector.tensor_copy(att.V_all[:, bass.ds(b, 1), 2 * n:2 * n + 2, :, 0:DH1].rearrange("p o t h d -> p (o t) h d"),
                                          c.pd[:, KT + n, :].rearrange("p (t h d) -> p t h d", h=H1, d=DH1)).then_inc(use_read, 1)
                for k in range(TOPK):
                    for t in range(TT):
                        h, at = par * TT + t, bass.ds(b * TT + t, 1)
                        xt = c.X[:, at, :].rearrange("p o d -> p (o d)")
                        if k == 0:
                            dve.wait_ge(y_in[h], (i + 1) * TOPK * DMA)
                        else:
                            dve.wait_ge(add_step, (b * (TOPK - 1) + k - 1) * TT + t + 1)
                        last_add = nc.vector.scalar_tensor_tensor(xt, y_rows[:, h, k, :], c.weight[:, k, at], xt, ALU.mult, ALU.add)
                        last_add.then_inc(add_step if k < TOPK - 1 else added, 1)
                for t in range(TT):
                    dve.wait_ge(added, b * TT + t + 1)
                    apart(dve, c)
                    token_stats(nc, c, b * TT + t)

            context_lo(0, 0)
            nc.vector.memset(att.V_all[:, :, :, :, DH1:].rearrange("p b t h r -> p (b t h) r"), 1.0)
            with dve.Fori(0, B // 2 - 1) as i:
                for par in range(2):
                    batch(i, par)
            for par in range(2):
                batch(B // 2 - 1, par, par == 1)

        @block.tensor
        def _(pe):
            pe.wait_ge(w_lo, 1)
            weight = lambda w, k, lo, n: [x[:, w, k * D + lo:k * D + lo + n] for x in (wH, wL)]
            with pe.Fori(0, B // 2) as i:
                for par in range(2):
                    b = i * 2 + par
                    pe.wait_ge(ctx_lo, b + 1)
                    for u in range(KT):
                        pe.wait_ge(use_read, b * USES + u + 1)
                        for k in range(KT):
                            last = hi_lo(pe, nc, c.pd[:, u, :], weight(0, k, u * P, P), [x[:, par, k, :] for x in (ctxH, ctxL)],
                                         k == 0, k == KT - 1)
                        last.then_inc(use_full, 1)
                    for n in range(2):
                        pe.wait_ge(use_read, b * USES + KT + n + 1)
                        for t in (2 * n, 2 * n + 1):
                            for k in range(KT):
                                last = hi_lo(pe, nc, c.pd[:, KT + n, (t % 2) * D:(t % 2 + 1) * D],
                                             [x[:, par, k, t * P:(t + 1) * P] for x in (ctxH, ctxL)], weight(1, k, 0, D), k == 0, k == KT - 1)
                        last.then_inc(use_full, 1)


def second_projection_phase(nc, c, att):
    with ExitStack() as ctx:
        sb = lambda n, s, d=F32: ctx.enter_context(nc.sbuf_tensor(f"p_{n}", s, d))
        raw = sb("raw", [P, KT * D])
        wH = sb("wH", [P, KT * D], F32R)
        wL = sb("wL", [P, KT * D], F32R)
        qH, qL = att.qH, att.qL
        (w_in, w_hi, w_lo, const, use_full, hi_done, use_read, set_in, wo_hi) = semaphores(
            nc, ctx, "p", "w_in w_hi w_lo const use_full hi_done use_read set_in wo_hi")
        stored, STORES = att.q_stored, att.STORES

        def load_first(sp):
            sp.dma_start(raw[:, :], c.ins["wq1"]).then_inc(w_in, DMA)
            for g in range(2):
                att.load_keys(sp, 0, g)
                att.load_values(sp, 0, g)
            sp.dma_start(att.wo_raw[:, :], c.ins["wo1"]).then_inc(set_in, DMA)
            for n, name in enumerate(("mask", "maskT")):
                sp.dma_start(att.mask_in[:, n, :, :], c.ins[name].rearrange("(n p) k -> p n k", p=P)).then_inc(set_in, DMA)

        def weights_hi(act):
            act.wait_ge(w_in, DMA)
            nc.scalar.activation(wH[:, :], raw[:, :], ACT.Copy).then_inc(w_hi, 1)

        def weights_lo(pool):
            pool.wait_ge(w_hi, 1)
            nc.gpsimd.tensor_tensor(wL[:, :], raw[:, :], wH[:, :].bitcast(F32), ALU.subtract).then_inc(w_lo, 1)
            pool.wait_ge(w_lo, 1)
            nc.gpsimd.memset(att.q4[att.AUX:P, :, :, :].bitcast(F32), 0.0).then_inc(const, 1)
            nc.gpsimd.memset(att.k4[att.AUX:P, :, :, :].bitcast(F32), 0.0).then_inc(const, 1)
            pool.wait_ge(const, 2)
            nc.gpsimd.memset(att.select[:, :], 0.0).then_inc(const, 1)
            pool.wait_ge(const, 3)
            nc.gpsimd.memset(att.k4[att.AUX:att.AUX + 1, :, :, :].bitcast(F32), 1.0).then_inc(const, 1)
            pool.wait_ge(const, 4)
            sel = att.select[:, :].rearrange("p (h r) -> p h r", r=att.R)
            nc.gpsimd.affine_select(out=sel, in_=sel, compare_op=ALU.not_equal, fill=1.0, base=-DH1,
                                    pattern=[[-att.R, GH], [0, att.R]], channel_multiplier=1).then_inc(const, 1)

        layernorm_phase(nc, c, 2, prefetch=load_first, split_hi=weights_hi, split_lo=weights_lo)
        block = ctx.enter_context(nc.Block())

        @block.sync
        def _(sp):
            def store(b, par):
                sp.wait_ge(use_read, b * KT + KT + 2 * KT)
                for l, src in enumerate((qH, qL)):
                    sp.dma_start(c.q_dram[bass.ds(b, 1), l, :, :].rearrange("o (m p) t -> p (o m) t", p=P),
                                 src[:, par, :, :].bitcast(F32)).then_inc(stored[par], DMA)

            with sp.Fori(0, B // 2 - 1) as i:
                for par in range(2):
                    store(i * 2 + par, par)
            sp.wait_ge(const, 5)
            sp.wait_ge(stored[0], 2 * STORES)
            for par in range(2):
                att.load_queries(sp, 0, par)
                store(B - 2 + par, par)

        @block.gpsimd
        def _(pool):
            pool.wait_ge(wo_hi, 1)
            nc.gpsimd.tensor_tensor(att.woL[:, :], att.wo_raw[:, :], att.woH[:, :].bitcast(F32), ALU.subtract)

        @block.scalar
        def _(act):
            for par in range(2):
                act.sem_inc(stored[par], STORES)
            act.wait_ge(set_in, 3 * DMA)
            nc.scalar.activation(att.woH[:, :], att.wo_raw[:, :], ACT.Copy).then_inc(wo_hi, 1)
            nc.scalar.activation(att.by_key[:, :, :], att.mask_in[:, 1, :, :], ACT.Copy, scale=MASKED)
            nc.scalar.activation(att.ident_bf[:, :], c.ident[:, :], ACT.Copy)
            with act.Fori(0, B // 2) as i:
                for par in range(2):
                    b = i * 2 + par
                    act.wait_ge(stored[par], i * STORES + STORES)
                    for u in range(KT):
                        act.wait_ge(use_full, b * KT + u + 1)
                        nc.scalar.activation(qH[:, par, u, :], c.pd[:, par * KT + u, :], ACT.Copy).then_inc(hi_done, 1)

        @block.vector
        def _(dve):
            dve.sem_inc(use_read, 2 * KT)
            dve.wait_ge(set_in, 3 * DMA)
            nc.vector.tensor_scalar(att.by_query[:, :, :], att.mask_in[:, 0, :, :], MASKED, None, ALU.mult)
            with dve.Fori(0, B // 2) as i:
                for par in range(2):
                    b = i * 2 + par
                    for u in range(KT):
                        dve.wait_ge(hi_done, b * KT + u + 1)
                        nc.vector.tensor_tensor(qL[:, par, u, :], c.pd[:, par * KT + u, :], qH[:, par, u, :].bitcast(F32),
                                                ALU.subtract).then_inc(use_read, 1)

        @block.tensor
        def _(pe):
            pe.wait_ge(w_lo, 1)
            with pe.Fori(0, B // 2) as i:
                for par in range(2):
                    b = i * 2 + par
                    for u in range(KT):
                        pe.wait_ge(use_read, b * KT + u + 1)
                        for k in range(KT):
                            last = hi_lo(pe, nc, c.pd[:, par * KT + u, :], [x[:, k * D + u * P:k * D + (u + 1) * P] for x in (wH, wL)],
                                         [x[:, k, bass.ds(b * S, S)] for x in (c.xnH, c.xnL)], k == 0, k == KT - 1)
                        last.then_inc(use_full, 1)


def second_attention_phase(nc, c, att):
    R, AUX = att.R, att.AUX
    q4, k4, V, by_query, by_key, ident_bf, select = att.q4, att.k4, att.V, att.by_query, att.by_key, att.ident_bf, att.select
    woH, woL = att.woH, att.woL
    with ExitStack() as ctx:
        sb = lambda n, s, d=F32: ctx.enter_context(nc.sbuf_tensor(f"b_{n}", s, d))
        masked = sb("masked", [P, 2, S], BF16)
        mx = sb("mx", [P, 4, TT])
        prob = sb("prob", [P, 2, GH, TT, S])
        osum = sb("osum", [P, 2, S])
        inv = sb("inv", [P, S])
        oH, oL = (x[:, :, :, :].rearrange("p n k s -> p (n k) s") for x in (att.qH, att.qL))
        (s_full, s_read, row_full, row_done, st_full,
         exp_done, pv_full, osum_done, sel_full, sel_read, norm_step, o_split, y_full, y_read) = semaphores(
            nc, ctx, "b", "s_full s_read row_full row_done st_full "
            "exp_done pv_full osum_done sel_full sel_read norm_step o_split y_full y_read")
        qk_ins, v_ins, QK_LOADS = att.qk_ins, att.v_ins, att.QK_LOADS
        PV_LAG, KEEP_LAG, SUM_LAG, NORM_LAG = 5, 8, 9, 11
        WO_AT = 10

        def behind(n, lag, first):
            m = n - lag
            return None if m < 0 and first else (0, m) if m >= 0 else (1, m + H1)

        block = ctx.enter_context(nc.Block())

        @block.sync
        def _(sp):
            def load(b, g):
                sp.wait_ge(st_full, b * 2 * H1 + (g + 1) * 2 * GH)
                att.load_keys(sp, b, g)
                att.load_queries(sp, b, g)
                sp.wait_ge(pv_full, b * GROUPS + g + 1)
                att.load_values(sp, b, g)

            for stored in att.q_stored:
                sp.wait_ge(stored, (B // 2 + 1) * att.STORES)
            with sp.Fori(0, B - 1) as b:
                for ahead, g in ((0, 2), (0, 3), (1, 0), (1, 1)):
                    load(b + ahead, g)
            for g in (2, 3):
                load(B - 1, g)

        @block.scalar
        def _(act):
            def keep_sums(b, g):
                act.wait_ge(pv_full, b * GROUPS + g + 1 + 2)
                act.wait_ge(o_split, b * GROUPS + g + 1)
                nc.scalar.activation(osum[:, g % 2, :], c.pd[:, 2, :], ACT.Copy).then_inc(osum_done, 1)

            def batch(b, first, last):
                for n in range(H1):
                    g, i = n // GH, n % GH
                    act.wait_ge(row_full, b * H1 + n + 1)
                    nc.scalar.activation(q4[AUX:AUX + 1, g % 2, i, :], c.pd[0:1, 3, :], ACT.Copy, scale=-1.0).then_inc(row_done, 1)
                    at = behind(n, KEEP_LAG, first)
                    if at and i == 0:
                        keep_sums(b - at[0], at[1] // GH)
                    for half in range(2):
                        act.wait_ge(st_full, (b * H1 + n) * 2 + half + 1 + 4 * GH)
                        act.wait_ge(pv_full, b * GROUPS + g + 1)
                        nc.scalar.activation(prob[:, g % 2, i, 2 * half:2 * half + 2, :], c.pa[:, 2 * half:2 * half + 2, :], ACT.Exp,
                                             scale=DH1 ** -0.5).then_inc(exp_done, 1)
                if last:
                    keep_sums(b, 2)
                    keep_sums(b, 3)

            all_batches(act, batch)

        @block.vector
        def _(dve):
            dve.sem_inc(s_read, 2)
            dve.sem_inc(o_split, 2)
            dve.sem_inc(y_read, 2)
            dve.sem_inc(sel_read, 1)
            def normalise(b, g, part, step):
                G = b * GROUPS + g
                at = slice(part * (S // 4), (part + 1) * (S // 4))
                if step == 0:
                    if part == 0:
                        dve.wait_ge(sel_full, G + 1)
                        dve.wait_ge(o_split, G + 2)
                        nc.vector.tensor_scalar(inv[:, :], c.pd[:, 3, :], 1e-30, None, ALU.max).then_inc(sel_read, 1)
                        dve.wait_ge(sel_read, G + 2)
                    nc.vector.reciprocal(inv[:, at], inv[:, at]).then_inc(norm_step, 1)
                elif part == 3:
                    dve.wait_ge(norm_step, 6 * G + 3 + step)
                    if step == 1:
                        nc.vector.tensor_tensor(inv[:, :], osum[:, g % 2, :], inv[:, :], ALU.mult).then_inc(norm_step, 1)
                    elif step == 2:
                        for stored in att.q_stored:
                            dve.wait_ge(stored, (B // 2 + 1) * att.STORES)
                        nc.vector.tensor_copy(oH[:, g, :], inv[:, :]).then_inc(norm_step, 1)
                    else:
                        nc.vector.tensor_tensor(oL[:, g, :], inv[:, :], oH[:, g, :].bitcast(F32), ALU.subtract).then_inc(o_split, 1)

            def add_output(b, n, bank):
                dve.wait_ge(y_full, 2 * b + n + 1)
                xb = c.X[:, bass.ds(b * TT + 2 * n, 2), :].rearrange("p n d -> p (n d)")
                nc.vector.tensor_tensor(xb, c.pd[:, bank, :], xb, ALU.add).then_inc(y_read, 1)
                dve.wait_ge(y_read, 2 * b + n + 3)
                apart(dve, c)
                for t in (2 * n, 2 * n + 1):
                    token_stats(nc, c, b * TT + t)

            def batch(b, first, last):
                for n in range(H1):
                    at = behind(n, NORM_LAG, first)
                    for t in range(TT):
                        dve.wait_ge(s_full, (b * H1 + n) * TT + t + 1)
                        dve.wait_ge(s_read, (b * H1 + n) * TT + t + 1)
                        apart(dve, c)
                        nc.vector.tensor_tensor_reduce(masked[:, t % 2, :], c.pd[:, t % 2, :], by_query[:, t, :], 1.0, LEAST_MAX, ALU.add, ALU.max,
                                                       accum_out=mx[:, n % 4, t:t + 1]).then_inc(s_read, 1)
                        for step in ((), (0, 1), (), (2, 3))[t] if at else ():
                            normalise(b - at[0], at[1] // GH, at[1] % GH, step)
                    if not first and n - 2 in (WO_AT, WO_AT + 1):
                        add_output(b - 1, n - 2 - WO_AT, 3)
                if last:
                    for m in range(H1 - NORM_LAG, H1):
                        for step in range(4):
                            normalise(b, m // GH, m % GH, step)
                    for n in range(2):
                        add_output(b, n, 3 - n)

            all_batches(dve, batch)

        @block.tensor
        def _(pe):
            pe.sem_inc(st_full, 4 * GH)
            pe.sem_inc(pv_full, 2)
            pe.sem_inc(row_done, 1)
            pe.sem_inc(osum_done, 1)
            pe.sem_inc(exp_done, 2)
            def by_query_scores(b, n, tiles):
                g, i = n // GH, n % GH
                if i == 0 and 0 in tiles:
                    pe.wait_ge(qk_ins[g % 2], (b * 2 + g // 2 + 1) * QK_LOADS)
                for t in tiles:
                    pe.wait_ge(s_read, (b * H1 + n) * TT + t + 1)
                    nc.tensor.matmul(c.pd[:, t % 2, :], q4[:, g % 2, i, t * P:(t + 1) * P], k4[:, g % 2, i, :],
                                     start=True, stop=True).then_inc(s_full, 1)

            def max_row(b, n, first):
                pe.wait_ge(s_read, (b * H1 + n) * TT + TT + 2)
                pe.wait_ge(row_done, b * H1 + n + 1)
                pe.wait_ge(sel_read, 1 + (max(0, (n - SUM_LAG + 3) // GH) if first else b * GROUPS + (n - SUM_LAG + 3) // GH))
                if not first and n > WO_AT:
                    pe.wait_ge(y_read, 2 * b + (1 if n == WO_AT + 1 else 2))
                for t in range(TT):
                    last = nc.tensor.transpose(c.pd[0:1, 3, t * P:(t + 1) * P], mx[:, n % 4, t:t + 1], c.ident[:, :])
                last.then_inc(row_full, 1)

            def by_key_scores(b, n, half):
                g, i = n // GH, n % GH
                if half == 0:
                    pe.wait_ge(row_done, b * H1 + n + 2)
                pe.wait_ge(exp_done, (b * H1 + n) * 2 + half + 1)
                for t in (2 * half, 2 * half + 1):
                    nc.tensor.matmul(c.pa[:, t, :], k4[:, g % 2, i, t * P:(t + 1) * P], q4[:, g % 2, i, :], start=True, stop=False)
                    last = nc.tensor.matmul(c.pa[:, t, :], ident_bf[:, :], by_key[:, t, :], start=False, stop=True)
                last.then_inc(st_full, 1)

            def values(b, g, t):
                if t == 0:
                    pe.wait_ge(v_ins[g % 2], (b * 2 + g // 2 + 1) * DMA)
                    pe.wait_ge(exp_done, (b * H1 + (g + 1) * GH) * 2 + 2)
                    pe.wait_ge(osum_done, b * GROUPS + g + 1)
                for i in range(GH):
                    last = nc.tensor.matmul(c.pd[i * R:(i + 1) * R, 2, :], V[:, g % 2, t, i, :], prob[:, g % 2, i, t, :],
                                            start=t == 0, stop=t == TT - 1, tile_position=(0, i * R))
                if t == TT - 1:
                    last.then_inc(pv_full, 1)

            def spread_sums(b, g, rows):
                pe.wait_ge(osum_done, b * GROUPS + g + 2)
                pe.wait_ge(row_done, rows + 1)
                pe.wait_ge(sel_read, b * GROUPS + g + 1)
                nc.tensor.matmul(c.pd[:, 3, :], select[:, :], osum[:, g % 2, :], start=True, stop=True).then_inc(sel_full, 1)

            def output(b, n, bank):
                if n == 0:
                    pe.wait_ge(o_split, b * GROUPS + GROUPS + 2)
                for t in (2 * n, 2 * n + 1):
                    for k in range(GROUPS):
                        last = hi_lo(pe, nc, c.pd[:, bank, (t % 2) * D:(t % 2 + 1) * D], [x[:, k, t * P:(t + 1) * P] for x in (oH, oL)],
                                     [x[:, k * D:(k + 1) * D] for x in (woH, woL)], k == 0, k == GROUPS - 1)
                last.then_inc(y_full, 1)

            def batch(b, first, last):
                if first:
                    by_query_scores(b, 0, range(TT))
                    by_query_scores(b, 1, range(TT))
                for n in range(H1):
                    ahead = (b, n + 2) if n + 2 < H1 else None if last else (b + 1, n + 2 - H1)
                    max_row(b, n, first)
                    if ahead:
                        by_query_scores(*ahead, (0, 1))
                    at = behind(n, PV_LAG, first)
                    if at:
                        values(b - at[0], at[1] // GH, at[1] % GH)
                    at = behind(n, SUM_LAG, first)
                    if at and at[1] % GH == 0:
                        spread_sums(b - at[0], at[1] // GH, b * H1 + n + 1)
                    by_key_scores(b, n, 0)
                    if ahead:
                        by_query_scores(*ahead, (2, 3))
                    by_key_scores(b, n, 1)
                    if not first and n in (WO_AT, WO_AT + 1):
                        output(b - 1, n - WO_AT, 3)
                if last:
                    for m in range(H1 - PV_LAG, H1):
                        if m % GH == 0:
                            spread_sums(b, m // GH - 1, b * H1 + H1)
                        values(b, m // GH, m % GH)
                    spread_sums(b, 3, b * H1 + H1)
                    pe.wait_ge(y_read, 2 * b + 2)
                    for n in range(2):
                        output(b, n, 3 - n)

            all_batches(pe, batch)


def ffn_phases(nc, c, ctx):
    TILES = 2 * HT
    AT_H1, AT_W3, AT_Z, AT_W12, AT_H2 = 0, 0, 2, HT, HT
    IN_W12, IN_H1, IN_H2, IN_W3 = 0, 2 * KT, 2 * KT + HT, 2 * KT + 2 * HT
    PER_BATCH = HT // B
    sb = lambda n, s, d=F32: ctx.enter_context(nc.sbuf_tensor(f"f_{n}", s, d))
    wH = sb("wH", [P, TILES, HID], F32R)
    wL = sb("wL", [P, TILES, HID], F32R)
    scales = sb("scales", [P, 4, HT])
    out_scale = c.bias[:, :].unsqueeze(1).to_broadcast([P, 2, D])
    hidden = sb("hidden", [P, HT, S])
    (scales_in, w12_in, first_in1, first_in2) = semaphores(nc, ctx, "f", "scales_in w12_in first_in1 first_in2")
    tile = lambda w, m: [x[:, w, m * P:(m + 1) * P] for x in (wH, wL)]

    def load_first(sp):
        sp.dma_start(scales[:, :, :], c.ins["ffn_scales"]).then_inc(scales_in, DMA)
        sp.dma_start(c.bias[:, :], c.ins["w3_s"].partition_broadcast(P)).then_inc(scales_in, DMA)
        for n in range(2 * KT):
            sp.dma_start(first_raw[:, n, :], c.ins["ffn_w"][IN_W12 + n]).then_inc(w12_in, DMA)

    def next_tiles(sp, b, raw, w_ins, w_lo, start):
        for q in range(PER_BATCH):
            sp.wait_ge(w_lo, b * PER_BATCH + PER_BATCH)
            sp.dma_start(raw[:, q, :], c.ins["ffn_w"][bass.ds(start + b * PER_BATCH + q, 1), :, :].rearrange("o p n -> (o p) n")).then_inc(w_ins[q], DMA)

    def tiles_hi(act, b, raw, w_ins, w_hi, at):
        for q in range(PER_BATCH):
            act.wait_ge(w_ins[q], b * DMA + DMA)
            apart(act, c)
            nc.scalar.activation(wH[:, bass.ds(at + b * PER_BATCH + q, 1), :].rearrange("p o n -> p (o n)"), raw[:, q, :], ACT.Copy).then_inc(w_hi, 1)

    def tiles_lo(dve, b, raw, w_hi, w_lo, at):
        for q in range(PER_BATCH):
            to = bass.ds(at + b * PER_BATCH + q, 1)
            dve.wait_ge(w_hi, b * PER_BATCH + q + 1)
            nc.vector.tensor_tensor(wL[:, to, :].rearrange("p o n -> p (o n)"), raw[:, q, :],
                                    wH[:, to, :].rearrange("p o n -> p (o n)").bitcast(F32), ALU.subtract).then_inc(w_lo, 1)

    with ExitStack() as inner:
        first_raw = hidden[:, :, :].rearrange("p m t -> p (m t)").rearrange("p (n f) -> p n f", f=HID)
        next_raw = first_raw[:, PER_BATCH:2 * PER_BATCH, :]
        gate_h = inner.enter_context(nc.sbuf_tensor("fa_gate_h", [P, 2 * TT, D], F32))
        c.xnH = inner.enter_context(nc.sbuf_tensor("f_xnH", [P, KT, T], F32R))
        c.xnL = inner.enter_context(nc.sbuf_tensor("f_xnL", [P, KT, T], F32R))
        (first_hi, first_lo, w_in0, w_in1, w_hi, w_lo, gate_full, gate_done, up_full, h_done, stored0, stored1) = semaphores(
            nc, inner, "fa", "first_hi first_lo w_in0 w_in1 w_hi w_lo gate_full gate_done up_full h_done stored0 stored1", reuse=True)

        def first_weights_hi(act):
            act.wait_ge(w12_in, 2 * KT * DMA)
            for n in range(2 * KT):
                nc.scalar.activation(wH[:, AT_W12 + n, :], first_raw[:, n, :], ACT.Copy).then_inc(first_hi, 1)

        def first_weights_lo(pool):
            for n in range(2 * KT):
                pool.wait_ge(first_hi, n + 1)
                nc.gpsimd.tensor_tensor(wL[:, AT_W12 + n, :], first_raw[:, n, :], wH[:, AT_W12 + n, :].bitcast(F32), ALU.subtract).then_inc(first_lo, 1)

        layernorm_phase(nc, c, 3, prefetch=load_first, split_hi=first_weights_hi, split_lo=first_weights_lo, xn=gate_h[:, :, :].rearrange("p (n t) d -> p n t d", n=2))
        gate, h = (gate_h[:, n * TT:(n + 1) * TT, :].rearrange("p t d -> p (t d)").rearrange("p (n s) -> p n s", s=S) for n in range(2))
        w_ins, stores = (w_in0, w_in1), (stored0, stored1)
        block = inner.enter_context(nc.Block())

        @block.sync
        def _(sp):
            sp.wait_ge(first_lo, 2 * KT)
            with sp.Fori(0, B) as b:
                next_tiles(sp, b, next_raw, w_ins, w_lo, IN_H1)
                for m in range(HT):
                    sp.wait_ge(h_done, b * HT + m + 1 + 2)
                    sp.dma_start(c.h_dram[bass.ds(b, 1), :, m, :].rearrange("o p t -> (o p) t"), h[:, m % 2, :]).then_inc(stores[m % 2], DMA)
            for done in stores:
                sp.wait_ge(done, (B * HT // 2 + 1) * DMA)

        @block.gpsimd
        def _(pool):
            for par in range(2):
                pool.wait_ge(stores[par], (HT // 2 + 1) * DMA)
            pool.dma_start(hidden[:, 0:HT // 2, :], c.h_dram[0, :, 0:HT // 2, :]).then_inc(first_in1, DMA)

        @block.scalar
        def _(act):
            act.wait_ge(scales_in, 2 * DMA)
            with act.Fori(0, B) as b:
                for m in range(HT):
                    act.wait_ge(gate_full, b * HT + m + 1)
                    act.wait_ge(h_done, b * HT + m + 1)
                    nc.scalar.activation(gate[:, m % 2, :], c.pa[:, m % 2, :], ACT.Silu, scale=scales[:, 0, m:m + 1]).then_inc(gate_done, 1)
                tiles_hi(act, b, next_raw, w_ins, w_hi, AT_H1)

        @block.vector
        def _(dve):
            dve.sem_inc(h_done, 2)
            dve.sem_inc(w_lo, PER_BATCH)
            for done in stores:
                dve.sem_inc(done, DMA)
            dve.wait_ge(scales_in, 2 * DMA)
            with dve.Fori(0, B) as b:
                for m in range(HT):
                    dve.wait_ge(up_full, b * HT + m + 1)
                    dve.wait_ge(gate_done, b * HT + m + 1)
                    dve.wait_ge(stores[m % 2], (b * HT // 2 + m // 2 + 1) * DMA)
                    nc.vector.scalar_tensor_tensor(h[:, m % 2, :], c.pd[:, m % 2, :], scales[:, 1, m:m + 1], gate[:, m % 2, :],
                                                   ALU.mult, ALU.mult).then_inc(h_done, 1)
                tiles_lo(dve, b, next_raw, w_hi, w_lo, AT_H1)

        @block.tensor
        def _(pe):
            with pe.Fori(0, B) as b:
                xn = lambda k: [x[:, k, bass.ds(b * S, S)] for x in (c.xnH, c.xnL)]
                for m in range(HT):
                    if m == 0:
                        pe.wait_ge(first_lo, 2 * KT)
                    pe.wait_ge(h_done, b * HT + m + 1)
                    for bank, w, full in ((c.pa, AT_W12, gate_full), (c.pd, AT_W12 + KT, up_full)):
                        for k in range(KT):
                            last = hi_lo(pe, nc, bank[:, m % 2, :], tile(w + k, m), xn(k), k == 0, k == KT - 1)
                        last.then_inc(full, 1)

    with ExitStack() as outer:
        sb = lambda n, s, d=F32: outer.enter_context(nc.sbuf_tensor(f"fh_{n}", s, d))
        raw = sb("raw", [P, PER_BATCH, HID])
        hH = sb("hH", [P, HT, S], F32R)
        hL = sb("hL", [P, HT, S], F32R)
        act_out = sb("act_out", [P, 2, S])

        PARTS = 4
        TILE_USES = HT - 1

        def read_hidden(pool, dram, hid_lo, hid_ins):
            size = HT // PARTS

            def load(b, q):
                pool.dma_start(hidden[:, q * size:(q + 1) * size, :],
                               dram[bass.ds(b, 1), :, q * size:(q + 1) * size, :].rearrange("o p m t -> p (o m) t")).then_inc(hid_ins[q], DMA)

            for q in range(PARTS // 2, PARTS):
                load(0, q)
            with pool.Fori(1, B) as b:
                for q in range(PARTS):
                    pool.wait_ge(hid_lo, (b - 1) * HT + (q + 1) * size)
                    apart(pool, c)
                    load(b, q)

        def hidden_hi(act, b, first, first_in, hid_ins, used, full, hid_hi):
            for k in range(HT):
                q = k * PARTS // HT
                if k % (HT // PARTS) == 0:
                    if q >= PARTS // 2:
                        act.wait_ge(hid_ins[q], b * DMA + DMA)
                    elif not first:
                        act.wait_ge(hid_ins[q], b * DMA)
                    elif k == 0:
                        act.wait_ge(first_in, DMA)
                if not first:
                    if k < TILE_USES:
                        act.wait_ge(used, (b - 1) * TILE_USES + k + 1)
                    else:
                        act.wait_ge(full, b * HT + 2)
                nc.scalar.activation(hH[:, k, :], hidden[:, k, :], ACT.Copy).then_inc(hid_hi, 1)

        def hidden_lo(dve, b, hid_hi, hid_lo):
            for k in range(HT):
                dve.wait_ge(hid_hi, b * HT + k + 1)
                nc.vector.tensor_tensor(hL[:, k, :], hidden[:, k, :], hH[:, k, :].bitcast(F32), ALU.subtract).then_inc(hid_lo, 1)

        def product(pe, b, m, at, hid_lo, done, used, full):
            pe.wait_ge(done, b * HT + m + 1)
            for k in range(HT):
                if m == 0:
                    pe.wait_ge(hid_lo, b * HT + k + 1)
                last = hi_lo(pe, nc, c.pa[:, m % 2, :], tile(at + k, m), [x[:, k, :] for x in (hH, hL)], k == 0, k == HT - 1)
                if m == HT - 1 and k < TILE_USES:
                    last.then_inc(used, 1)
            last.then_inc(full, 1)

        with ExitStack() as inner:
            (w_in0, w_in1, w_hi, w_lo, hid_in0, hid_in1, hid_in2, hid_in3, hid_hi, hid_lo, used, full, done, stored0, stored1) = semaphores(
                nc, inner, "fb", "w_in0 w_in1 w_hi w_lo hid_in0 hid_in1 hid_in2 hid_in3 hid_hi hid_lo used full done stored0 stored1", reuse=True)
            w_ins, stores, hid_ins = (w_in0, w_in1), (stored0, stored1), (hid_in0, hid_in1, hid_in2, hid_in3)
            block = inner.enter_context(nc.Block())

            @block.sync
            def _(sp):
                with sp.Fori(0, B) as b:
                    next_tiles(sp, b, raw, w_ins, w_lo, IN_H2)
                    for m in range(HT):
                        sp.wait_ge(done, b * HT + m + 1 + 2)
                        sp.dma_start(c.hidden_dram[bass.ds(b, 1), :, m, :].rearrange("o p t -> (o p) t"),
                                     act_out[:, m % 2, :]).then_inc(stores[m % 2], DMA)
                for stored in stores:
                    sp.wait_ge(stored, (B * HT // 2 + 1) * DMA)

            @block.gpsimd
            def _(pool):
                read_hidden(pool, c.h_dram, hid_lo, hid_ins)
                pool.wait_ge(hid_lo, B * HT)
                for par in range(2):
                    pool.wait_ge(stores[par], (HT // 2 + 1) * DMA)
                pool.dma_start(hidden[:, 0:HT // 2, :], c.hidden_dram[0, :, 0:HT // 2, :]).then_inc(first_in2, DMA)

            @block.scalar
            def _(act):
                def activate(b, m):
                    act.wait_ge(full, b * HT + m + 1 + 2)
                    act.wait_ge(stores[m % 2], (b * (HT // 2) + m // 2 + 1) * DMA)
                    nc.scalar.activation(act_out[:, m % 2, :], c.pa[:, m % 2, :], ACT.Gelu, scale=scales[:, 2, m:m + 1]).then_inc(done, 1)

                def batch(b, first, last):
                    hidden_hi(act, b, first, first_in1, hid_ins, used, full, hid_hi)
                    if not first:
                        activate(b - 1, HT - 1)
                    for m in range(HT - 1):
                        activate(b, m)
                        if m == HT // 2:
                            tiles_hi(act, b, raw, w_ins, w_hi, AT_H2)
                    if last:
                        activate(b, HT - 1)

                all_batches(act, batch)

            @block.vector
            def _(dve):
                dve.sem_inc(w_lo, PER_BATCH)
                with dve.Fori(0, B) as b:
                    hidden_lo(dve, b, hid_hi, hid_lo)
                    tiles_lo(dve, b, raw, w_hi, w_lo, AT_H2)

            @block.tensor
            def _(pe):
                pe.sem_inc(full, 2)
                pe.sem_inc(done, 2)
                for stored in stores:
                    pe.sem_inc(stored, DMA)
                with pe.Fori(0, B) as b:
                    for m in range(HT):
                        product(pe, b, m, AT_H1, hid_lo, done, used, full)

        with ExitStack() as inner:
            (w_in, w_hi, w_lo, hid_in0, hid_in1, hid_in2, hid_in3, hid_hi, hid_lo, used, full, done, z_hi, z_split, y_full, y_scaled, y_done, stored) = semaphores(
                nc, inner, "fc", "w_in w_hi w_lo hid_in0 hid_in1 hid_in2 hid_in3 hid_hi hid_lo used full done z_hi z_split y_full y_scaled y_done stored", reuse=True)
            y = raw[:, :, 0:2 * D].rearrange("p n (t d) -> p n t d", d=D)
            hid_ins = (hid_in0, hid_in1, hid_in2, hid_in3)
            z = lambda x, m: x[:, AT_Z + m // 2, (m % 2) * S:(m % 2 + 1) * S]
            w3 = lambda k: [x[:, AT_W3 + k // 4, (k % 4) * D:(k % 4 + 1) * D] for x in (wH, wL)]
            out_rows = c.out.rearrange("(b n p) d -> p (b n) d", p=P, n=TT)
            block = inner.enter_context(nc.Block())

            @block.sync
            def _(sp):
                for n in range(2):
                    sp.dma_start(raw[:, n, :], c.ins["ffn_w"][IN_W3 + n]).then_inc(w_in, DMA)
                with sp.Fori(0, B) as b:
                    sp.wait_ge(y_done, 2 * b + 2 + 2)
                    sp.dma_start(out_rows[:, bass.ds(b * TT, TT), :], c.X[:, bass.ds(b * TT, TT), :]).then_inc(stored, DMA)
                sp.wait_ge(stored, B * DMA)

            @block.gpsimd
            def _(pool):
                read_hidden(pool, c.hidden_dram, hid_lo, hid_ins)

            @block.scalar
            def _(act):
                def activate(b, m):
                    act.wait_ge(full, b * HT + m + 1 + 2)
                    act.wait_ge(z_split, b * HT + m + 1)
                    nc.scalar.activation(act_out[:, m % 2, :], c.pa[:, m % 2, :], ACT.Gelu, scale=scales[:, 3, m:m + 1]).then_inc(done, 1)

                def batch(b, first, last):
                    hidden_hi(act, b, first, first_in2, hid_ins, used, full, hid_hi)
                    if first:
                        act.wait_ge(w_in, 2 * DMA)
                        nc.scalar.activation(wH[:, AT_W3:AT_W3 + 2, :], raw[:, 0:2, :], ACT.Copy).then_inc(w_hi, 1)
                    else:
                        activate(b - 1, HT - 1)
                    for m in range(HT - 1):
                        activate(b, m)
                    if last:
                        activate(b, HT - 1)

                all_batches(act, batch)

            @block.vector
            def _(dve):
                dve.sem_inc(z_split, 2)
                dve.sem_inc(y_done, 2)

                def add_output(b):
                    for n in range(2):
                        dve.wait_ge(y_full, 2 * b + n + 1)
                        nc.vector.tensor_tensor(y[:, n, :, :], c.pd[:, n, :].rearrange("p (t d) -> p t d", d=D), out_scale,
                                                ALU.mult).then_inc(y_scaled, 1)
                        dve.wait_ge(y_scaled, 2 * b + n + 1)
                        xb = c.X[:, bass.ds(b * TT + 2 * n, 2), :]
                        nc.vector.tensor_tensor(xb, y[:, n, :, :], xb, ALU.add).then_inc(y_done, 1)

                def split(b, m):
                    dve.wait_ge(done, b * HT + m + 1 + 2)
                    nc.vector.tensor_copy(z(wH, m), act_out[:, m % 2, :]).then_inc(z_hi, 1)
                    dve.wait_ge(z_hi, b * HT + m + 1)
                    nc.vector.tensor_tensor(z(wL, m), act_out[:, m % 2, :], z(wH, m).bitcast(F32), ALU.subtract).then_inc(z_split, 1)

                def batch(b, first, last):
                    hidden_lo(dve, b, hid_hi, hid_lo)
                    if first:
                        dve.wait_ge(w_hi, 1)
                        nc.vector.tensor_tensor(wL[:, AT_W3:AT_W3 + 2, :], raw[:, 0:2, :], wH[:, AT_W3:AT_W3 + 2, :].bitcast(F32),
                                                ALU.subtract).then_inc(w_lo, 1)
                    else:
                        split(b - 1, HT - 1)
                        add_output(b - 1)
                    for m in range(HT - 1):
                        split(b, m)
                    if last:
                        split(b, HT - 1)
                        add_output(b)

                all_batches(dve, batch)

            @block.tensor
            def _(pe):
                pe.sem_inc(full, 2)
                pe.sem_inc(done, 2)

                def output(b):
                    pe.wait_ge(z_split, b * HT + HT + 2)
                    for n in range(2):
                        pe.wait_ge(y_done, 2 * b + n + 1)
                        for t in (2 * n, 2 * n + 1):
                            for k in range(HT):
                                last = hi_lo(pe, nc, c.pd[:, n, (t % 2) * D:(t % 2 + 1) * D],
                                             [z(x, k)[:, t * P:(t + 1) * P] for x in (wH, wL)], w3(k), k == 0, k == HT - 1)
                        last.then_inc(y_full, 1)

                def batch(b, first, last):
                    for m in range(HT):
                        product(pe, b, m, AT_H2, hid_lo, done, used, full)
                        if m == 0 and first:
                            pe.wait_ge(w_lo, 1)
                        if m == 0 and not first:
                            output(b - 1)
                    if last:
                        output(b)

                all_batches(pe, batch)


def build_program(nc, ins, out):
    c = Core()
    c.ins, c.out = ins, out
    c.q_dram = nc.dram_tensor("q_dram", (B, 2, D, S), F32).ap()
    c.k_dram = nc.dram_tensor("k_dram", (B, 2, D, S), F32).ap()
    c.rows_dram = nc.dram_tensor("rows_dram", (T, D), F32).ap()
    c.y_dram = nc.dram_tensor("y_dram", (BLOCKS * P, D), F32).ap()
    c.h_dram = nc.dram_tensor("h_dram", (B, P, HT, S), F32).ap()
    c.hidden_dram = nc.dram_tensor("hidden_dram", (B, P, HT, S), F32).ap()
    with ExitStack() as ctx:
        sb = lambda n, s, d=F32: ctx.enter_context(nc.sbuf_tensor(n, s, d))
        c.X = sb("X", [P, NT, D])
        c.ident = sb("ident", [P, P])
        c.bias = sb("bias", [P, D])
        c.stats = sb("stats", [P, NT, 6])
        c.slot_id = sb("slot_id", [P, TOPK, NT], I32)
        c.weight = sb("weight", [P, TOPK, NT])
        c.pa = ctx.enter_context(nc.psum_tensor("pa", [P, 4, S], F32))
        c.pd = ctx.enter_context(nc.psum_tensor("pd", [P, 4, S], F32))
        c.ln_sems = semaphores(nc, ctx, "ln", "loaded loaded2 const stat_done step var_done pow_done rstd_done xn_done tr_done hi_done lo_done")
        c.waited = ctx.enter_context(nc.semaphore("waited"))
        def normed(stack, part):
            c.xnH = stack.enter_context(nc.sbuf_tensor(f"xnH_{part}", [P, KT, T], F32R))
            c.xnL = stack.enter_context(nc.sbuf_tensor(f"xnL_{part}", [P, KT, T], F32R))

        with ExitStack() as stack:
            normed(stack, "a")
            first_attention_phase(nc, c)
        mixture_phase(nc, c)
        with ExitStack() as stack:
            att = SecondAttention(nc, c, stack)
            combination_phase(nc, c, att)
            with ExitStack() as inner:
                normed(inner, "c")
                second_projection_phase(nc, c, att)
            second_attention_phase(nc, c, att)
        with ExitStack() as stack:
            ffn_phases(nc, c, stack)


def kernel(**inputs):
    import concourse.bacc as bacc
    from concourse.bass_utils import run_bass_kernel_spmd

    inp = {n: np.asarray(a) for n, a in inputs.items()}
    of = lambda part: {n[len(part):]: a for n, a in inp.items() if n.startswith(part)}
    a0, moe, a1, ffn = of("L0_xattn_"), of("L0_ffn_"), of("L1_xattn_"), of("L1_ffn_")

    def by_contraction(w):
        return w.reshape(-1, P, w.shape[1]).transpose(1, 0, 2).reshape(P, -1)

    def columns(v, *lead):
        return np.moveaxis(v.reshape(*lead, -1, P), -1, 0)

    mask = inp["mask_1x1xSxS2_bk1"].reshape(S, S)
    wo1 = np.zeros((GROUPS, GH, 2, DH1, D), np.float32)
    wo1[:, :, 0] = a1["Wo"].T.reshape(GROUPS, GH, DH1, D)
    expert = lambda e: np.concatenate([by_contraction(moe["fc1_w"][e].T), by_contraction(moe["fc2_w"][e].T)], 1)
    feature_tiles = lambda w: w.T.reshape(-1, P, HID)
    layout = {
        "x": inp["x"].reshape(T, D),
        "ctx": inp["ctx_1024"].reshape(T, KT, P).transpose(2, 1, 0),
        "bo": a0["bo"],
        "wq0": by_contraction(a0["Wq"]), "wk0": by_contraction(a0["Wk"]),
        "wv0": by_contraction(a0["Wv"]), "wo0": by_contraction(a0["Wo"]),
        "gate": by_contraction(np.concatenate([moe["gate_w"].T, np.zeros((D, 1), np.float32)], 1)),
        "b1row": moe["fc1_b"].reshape(-1), "b2row": moe["fc2_b"].reshape(-1), "s_b2": moe["s_fc2_b"], "mult": columns(moe["geglu_mult"], E),
        "sb1": columns(moe["s_fc1_b"]), "smult": columns(moe["s_geglu_mult"]),
        "sw": np.concatenate([by_contraction(moe["s_fc1_w"].T), by_contraction(moe["s_fc2_w"].T)], 1),
        "ew": np.stack([expert(e) for e in range(E)]),
        "wq1": by_contraction(a1["Wq"].T), "wk1": by_contraction(a1["Wk"].T), "wv1": by_contraction(a1["Wv"].T),
        "wo1": by_contraction(wo1.reshape(-1, D)),
        "mask": mask, "maskT": mask.T,
        "ffn_w": np.concatenate([feature_tiles(ffn["w1_w"]), feature_tiles(ffn["w2_w"]), feature_tiles(ffn["h1_w"]),
                                 feature_tiles(ffn["h2_w"]),
                                 ffn["w3_w"].T.reshape(2, 4, P, D).transpose(0, 2, 1, 3).reshape(2, P, HID)], 0),
        "ffn_scales": np.stack([columns(ffn[n]) for n in ("w1_s", "w2_s", "h1_s", "h2_s")], 1),
        "w3_s": ffn["w3_s"],
    }
    arrays = {f"in_{n}": np.ascontiguousarray(a) for n, a in layout.items()}
    nc = bacc.Bacc("TRN2", target_bir_lowering=False, num_devices=1)
    ins = {n[3:]: nc.dram_tensor(n, a.shape, mybir.dt.from_np(a.dtype), kind="ExternalInput").ap() for n, a in arrays.items()}
    out = nc.dram_tensor("out", (T, D), F32, kind="ExternalOutput").ap()
    build_program(nc, ins, out)
    return run_bass_kernel_spmd(nc, [arrays], core_ids=[0]).results[0]["out"].reshape(B, S, D)
```
